# Optimizing a Trainium2 kernel written in Bass

```python
import numpy as np
import jax
import jax.numpy as jnp

def _softmax(x, axis=-1):
    return jax.nn.softmax(x, axis=axis)

def _gelu(x):
    return jax.nn.gelu(x, approximate=True)

def _silu(x):
    return jax.nn.silu(x)

def _sigmoid(x):
    return jax.nn.sigmoid(x)

def _layernorm(x, axis=-1, eps=1e-05):
    m = jnp.mean(x, axis=axis, keepdims=True)
    v = jnp.var(x, axis=axis, keepdims=True)
    return (x - m) / jnp.sqrt(v + eps)

def _scatter_add(tgt, idx, src, axis=0):
    return tgt.at[idx].add(src)

def _segment_sum(src, seg, n):
    return jax.ops.segment_sum(src, seg, n)
kernel_name = 'mk_gnn_resnorm_d4_gnn_r8_03eb74'

def setup_inputs(seed: int=0):
    np.random.seed(seed)
    _w = jnp.asarray

    def _rec_inputs():
        import jax
        import jax.numpy as jnp
        _gk = jax.random.key(seed)
        x = -0.0003019 + 1 * jax.random.normal(jax.random.fold_in(_gk, 1), (1250, 1024), jnp.float32)
        _s = jax.random.randint(jax.random.fold_in(_gk, 2), (10000,), 0, 1250, jnp.int32)
        _d = jax.random.randint(jax.random.fold_in(_gk, 3), (10000,), 0, 1250, jnp.int32)
        _loop = jnp.arange(1250, dtype=jnp.int32)
        src = jnp.concatenate([_s, _d, _loop])
        dst = jnp.concatenate([_d, _s, _loop])
        _o = jnp.argsort(dst, stable=True)
        src = src[_o]
        dst = dst[_o]
        edge_type_8 = jax.random.randint(jax.random.fold_in(_gk, 13), (21250,), 0, 8, jnp.int32)
        return (x, src, dst, edge_type_8)
    x, src, dst, edge_type_8 = _rec_inputs()

    def _L0_gnn_setup():
        import jax, jax.numpy as jnp
        import numpy as np
        N = 2500
        E = 40000
        D_IN = 1024
        D_OUT = 1024
        key = jax.random.key(seed)
        k1, k2, k3, k4 = jax.random.split(key, 4)
        x = jax.random.normal(k1, (N, D_IN), dtype=jnp.float32)
        edge_index = jax.random.randint(k2, (2, E), 0, N, dtype=jnp.int64)
        W = jax.random.normal(k3, (D_OUT, D_IN), dtype=jnp.float32) * (1.0 / np.sqrt(D_IN))
        b = jax.random.normal(k4, (D_OUT,), dtype=jnp.float32) * 0.01
        return {'x': x, 'edge_index': edge_index, 'W': W, 'b': b}
    _L0_gnn_all = _L0_gnn_setup()
    _L0_gnn_in = {k: v for k, v in _L0_gnn_all.items() if k in ('W', 'b')}
    del _L0_gnn_all

    def _L1_gnn_setup():
        import jax, jax.numpy as jnp
        import numpy as np
        N_NODES = 3125
        N_EDGES = 50000
        D = 1024

        def _sage_layer(h, edge_src, edge_dst, deg_inv, W_self, W_neigh, b):
            msg = h[edge_src]
            agg = jax.ops.segment_sum(msg, edge_dst, num_segments=h.shape[0])
            mean = agg * deg_inv[:, None]
            return h @ W_self + mean @ W_neigh + b
        key = jax.random.key(seed)
        ks = jax.random.split(key, 8)
        s = 1.0 / np.sqrt(D)
        return {'x': jax.random.normal(ks[0], (N_NODES, D), dtype=jnp.float32), 'edge_src': jax.random.randint(ks[1], (N_EDGES,), 0, N_NODES, dtype=jnp.int32), 'edge_dst': jax.random.randint(ks[2], (N_EDGES,), 0, N_NODES, dtype=jnp.int32), 'W_self0': jax.random.normal(ks[3], (D, D), dtype=jnp.float32) * s, 'W_neigh0': jax.random.normal(ks[4], (D, D), dtype=jnp.float32) * s, 'b0': jnp.zeros((D,), dtype=jnp.float32), 'W_self1': jax.random.normal(ks[5], (D, D), dtype=jnp.float32) * s, 'W_neigh1': jax.random.normal(ks[6], (D, D), dtype=jnp.float32) * s, 'b1': jnp.zeros((D,), dtype=jnp.float32)}
    _L1_gnn_all = _L1_gnn_setup()
    _L1_gnn_in = {k: v for k, v in _L1_gnn_all.items() if k in ('W_self0', 'W_neigh0', 'b0', 'W_self1', 'W_neigh1', 'b1')}
    del _L1_gnn_all

    def _L2_gnn_setup():
        import jax, jax.numpy as jnp
        import numpy as np
        N = 2500
        E = 40000
        IN = 1024
        HID = 256
        H = 4
        D = HID // H
        OUT = 1024
        EPS = 1e-06
        NEG_SLOPE = 0.2
        key = jax.random.key(seed)
        ks = jax.random.split(key, 8)
        x = jax.random.normal(ks[0], (N, IN), dtype=jnp.float32)
        edge_index = jax.random.randint(ks[1], (2, E), 0, N, dtype=jnp.int64)
        s = 0.02
        return {'x': x, 'edge_index': edge_index, 'rms_w': jnp.ones((IN,), dtype=jnp.float32), 'W_down': jax.random.normal(ks[2], (IN, HID), dtype=jnp.float32) * s, 'Wl': jax.random.normal(ks[3], (HID, HID), dtype=jnp.float32) * s, 'Wr': jax.random.normal(ks[4], (HID, HID), dtype=jnp.float32) * s, 'att': jax.random.normal(ks[5], (H, D), dtype=jnp.float32) * s, 'W_up': jax.random.normal(ks[6], (HID, OUT), dtype=jnp.float32) * s}
    _L2_gnn_all = _L2_gnn_setup()
    _L2_gnn_in = {k: v for k, v in _L2_gnn_all.items() if k in ('rms_w', 'W_down', 'Wl', 'Wr', 'att', 'W_up')}
    del _L2_gnn_all

    def _L3_gnn_setup():
        import jax, jax.numpy as jnp
        import numpy as np
        N, D, R, E = (1250, 1024, 8, 10000)

        def _rgcn(x, edge_index, edge_type, weight, root, bias):
            src, dst = (edge_index[0], edge_index[1])
            msgs = x[src]
            out = x @ root + bias
            n = x.shape[0]
            for r in range(weight.shape[0]):
                mask = (edge_type == r).astype(x.dtype)
                sums = jax.ops.segment_sum(msgs * mask[:, None], dst, num_segments=n)
                cnt = jax.ops.segment_sum(mask, dst, num_segments=n)
                mean = sums / jnp.maximum(cnt, 1.0)[:, None]
                out = out + mean @ weight[r]
            return out
        key = jax.random.key(seed)
        ks = jax.random.split(key, 8)
        s = 1.0 / np.sqrt(D)
        x = jax.random.normal(ks[0], (N, D), dtype=jnp.float32)
        edge_index = jax.random.randint(ks[1], (2, E), 0, N, dtype=jnp.int64)
        edge_type = jax.random.randint(ks[2], (E,), 0, R, dtype=jnp.int64)
        weight = jax.random.normal(ks[3], (R, D, D), dtype=jnp.float32) * s
        root = jax.random.normal(ks[4], (D, D), dtype=jnp.float32) * s
        bias = jnp.zeros((D,), dtype=jnp.float32)
        w_gate = jax.random.normal(ks[5], (2 * D, D), dtype=jnp.float32) * (1.0 / np.sqrt(2 * D))
        b_gate = jnp.zeros((D,), dtype=jnp.float32)
        return {'x': x, 'edge_index': edge_index, 'edge_type': edge_type, 'weight': weight, 'root': root, 'bias': bias, 'w_gate': w_gate, 'b_gate': b_gate}
    _L3_gnn_all = _L3_gnn_setup()
    _L3_gnn_in = {k: v for k, v in _L3_gnn_all.items() if k in ('weight', 'root', 'bias', 'w_gate', 'b_gate')}
    del _L3_gnn_all
    return {'x': x, 'src': src, 'dst': dst, 'edge_type_8': edge_type_8, 'L0_gnn_W': _L0_gnn_in['W'], 'L0_gnn_b': _L0_gnn_in['b'], 'L1_gnn_W_self0': _L1_gnn_in['W_self0'], 'L1_gnn_W_neigh0': _L1_gnn_in['W_neigh0'], 'L1_gnn_b0': _L1_gnn_in['b0'], 'L1_gnn_W_self1': _L1_gnn_in['W_self1'], 'L1_gnn_W_neigh1': _L1_gnn_in['W_neigh1'], 'L1_gnn_b1': _L1_gnn_in['b1'], 'L2_gnn_rms_w': _L2_gnn_in['rms_w'], 'L2_gnn_W_down': _L2_gnn_in['W_down'], 'L2_gnn_Wl': _L2_gnn_in['Wl'], 'L2_gnn_Wr': _L2_gnn_in['Wr'], 'L2_gnn_att': _L2_gnn_in['att'], 'L2_gnn_W_up': _L2_gnn_in['W_up'], 'L3_gnn_weight': _L3_gnn_in['weight'], 'L3_gnn_root': _L3_gnn_in['root'], 'L3_gnn_bias': _L3_gnn_in['bias'], 'L3_gnn_w_gate': _L3_gnn_in['w_gate'], 'L3_gnn_b_gate': _L3_gnn_in['b_gate']}

def reference(x, src, dst, edge_type_8, L0_gnn_W, L0_gnn_b, L1_gnn_W_self0, L1_gnn_W_neigh0, L1_gnn_b0, L1_gnn_W_self1, L1_gnn_W_neigh1, L1_gnn_b1, L2_gnn_rms_w, L2_gnn_W_down, L2_gnn_Wl, L2_gnn_Wr, L2_gnn_att, L2_gnn_W_up, L3_gnn_weight, L3_gnn_root, L3_gnn_bias, L3_gnn_w_gate, L3_gnn_b_gate):
    import jax
    import jax.numpy as jnp

    def _L0_gnn_ref(x, edge_index, W, b):
        import jax, jax.numpy as jnp
        import numpy as np
        N = 2500
        E = 40000
        D_IN = 1024
        D_OUT = 1024
        num_nodes = x.shape[0]
        self_idx = jnp.arange(num_nodes, dtype=edge_index.dtype)
        ei = jnp.concatenate([edge_index, jnp.stack([self_idx, self_idx], axis=0)], axis=1)
        row, col = (ei[0], ei[1])
        h = jnp.einsum('nd,od->no', x, W) + b
        deg = jnp.zeros((num_nodes,), dtype=h.dtype).at[row].add(1.0)
        deg_inv_sqrt = deg ** (-0.5)
        norm = deg_inv_sqrt[row] * deg_inv_sqrt[col]
        msg = norm[:, None] * h[col]
        out = jax.ops.segment_sum(msg, row, num_segments=num_nodes)
        return out

    def _L1_gnn_ref(x, edge_src, edge_dst, W_self0, W_neigh0, b0, W_self1, W_neigh1, b1):
        import jax, jax.numpy as jnp
        import numpy as np
        N_NODES = 3125
        N_EDGES = 50000
        D = 1024

        def _sage_layer(h, edge_src, edge_dst, deg_inv, W_self, W_neigh, b):
            msg = h[edge_src]
            agg = jax.ops.segment_sum(msg, edge_dst, num_segments=h.shape[0])
            mean = agg * deg_inv[:, None]
            return h @ W_self + mean @ W_neigh + b
        N = x.shape[0]
        deg = jax.ops.segment_sum(jnp.ones_like(edge_dst, dtype=x.dtype), edge_dst, num_segments=N)
        deg_inv = 1.0 / jnp.maximum(deg, 1.0)
        h = jax.nn.relu(_sage_layer(x, edge_src, edge_dst, deg_inv, W_self0, W_neigh0, b0))
        out = _sage_layer(h, edge_src, edge_dst, deg_inv, W_self1, W_neigh1, b1)
        return out

    def _L2_gnn_ref(x, edge_index, rms_w, W_down, Wl, Wr, att, W_up):
        import jax, jax.numpy as jnp
        import numpy as np
        N = 2500
        E = 40000
        IN = 1024
        HID = 256
        H = 4
        D = HID // H
        OUT = 1024
        EPS = 1e-06
        NEG_SLOPE = 0.2
        n = x.shape[0]
        ms = jnp.mean(jnp.square(x), axis=-1, keepdims=True)
        x = x * jax.lax.rsqrt(ms + EPS) * rms_w
        x = x @ W_down
        loop = jnp.arange(n, dtype=edge_index.dtype)
        src = jnp.concatenate([edge_index[0], loop])
        dst = jnp.concatenate([edge_index[1], loop])
        xl = (x @ Wl).reshape(n, H, D)
        xr = (x @ Wr).reshape(n, H, D)
        msg = xl[src] + xr[dst]
        act = jnp.where(msg > 0, msg, NEG_SLOPE * msg)
        e = jnp.einsum('ehd,hd->eh', act, att)
        m = jax.ops.segment_max(e, dst, num_segments=n)
        p = jnp.exp(e - m[dst])
        denom = jax.ops.segment_sum(p, dst, num_segments=n)
        alpha = p / (denom[dst] + 1e-16)
        out = jax.ops.segment_sum(alpha[..., None] * xl[src], dst, num_segments=n)
        out = out.reshape(n, HID)
        return out @ W_up

    def _L3_gnn_ref(x, edge_index, edge_type, weight, root, bias, w_gate, b_gate):
        import jax, jax.numpy as jnp
        import numpy as np
        N, D, R, E = (1250, 1024, 8, 10000)

        def _rgcn(x, edge_index, edge_type, weight, root, bias):
            src, dst = (edge_index[0], edge_index[1])
            msgs = x[src]
            out = x @ root + bias
            n = x.shape[0]
            for r in range(weight.shape[0]):
                mask = (edge_type == r).astype(x.dtype)
                sums = jax.ops.segment_sum(msgs * mask[:, None], dst, num_segments=n)
                cnt = jax.ops.segment_sum(mask, dst, num_segments=n)
                mean = sums / jnp.maximum(cnt, 1.0)[:, None]
                out = out + mean @ weight[r]
            return out
        u = _rgcn(x, edge_index, edge_type, weight, root, bias)
        z = jnp.concatenate([u, x], axis=1) @ w_gate + b_gate
        h = jnp.tanh(u) * z + x * (1.0 - z)
        return h
    edge_index = jnp.stack([src, dst])
    x = _layernorm(x + _L0_gnn_ref(x, edge_index, L0_gnn_W, L0_gnn_b), axis=-1)
    x = _layernorm(x + _L1_gnn_ref(x, src, dst, L1_gnn_W_self0, L1_gnn_W_neigh0, L1_gnn_b0, L1_gnn_W_self1, L1_gnn_W_neigh1, L1_gnn_b1), axis=-1)
    x = _layernorm(x + _L2_gnn_ref(x, edge_index, L2_gnn_rms_w, L2_gnn_W_down, L2_gnn_Wl, L2_gnn_Wr, L2_gnn_att, L2_gnn_W_up), axis=-1)
    x = _layernorm(x + _L3_gnn_ref(x, edge_index, edge_type_8, L3_gnn_weight, L3_gnn_root, L3_gnn_bias, L3_gnn_w_gate, L3_gnn_b_gate), axis=-1)
    return x

_drawn_inputs = setup_inputs


def setup_inputs(seed=0):
    import zlib

    import numpy as np

    out = dict(_drawn_inputs(seed))
    spreads = {'L1_gnn_b0': (0.0, 0.1),
     'L1_gnn_b1': (0.0, 0.1),
     'L2_gnn_rms_w': (1.0, 0.6),
     'L3_gnn_bias': (0.0, 0.1),
     'L3_gnn_b_gate': (0.0, 0.1)}
    factors = {'L0_gnn_b': 3.615, 'L2_gnn_Wr': 64.0, 'L2_gnn_att': 55.842}
    for name, (base, spread) in spreads.items():
        noise = np.random.default_rng([zlib.crc32(name.encode()), seed]).standard_normal(out[name].shape)
        drawn = base * np.exp(spread * noise) if base else spread * noise
        out[name] = jnp.asarray(drawn.astype(out[name].dtype))
    for name, factor in factors.items():
        out[name] = (out[name] * factor).astype(out[name].dtype)
    return out
```

```python
from contextlib import ExitStack

import concourse.bass as bass
from concourse import mybir

F32 = mybir.dt.float32
F32R = mybir.dt.float32r
F16 = mybir.dt.float16
I32 = mybir.dt.int32
ALU = mybir.AluOpType
ACT = mybir.ActivationFunctionType
AX = mybir.AxisListType

N = 1250
D = 1024
NT = 10
EP = 125
ET = 170
NREL = 8
ROWS = [128] * 9 + [98]
CH = [(0, 418), (418, 416), (834, 416)]
TPAD = 1280
RPAD = 10240
LN_EPS = 1e-5
RMS_EPS = 1e-6
NEG = -3.0e38
XS = 1024.0
KB = 1024
BASE = 16512


class Sem:

    def __init__(self, h):
        self.h = h
        self.n = 0


class Queue:

    def __init__(self):
        self.items = []
        self.seen = {}

    def wait(self, tok):
        sem, v = tok
        if v > self.seen.get(sem, 0):
            self.seen[sem] = v
            self.items.append(lambda e: e.wait_ge(sem.h, v))

    def put(self, fn, deps, sem, k):
        last = {}
        for s, v in deps:
            last[s] = max(v, last.get(s, 0))
        for t in last.items():
            self.wait(t)
        if sem is None:
            self.items.append(fn)
            return None
        sem.n += k
        self.items.append(lambda e: fn(e).then_inc(sem.h, k))
        return (sem, sem.n)

    def run(self, e):
        for f in self.items:
            f(e)


def program(nc, x, src, dst, ety, w0, b0, ws0, wn0, bb0, ws1, wn1, bb1, rmsw, wdown, wl, wr, att, wup,
            wrel, root, bias, wgate, bgate, out):
    ctx = ExitStack()
    with ctx:
        def sem(name):
            return Sem(ctx.enter_context(nc.semaphore(name)))

        def at(name, shape, dt, kb):
            return nc.alloc_sbuf_tensor_at(name, shape, dt, offset=BASE + int(kb * KB))

        def dram(name, shape):
            return nc.dram_tensor(name, shape, F32, kind="Internal").ap()

        T0 = [dram(f"T0_{i}", (TPAD, N)) for i in range(3)]
        TR = dram("TR", (RPAD, N))
        EM = dram("EM", (TPAD, N * 4))
        X1 = dram("X1", (N, D))
        X2 = dram("X2", (N, D))
        X3 = dram("X3", (N, D))
        HD = dram("HD", (N, D))
        ZD = dram("ZD", (N, D))
        XL = dram("XL", (N, 256))
        XR = dram("XR", (N, 256))

        PE, DV, AC, PL, SP = Queue(), Queue(), Queue(), Queue(), Queue()
        P, V, A, G = sem("P"), sem("V"), sem("A"), sem("G")
        dmas = []

        def dsem(name):
            s = sem(name)
            dmas.append(s)
            return s

        def pe(fn, *deps):
            return PE.put(fn, deps, P, 1)

        def dv(fn, *deps, chain=True):
            if chain:
                DV.wait((V, V.n))
            return DV.put(fn, deps, V, 1)

        def ac(fn, *deps):
            return AC.put(fn, deps, A, 1)

        def pl(fn, *deps):
            return PL.put(fn, deps, G, 1)

        def dma(q, s, o, i, *deps, scattered=False):
            return q.put(lambda e: e.dma_start(o, i, allow_slow_non_contiguous=scattered), deps, s, 16)

        def barrier(also=()):
            for q in (PE, DV, AC, SP):
                for s in (P, V, A, *bar_dmas, *also):
                    q.wait((s, s.n))

        banks = [ctx.enter_context(nc.psum_tensor(f"ps{i}", [128, 512], F32)) for i in range(8)]
        free = [[] for _ in range(8)]
        turn = [0]

        def bank(n=8):
            b = turn[0] % n
            turn[0] += 1
            return b, banks[b]

        def mm(b, ap, pairs, *deps):
            for t in (*free[b], *deps):
                PE.wait(t)
            n = len(pairs)
            for q, (l, r) in enumerate(pairs):
                f = (lambda e, l=l, r=r, q=q: e.matmul(ap, l, r, start=(q == 0), stop=(q == n - 1)))
                tok = PE.put(f, (), P if q == n - 1 else None, 1)
            return tok

        ident = at("ident", [128, 128], F32, 0)
        lmask = at("lmask", [128, 128], F32, 0.5)
        zero = at("zero", [128, 625], F32, 1)
        neg = at("neg", [128, 625], F32, 3.5)
        bc = at("bc", [128, D], F32, 6)
        ei = at("ei", [EP, 3, ET], I32, 10)
        ef = at("ef", [EP, 3, ET], F32, 12)
        key = at("key", [EP, 2, ET], F32, 14)
        cnt = at("cnt", [EP, 2, ET], F32, 15.375)
        dup = at("dup", [EP, 2, ET], F32, 16.75)
        adr = at("adr", [EP, 2, ET], I32, 18.125)
        eqj = at("eqj", [EP, 2, 125], F32, 19.5)
        trash_i = at("trash_i", [128, 2], I32, 20.5)
        trash = at("trash", [128, 2], F32, 20.53125)
        onesr = at("onesr", [128, 2], F32R, 20.5625)
        deg = at("deg", [128, 10], F32, 20.625)
        dis = at("dis", [128, 10], F32, 20.6875)
        t10 = at("t10", [128, 2, 10], F32, 20.75)
        dinv = at("dinv", [128, 10], F32, 20.875)
        st = at("st", [128, 3, 2, 6], F32, 20.9375)
        mv = at("mv", [128, 3, 12], F32, 21.125)
        rw = at("rw", [128, 8], F32, 21.3125)
        brel = at("brel", [128, 8], F32, 21.34375)
        bg = at("bg", [128, 8], F32, 21.375)
        ones16 = at("ones16", [128, 128], F16, 21.4375)
        O = 21.75
        onesf = at("onesf", [128, 2], F32, 21.6875)

        g_zero = pl(lambda e: e.memset(zero[:, :], 0.0))
        g_neg = pl(lambda e: e.memset(neg[:, :], NEG))
        g0 = pl(lambda e: e.memset(ident[:, :], 0.0))
        g1 = pl(lambda e: e.memset(lmask[:, :], 1.0))
        pl(lambda e: e.affine_select(out=ident[:, :], in_=ident[:, :], compare_op=ALU.not_equal, fill=1.0, base=0,
                                     pattern=[[-1, 128]], channel_multiplier=1), g0)
        pl(lambda e: e.affine_select(out=lmask[:, :], in_=lmask[:, :], compare_op=ALU.is_gt, fill=0.0, base=0,
                                     pattern=[[-1, 128]], channel_multiplier=1), g1)
        pl(lambda e: e.iota(trash_i[:, 0:1], pattern=[[0, 1]], base=N * N, channel_multiplier=1))
        pl(lambda e: e.iota(trash_i[:, 1:2], pattern=[[0, 1]], base=NREL * N * N, channel_multiplier=1))
        pl(lambda e: e.memset(ones16[:, :], 1.0))
        g_const = pl(lambda e: e.memset(onesf[:, :], 1.0))

        s_e = dsem("s_e")
        for n, a in enumerate((src, dst, ety)):
            t_e = dma(SP, s_e, ei[:, n, :], a.rearrange("(p t) -> p t", t=ET))
        s_z0 = dsem("s_z0")
        for t in T0:
            t_z0 = dma(SP, s_z0, t.rearrange("(p a) (b f) -> p (a b) f", p=128, f=625),
                       zero[:, None, :].broadcast_to([128, 20, 625]), g_zero)
        s_w0 = dsem("s_w0")
        wnat = at("wnat", [128, 8, D], F32, O + 120)
        t_w0 = dma(SP, s_w0, wnat[:, :, :], w0.rearrange("(k p) n -> p k n", p=128))
        s_bc = dsem("s_bc")
        t_b = dma(SP, s_bc, bc[:, :], b0.rearrange("(a n) -> a n", a=1).broadcast_to([128, D]))

        t_ef = dv(lambda e: e.tensor_copy(ef[:, :, :], ei[:, :, :]), t_e)
        dv(lambda e: e.tensor_copy(trash[:, :], trash_i[:, :]), g_const, chain=False)
        dv(lambda e: e.tensor_copy(onesr[:, :], onesf[:, :]), chain=False)
        dv(lambda e: e.scalar_tensor_tensor(out=key[:, 0, :], in0=ef[:, 1, :], scalar=float(N), in1=ef[:, 0, :],
                                            op0=ALU.mult, op1=ALU.add))
        dv(lambda e: e.scalar_tensor_tensor(out=key[:, 1, :], in0=ef[:, 2, :], scalar=float(N), in1=ef[:, 0, :],
                                            op0=ALU.mult, op1=ALU.add))
        t_key = dv(lambda e: e.scalar_tensor_tensor(out=key[:, 1, :], in0=key[:, 1, :], scalar=float(N),
                                                    in1=ef[:, 1, :], op0=ALU.mult, op1=ALU.add))
        t_adr = {}

        def dedupe(w, t0, n):
            for g in range(t0, t0 + n, 4):
                ts = list(range(g, min(g + 4, t0 + n)))
                b, ps = bank()
                for t in free[b]:
                    PE.wait(t)
                for m, t in enumerate(ts):
                    tok = mm(b, ps[0:EP, 125 * m:125 * m + 125],
                             [(key[:, w, t:t + 1].broadcast_to([EP, EP]), ident[0:EP, 0:EP])], t_key, g_const)
                for m, t in enumerate(ts):
                    pv = ps[0:EP, 125 * m:125 * m + 125]
                    dv(lambda e, pv=pv, t=t: e.tensor_scalar(
                        out=eqj[:, 0, :], in0=pv, scalar1=key[:, w, t:t + 1], scalar2=0.0, op0=ALU.is_equal,
                        op1=ALU.add, accum_out=cnt[:, w, t:t + 1]), tok)
                    last = dv(lambda e, pv=pv, t=t: e.scalar_tensor_tensor(
                        out=eqj[:, 1, :], in0=pv, scalar=key[:, w, t:t + 1], in1=lmask[0:EP, 0:125],
                        op0=ALU.is_equal, op1=ALU.mult, accum_out=dup[:, w, t:t + 1]))
                free[b] = [last]
            s = slice(t0, t0 + n)
            dv(lambda e: e.tensor_scalar(out=dup[:, w, s], in0=dup[:, w, s], scalar1=1.0, scalar2=None, op0=ALU.min))
            dv(lambda e: e.tensor_scalar(out=ef[:, w, s], in0=key[:, w, s], scalar1=trash[0:EP, w:w + 1],
                                         scalar2=-1.0, op0=ALU.subtract, op1=ALU.mult))
            dv(lambda e: e.tensor_tensor(ef[:, w, s], ef[:, w, s], dup[:, w, s], ALU.mult))
            tok = dv(lambda e: e.tensor_tensor(adr[:, w, s], ef[:, w, s], key[:, w, s], ALU.add))
            for t in range(t0, t0 + n):
                t_adr[w, t] = tok

        for q in range(5):
            dedupe(0, 34 * q, 34)

        def scatter(s, table, w, t, bound, *deps):
            flat = table.rearrange("a b -> (a b)").rearrange("(c d) -> c d", d=1)
            return PL.put(lambda e: e.indirect_dma_start(
                out=flat, out_offset=bass.IndirectOffsetOnAxis(ap=adr[:, w, t:t + 1], axis=0),
                in_=cnt[:, w, t:t + 1], in_offset=None, bounds_check=bound, oob_is_err=True, compute_op=ALU.add),
                deps, s, 16)

        s_t0 = [dsem(f"s_t0{i}") for i in range(3)]
        for t in range(ET):
            s = s_t0[t % 3]
            scatter(s, T0[t % 3], 0, t, TPAD * N - 1, t_z0, (s, s.n), t_adr[0, t])
        t_t0 = [(s, s.n) for s in s_t0]

        wt = at("wt", [128, 8, D], F32, O + 80)
        xT = at("xT", [128, 8, N], F32, O)
        yraw = at("yraw", [128, NT, D], F32, O + 40)
        xin = [at(f"xin{i}", [128, D], F32, O + 152 + 4 * i) for i in range(3)]
        s_xin = [dsem(f"s_xin{i}") for i in range(3)]
        s_xin_use = [[], [], []]
        bar_dmas = []

        def transpose_rows(i, tile, dst_t, deps, scale=None, use=None):
            r = ROWS[i]
            for h in range(2):
                b, ps = bank()
                for t in (*free[b], *deps):
                    PE.wait(t)
                for m in range(4):
                    k = 4 * h + m
                    f = (lambda e, k=k, m=m, ps=ps: e.transpose(
                        ps[:, 128 * m:128 * m + r], tile[0:r, 128 * k:128 * k + 128], ident[0:r, 0:r]))
                    tok = PE.put(f, (), P if m == 3 else None, 1)
                pv = ps[:, :].rearrange("p (m c) -> p m c", m=4)[:, :, 0:r]
                if scale is None:
                    free[b] = [ac(lambda e, pv=pv, h=h: e.activation(
                        dst_t[:, 4 * h:4 * h + 4, 128 * i:128 * i + r], pv, ACT.Copy), tok)]
                else:
                    for m in range(4):
                        k = 4 * h + m
                        free[b] = [ac(lambda e, pv=pv, k=k, m=m: e.mul(
                            dst_t[:, k, 128 * i:128 * i + r], pv[:, m, :], scale[:, k:k + 1]), tok)]
            return tok

        PE.wait(g_const)
        for i in range(NT):
            r = ROWS[i]
            t_x = dma(SP, s_xin[i % 3], xin[i % 3][0:r, :], x[128 * i:128 * i + r, :], *s_xin_use[i % 3])
            s_xin_use[i % 3] = [transpose_rows(i, xin[i % 3], xT, [t_x])]
        for k in range(8):
            for h in range(2):
                b, ps = bank()
                for t in (*free[b], t_w0):
                    PE.wait(t)
                for m in range(4):
                    o = 4 * h + m
                    f = (lambda e, k=k, m=m, o=o, ps=ps: e.transpose(
                        ps[:, 128 * m:128 * m + 128], wnat[:, o, 128 * k:128 * k + 128], ident[:, :]))
                    tok = PE.put(f, (), P if m == 3 else None, 1)
                free[b] = [ac(lambda e, k=k, h=h, ps=ps: e.activation(
                    wt[:, k, 512 * h:512 * h + 512], ps[:, :], ACT.Copy), tok)]
        t_wt = (A, A.n)
        for i in range(NT):
            r = ROWS[i]
            for j in range(2):
                b, ps = bank()
                tok = mm(b, ps[0:r, :], [(xT[:, k, 128 * i:128 * i + r], wt[:, k, 512 * j:512 * j + 512])
                                         for k in range(8)], t_wt)
                free[b] = [dv(lambda e, i=i, j=j, r=r, ps=ps: e.tensor_tensor(
                    yraw[0:r, i, 512 * j:512 * j + 512], ps[0:r, :], bc[0:r, 512 * j:512 * j + 512], ALU.add),
                    tok, t_b, chain=False)]
        for q in range(5):
            dedupe(1, 34 * q, 34)

        s_z1 = dsem("s_z1")
        for c in range(4):
            t_z1 = dma(SP, s_z1, TR[2560 * c:2560 * c + 2560, :].rearrange("(p a) (b f) -> p (a b) f", p=128, f=625),
                       zero[:, None, :].broadcast_to([128, 40, 625]))
        s_tr = dsem("s_tr")
        for t in range(ET):
            scatter(s_tr, TR, 1, t, RPAD * N - 1, t_z1, (s_tr, s_tr.n), t_adr[1, t])
        t_tr = (s_tr, s_tr.n)
        s_em = dsem("s_em")
        for c in range(2):
            t_em = dma(SP, s_em, EM[640 * c:640 * c + 640, :].rearrange("(p a) (b f) -> p (a b) f", p=128, f=625),
                       neg[:, None, :].broadcast_to([128, 40, 625]), g_neg)

        bar_dmas = [s_w0, s_bc, *s_xin]
        barrier()
        bp = at("bp", [128, NT, N], F32R, O + 120)
        slab = [[at(f"slab{a}{i}", [128, N], F32, O + 5 * (3 * a + i)) for i in range(3)] for a in range(2)]
        s_sl = [[dsem(f"s_sl{a}{i}") for i in range(3)] for a in range(2)]
        used = [[], []]
        for i in range(NT):
            r, a = ROWS[i], i % 2
            toks = [dma(SP, s_sl[a][n], slab[a][n][0:r, :], T0[n][128 * i:128 * i + r, :], t_t0[n], *used[a])
                    for n in range(3)]
            dv(lambda e, a=a, r=r: e.tensor_tensor(slab[a][0][0:r, :], slab[a][0][0:r, :], slab[a][1][0:r, :], ALU.add),
               *toks)
            dv(lambda e, a=a, r=r: e.tensor_tensor(slab[a][0][0:r, :], slab[a][0][0:r, :], slab[a][2][0:r, :], ALU.add))
            dv(lambda e, a=a, r=r, i=i: e.tensor_tensor(
                slab[a][0][0:r, 128 * i:128 * i + r], slab[a][0][0:r, 128 * i:128 * i + r], ident[0:r, 0:r], ALU.add))
            used[a] = [dv(lambda e, a=a, r=r, i=i: e.tensor_copy(bp[0:r, i, :], slab[a][0][0:r, :]))]
        t_bp = used[1][0]

        def degrees(mat, dst, *deps):
            b, ps = bank()
            t0 = dv(lambda e: e.memset(dst[:, :], 1.0))
            for i in range(NT):
                tok = mm(b, ps[0:ROWS[i], 2 * i:2 * i + 2],
                         [(mat[0:ROWS[k], k, 128 * i:128 * i + ROWS[i]], onesr[0:ROWS[k], :]) for k in range(NT)], *deps)
            pv = ps[:, 0:20].rearrange("p (i c) -> p i c", c=2)
            dv(lambda e: e.tensor_copy(dst[:, 0:9], pv[:, 0:9, 0]), tok)
            free[b] = [dv(lambda e: e.tensor_copy(dst[0:98, 9:10], pv[0:98, 9:10, 0]), tok)]

        def rsqrt(y, v, t, deps=()):
            s = ac(lambda e: e.activation(y, v, ACT.Sqrt), (V, V.n), *deps)
            dv(lambda e: e.reciprocal(y, y), s)
            dv(lambda e: e.tensor_tensor(t, v, y, ALU.mult))
            dv(lambda e: e.tensor_tensor(t, t, y, ALU.mult))
            dv(lambda e: e.tensor_scalar(out=t, in0=t, scalar1=-0.5, scalar2=1.5, op0=ALU.mult, op1=ALU.add))
            return dv(lambda e: e.tensor_tensor(y, y, t, ALU.mult))

        degrees(bp, deg, t_bp)
        rsqrt(dis[:, :], deg[:, :], t10[:, 0, :])

        yhi = at("yhi", [128, NT, D], F32R, O + 40)
        ylo = at("ylo", [128, NT, D], F32R, O + 80)
        yt = [at(f"yt{i}", [128, D], F32, O + 30 + 4 * i) for i in range(2)]
        for i in range(NT):
            r, a = ROWS[i], i % 2
            t0 = dv(lambda e, i=i, r=r, a=a: e.tensor_scalar(
                out=yt[a][0:r, :], in0=yraw[0:r, i, :], scalar1=dis[0:r, i:i + 1], scalar2=None, op0=ALU.mult))
            t1 = ac(lambda e, i=i, r=r, a=a: e.activation(yhi[0:r, i, :], yt[a][0:r, :], ACT.Copy), t0)
            t_y = dv(lambda e, i=i, r=r, a=a: e.tensor_tensor(
                ylo[0:r, i, :], yt[a][0:r, :], yhi[0:r, i, :].bitcast(F32), ALU.subtract), t1)
        barrier()

        zt = [at(f"zt{i}", [128, D], F32, O + 170 + 4 * i) for i in range(2)]
        xres = [at(f"xres{i}", [128, D], F32, O + 178 + 4 * i) for i in range(2)]
        s_xr = [dsem(f"s_xr{i}") for i in range(2)]
        s_xo = [dsem(f"s_xo{i}") for i in range(2)]

        def layer_norm(i, z, o, m, deps=()):
            r = ROWS[i]
            for h in range(2):
                dv(lambda e, h=h: e.bn_stats(st[0:r, m, h, :], z[0:r, 512 * h:512 * h + 512]), *deps, chain=(h == 0))
            dv(lambda e: e.bn_aggr(mv[0:r, m, 0:2], st[0:r, m, :, :].rearrange("p a b -> p (a b)")))
            dv(lambda e: e.tensor_scalar(out=mv[0:r, m, 2:3], in0=mv[0:r, m, 1:2], scalar1=LN_EPS, scalar2=None,
                                         op0=ALU.add))
            rsqrt(mv[0:r, m, 3:4], mv[0:r, m, 2:3], mv[0:r, m, 4:5])
            return dv(lambda e: e.tensor_scalar(out=o[0:r, :], in0=z[0:r, :], scalar1=mv[0:r, m, 0:1],
                                                scalar2=mv[0:r, m, 3:4], op0=ALU.subtract, op1=ALU.mult))

        used = [[], []]
        for i in range(NT):
            r, a = ROWS[i], i % 2
            t_x = dma(SP, s_xr[a], xres[a][0:r, :], x[128 * i:128 * i + r, :], *used[a])
            for j in range(2):
                b, ps = bank()
                c = slice(512 * j, 512 * j + 512)
                tok = mm(b, ps[0:r, :], [(bp[0:ROWS[k], k, 128 * i:128 * i + r], y[0:ROWS[k], k, c])
                                         for k in range(NT) for y in (yhi, ylo)])
                free[b] = [dv(lambda e, i=i, r=r, a=a, c=c, ps=ps: e.scalar_tensor_tensor(
                    out=zt[a][0:r, c], in0=ps[0:r, :], scalar=dis[0:r, i:i + 1], in1=xres[a][0:r, c],
                    op0=ALU.mult, op1=ALU.add), tok, t_x, *used[a], chain=False)]
            t_n = layer_norm(i, zt[a], zt[a], a)
            t_o = dma(AC, s_xo[a], X1[128 * i:128 * i + r, :], zt[a][0:r, :], t_n)
            t_p = transpose_rows(i, zt[a], xT, [t_n])
            used[a] = [t_n, t_o, t_p]
        bar_dmas = [*s_xr, *s_xo]
        barrier()

        am = at("am", [128, NT, N], F32R, O + 40)
        for k in range(NT):
            rk = ROWS[k]
            for g in range(3):
                b, ps = bank()
                ds = list(range(4 * g, min(4 * g + 4, NT)))
                for t in free[b]:
                    PE.wait(t)
                for m, d in enumerate(ds):
                    f = (lambda e, m=m, d=d, ps=ps, k=k, rk=rk: e.transpose(
                        ps[0:rk, 128 * m:128 * m + ROWS[d]],
                        bp[0:ROWS[d], d, 128 * k:128 * k + rk].bitcast(F32), ident[0:ROWS[d], 0:ROWS[d]]))
                    tok = PE.put(f, (), P if d == ds[-1] else None, 1)
                w = sum(ROWS[d] for d in ds)
                free[b] = [ac(lambda e, ps=ps, k=k, g=g, rk=rk, w=w: e.activation(
                    am[0:rk, k, 512 * g:512 * g + w], ps[0:rk, 0:w], ACT.Copy), tok)]
        for k in range(NT):
            rk = ROWS[k]
            blk = (lambda k=k, rk=rk: am[0:rk, k, 128 * k:128 * k + rk])
            t_am = dv(lambda e, blk=blk, rk=rk: e.tensor_tensor(blk(), blk().bitcast(F32), ident[0:rk, 0:rk],
                                                                ALU.subtract), (A, A.n), chain=False)
        degrees(am, deg, t_am)
        dv(lambda e: e.tensor_scalar(out=deg[:, :], in0=deg[:, :], scalar1=1.0, scalar2=None, op0=ALU.max))
        dv(lambda e: e.reciprocal(dinv[:, :], deg[:, :]))
        barrier()

        wb = [at(f"wb{i}", [128, 8, 512], F32, O + 129 + 16 * i) for i in range(3)]
        hhi = at("hhi", [128, NT, 512], F32R, O + 89)
        hlo = at("hlo", [128, NT, 512], F32R, O + 109)
        tt = [at(f"tt{i}", [128, 512], F32, O + 177 + 2 * i) for i in range(4)]
        s_wb = [dsem(f"s_wb{i}") for i in range(3)]
        s_ho = [dsem(f"s_ho{i}") for i in range(4)]
        wb_used = [[], [], []]
        tt_used = [[], [], [], []]
        wturn = [0]

        def load_w(w, j):
            n = wturn[0] % 3
            wturn[0] += 1
            return n, dma(SP, s_wb[n], wb[n][:, :, :],
                          w.rearrange("(k p) n -> p k n", p=128)[:, :, 512 * j:512 * j + 512], *wb_used[n])

        def sage(ws, wn, bias_v, dest, relu):
            t_b = dma(SP, s_bc, bc[:, :], bias_v.rearrange("(a n) -> a n", a=1).broadcast_to([128, D]))
            for j in range(2):
                n1, t_n = load_w(wn, j)
                n2, t_s = load_w(ws, j)
                for i in range(NT):
                    r = ROWS[i]
                    b, ps = bank()
                    tok = mm(b, ps[0:r, :], [(xT[:, k, 128 * i:128 * i + r], wb[n1][:, k, :]) for k in range(8)], t_n)
                    wb_used[n1] = [tok]
                    t1 = ac(lambda e, i=i, r=r, ps=ps: e.activation(hhi[0:r, i, :], ps[0:r, :], ACT.Copy), tok)
                    t_h = dv(lambda e, i=i, r=r, ps=ps: e.tensor_tensor(
                        hlo[0:r, i, :], ps[0:r, :], hhi[0:r, i, :].bitcast(F32), ALU.subtract), t1, chain=False)
                    free[b] = [t_h]
                for i in range(NT):
                    r = ROWS[i]
                    a = (NT * j + i) % 4
                    b, ps = bank()
                    tok = mm(b, ps[0:r, :], [(xT[:, k, 128 * i:128 * i + r], wb[n2][:, k, :]) for k in range(8)], t_s)
                    wb_used[n2] = [tok]
                    free[b] = [dv(lambda e, r=r, a=a, j=j, ps=ps: e.tensor_tensor(
                        tt[a][0:r, :], ps[0:r, :], bc[0:r, 512 * j:512 * j + 512], ALU.add),
                        tok, t_b, *tt_used[a], chain=False)]
                    b, ps = bank()
                    tok = mm(b, ps[0:r, :], [(am[0:ROWS[k], k, 128 * i:128 * i + r], h[0:ROWS[k], k, :])
                                             for k in range(NT) for h in (hhi, hlo)], t_h)
                    last = dv(lambda e, i=i, r=r, a=a, ps=ps: e.scalar_tensor_tensor(
                        out=tt[a][0:r, :], in0=ps[0:r, :], scalar=dinv[0:r, i:i + 1], in1=tt[a][0:r, :],
                        op0=ALU.mult, op1=ALU.add), tok)
                    free[b] = [last]
                    if relu:
                        last = dv(lambda e, r=r, a=a: e.tensor_scalar(
                            out=tt[a][0:r, :], in0=tt[a][0:r, :], scalar1=0.0, scalar2=None, op0=ALU.max))
                    tt_used[a] = [dma(AC, s_ho[a], dest[128 * i:128 * i + r, 512 * j:512 * j + 512],
                                      tt[a][0:r, :], last)]

        bar_dmas = [*s_wb, *s_ho, s_bc]
        sage(ws0, wn0, bb0, HD, True)
        barrier()
        lt = [at(f"lt{i}", [128, D], F32, O + 89 + 4 * i) for i in range(4)]
        s_lt = [dsem(f"s_lt{i}") for i in range(4)]
        used = [[], [], [], []]
        for i in range(NT):
            r, a = ROWS[i], i % 4
            t_l = dma(SP, s_lt[a], lt[a][0:r, :], HD[128 * i:128 * i + r, :], *used[a])
            used[a] = [transpose_rows(i, lt[a], xT, [t_l])]
        bar_dmas = [*s_lt]
        barrier()
        bar_dmas = [*s_wb, *s_ho, s_bc]
        sage(ws1, wn1, bb1, ZD, False)
        barrier()

        t_rw = dma(SP, s_bc, rw[:, :], rmsw.rearrange("(k p) -> p k", p=128), scattered=True)
        zl = [at(f"zl{i}", [128, D], F32, O + 89 + 4 * i) for i in range(3)]
        xl2 = [at(f"xl2{i}", [128, D], F32, O + 101 + 4 * i) for i in range(3)]
        xn = [at(f"xn{i}", [128, D], F32, O + 113 + 4 * i) for i in range(3)]
        s_zl = [dsem(f"s_zl{i}") for i in range(3)]
        s_x2 = [dsem(f"s_x2{i}") for i in range(3)]
        used = [[], [], []]
        for i in range(NT):
            r, a = ROWS[i], i % 3
            t0 = dma(SP, s_zl[a], zl[a][0:r, :], ZD[128 * i:128 * i + r, :], *used[a])
            t1 = dma(SP, s_zl[a], xl2[a][0:r, :], X1[128 * i:128 * i + r, :], *used[a])
            dv(lambda e, a=a, r=r: e.tensor_tensor(zl[a][0:r, :], zl[a][0:r, :], xl2[a][0:r, :], ALU.add), t0, t1)
            t_n = layer_norm(i, zl[a], zl[a], a)
            t_o = dma(AC, s_x2[a], X2[128 * i:128 * i + r, :], zl[a][0:r, :], t_n)
            t_q = ac(lambda e, a=a, r=r: e.activation(xn[a][0:r, :], zl[a][0:r, :], ACT.Square,
                                                      accum_out=mv[0:r, a, 5:6]), t_n, *used[a])
            dv(lambda e, a=a, r=r: e.tensor_scalar(out=mv[0:r, a, 6:7], in0=mv[0:r, a, 5:6], scalar1=1.0 / D,
                                                   scalar2=RMS_EPS, op0=ALU.mult, op1=ALU.add), t_q)
            rsqrt(mv[0:r, a, 7:8], mv[0:r, a, 6:7], mv[0:r, a, 8:9])
            t_s = dv(lambda e, a=a, r=r: e.tensor_scalar(out=xn[a][0:r, :], in0=zl[a][0:r, :],
                                                         scalar1=mv[0:r, a, 7:8], scalar2=None, op0=ALU.mult))
            AC.wait(t_rw)
            t_p = transpose_rows(i, xn[a], xT, [t_s], scale=rw)
            used[a] = [t_n, t_s, t_o, t_p]
        bar_dmas = [*s_zl, *s_x2, s_bc]
        barrier()

        wd = at("wd", [128, 8, 256], F32, O + 89)
        wlr = at("wlr", [128, 2, 2, 256], F32, O + 97)
        xd = at("xd", [128, 2, N], F32, O + 101)
        xlx = at("xlx", [128, NT, 4, 65], F32, O + 111)
        xrn = at("xrn", [128, NT, 256], F32, O + 121.5)
        atb = at("atb", [128, 256], F32, O + 131.5)
        zg = at("zg", [128, NT, 256], F32, O + 132.5)
        zh = at("zh", [128, NT, 256], F32, O + 142.5)
        ed = at("ed", [128, NT, 4], F32, O + 152.5)
        s_wd = dsem("s_wd")
        dma(SP, s_wd, wd[:, :, :], wdown.rearrange("(k p) n -> p k n", p=128))
        dma(SP, s_wd, wlr[:, 0, :, :], wl.rearrange("(k p) n -> p k n", p=128))
        dma(SP, s_wd, wlr[:, 1, :, :], wr.rearrange("(k p) n -> p k n", p=128))
        t_wd = dma(SP, s_wd, atb[:, :],
                   att.rearrange("h d -> (h d)").rearrange("(a n) -> a n", a=1).broadcast_to([128, 256]))
        for o in range(2):
            for c0, cn in CH:
                b, ps = bank()
                tok = mm(b, ps[:, 0:cn], [(wd[:, k, 128 * o:128 * o + 128], xT[:, k, c0:c0 + cn]) for k in range(8)], t_wd)
                free[b] = [ac(lambda e, o=o, c0=c0, cn=cn, ps=ps: e.activation(
                    xd[:, o, c0:c0 + cn], ps[:, 0:cn], ACT.Copy), tok)]
        t_xd = (A, A.n)
        t_on = dv(lambda e: e.memset(xlx[:, :, :, 64:65], 1.0))
        s_xl = dsem("s_xl")
        for i in range(NT):
            r = ROWS[i]
            b, ps = bank()
            for w in range(2):
                tok = mm(b, ps[0:r, 256 * w:256 * w + 256],
                         [(xd[:, k, 128 * i:128 * i + r], wlr[:, w, k, :]) for k in range(2)], t_xd, t_wd)
            dv(lambda e, i=i, r=r, ps=ps: e.tensor_copy(
                xlx[0:r, i, :, 0:64], ps[0:r, 0:256].rearrange("p (h d) -> p h d", h=4)), tok, chain=False)
            t0 = dv(lambda e, i=i, r=r, ps=ps: e.tensor_copy(xrn[0:r, i, :], ps[0:r, 256:512]), chain=False)
            free[b] = [t0]
            dma(AC, s_xl, XL[128 * i:128 * i + r, :].rearrange("p (h d) -> p h d", h=4), xlx[0:r, i, :, 0:64], t0)
            t_xl = dma(AC, s_xl, XR[128 * i:128 * i + r, :], xrn[0:r, i, :], t0)

        def logits(z, tmp, tgt, m, xa, xb, *deps):
            pr = z.shape[0]
            dv(lambda e: e.tensor_tensor(z, xa, xb, ALU.add), *deps, chain=False)
            dv(lambda e: e.scalar_tensor_tensor(out=tmp.rearrange("p m f -> p (m f)"), in0=z.rearrange("p m f -> p (m f)"),
                                                scalar=0.2, in1=z.rearrange("p m f -> p (m f)"), op0=ALU.mult,
                                                op1=ALU.max))
            dv(lambda e: e.tensor_tensor(z, tmp, atb[0:pr, None, :].broadcast_to([pr, m, 256]), ALU.mult))
            return dv(lambda e: e.tensor_reduce(out=tgt, in_=z.rearrange("p m (h d) -> p (m h) d", h=4), axis=AX.X,
                                                op=ALU.add))

        for i0, i1, r in ((0, 9, 128), (9, 10, 98)):
            t_ed = diag_logits(dv, zg, zh, ed, atb, xlx, xrn, i0, i1, r, t_wd)
        s_ed = dsem("s_ed")
        diag = EM.rearrange("a (b h) -> (a b) h", h=4)
        for i in range(NT):
            r = ROWS[i]
            a0 = 128 * i * (N + 1)
            t_dg = dma(AC, s_ed, diag[a0:a0 + (r - 1) * (N + 1) + 1:N + 1, :], ed[0:r, i, :], t_ed, t_em)

        NB = 5
        gl = [at(f"gl{i}", [EP, NB, 256], F32, O + 153 + 5 * i) for i in range(2)]
        gr = [at(f"gr{i}", [EP, NB, 256], F32, O + 163 + 5 * i) for i in range(2)]
        ee = at("ee", [EP, ET, 4], F32, O + 173)
        s_g = [dsem(f"s_g{i}") for i in range(2)]
        s_sc = dsem("s_sc")
        t_ee = {}
        used = [[], []]
        LAG = 8

        def put_logits(t):
            PL.put(lambda e: e.indirect_dma_start(
                out=diag, out_offset=bass.IndirectOffsetOnAxis(ap=adr[:, 0, t:t + 1], axis=0),
                in_=ee[:, t, :], in_offset=None, bounds_check=TPAD * N - 1, oob_is_err=True),
                (t_ee[t], t_dg, (s_sc, s_sc.n)), s_sc, 16)

        for t in range(ET):
            a, m = (t // NB) % 2, t % NB
            for buf, tab, row in ((gl, XL, 0), (gr, XR, 1)):
                tok = PL.put(lambda e, buf=buf, tab=tab, row=row, a=a, m=m, t=t: e.indirect_dma_start(
                    out=buf[a][:, m, :], out_offset=None, in_=tab,
                    in_offset=bass.IndirectOffsetOnAxis(ap=ei[:, row, t:t + 1], axis=0)),
                    (t_xl, *used[a]), s_g[a], 16)
            if m == NB - 1:
                last = logits(gl[a][:, :, :], gr[a][:, :, :],
                              ee[:, t - NB + 1:t + 1, :].rearrange("p m h -> p (m h)"), NB,
                              gl[a][:, :, :], gr[a][:, :, :], tok)
                used[a] = [last]
                for q in range(t - NB + 1, t + 1):
                    t_ee[q] = last
            if t >= LAG:
                put_logits(t - LAG)
        for t in range(ET - LAG, ET):
            put_logits(t)
        t_sc = (s_sc, s_sc.n)
        for k in range(NT):
            rk = ROWS[k]
            blk = (lambda k=k, rk=rk: am[0:rk, k, 128 * k:128 * k + rk])
            t_am = dv(lambda e, blk=blk, rk=rk: e.tensor_tensor(blk(), blk().bitcast(F32), ident[0:rk, 0:rk],
                                                                ALU.add), chain=False)
        bar_dmas = [s_wd, s_xl, s_ed, *s_g]
        barrier()

        eb = [at(f"eb{i}", [128, N, 4], F32, O + 123 + 19.75 * i) for i in range(2)]
        pb = at("pb", [128, 4, N], F32, O + 162.5)
        pt = [at(f"pt{i}", [128, 4, 128], F32, O + 89 + 2 * i) for i in range(6)]
        gn = at("gn", [128, NT, 256], F32, O)
        gT = at("gT", [128, 2, N], F32, O + 10)
        wu = at("wu", [128, 2, D], F32, O + 20)
        mx = at("mx", [128, 2, 4], F32, O + 28)
        rd = at("rd", [128, 2, 4], F32, O + 28.0625)
        s_eb = [dsem(f"s_eb{i}") for i in range(2)]
        t_wu = dma(SP, s_wd, wu[:, :, :], wup.rearrange("(k p) n -> p k n", p=128))
        eb_used = [[], []]
        pt_used = [[] for _ in range(6)]
        pb_used = []
        pturn = 0
        for i in range(NT):
            r, a = ROWS[i], i % 2
            t0 = dma(SP, s_eb[a], eb[a][0:r, :, :], EM[128 * i:128 * i + r, :].rearrange("p (s h) -> p s h", h=4),
                     t_sc, *eb_used[a])
            t1 = dv(lambda e, a=a, r=r: e.tensor_reduce(out=mx[0:r, a, :], in_=eb[a][0:r, :, :].rearrange("p s h -> p h s"),
                                                        axis=AX.X, op=ALU.max, negate=True), t0, *eb_used[a], chain=False)
            for h in range(4):
                t2 = ac(lambda e, a=a, r=r, h=h: e.activation(pb[0:r, h, :], eb[a][0:r, :, h], ACT.Exp,
                                                              bias=mx[0:r, a, h:h + 1]), t1, *pb_used)
            eb_used[a] = [t2]
            bo, po = 6 + i % 2, banks[6 + i % 2]
            for h in range(4):
                prs = []
                for g in range(3):
                    ks = list(range(4 * g, min(4 * g + 4, NT)))
                    b, ps = bank(6)
                    for t in (*free[b], t2):
                        PE.wait(t)
                    for m, k in enumerate(ks):
                        f = (lambda e, m=m, k=k, ps=ps, h=h, r=r: e.transpose(
                            ps[0:ROWS[k], 128 * m:128 * m + r], pb[0:r, h, 128 * k:128 * k + ROWS[k]], ident[0:r, 0:r]))
                        tok = PE.put(f, (), P if k == ks[-1] else None, 1)
                    n = pturn % 6
                    pturn += 1
                    parts = [(ks, 128)] if g < 2 else [(ks[0:1], 128), (ks[1:2], 98)]
                    for kk, rk in parts:
                        m0 = kk[0] - ks[0]
                        pv = ps[0:rk, :].rearrange("p (m c) -> p m c", m=4)[:, m0:m0 + len(kk), 0:r]
                        last = dv(lambda e, n=n, kk=kk, rk=rk, m0=m0, pv=pv, i=i, r=r: e.tensor_tensor(
                            pt[n][0:rk, m0:m0 + len(kk), 0:r], pv,
                            am[0:rk, kk[0]:kk[0] + len(kk), 128 * i:128 * i + r].bitcast(F32), ALU.mult),
                            tok, t_am, *pt_used[n], chain=False)
                    free[b] = [last]
                    prs += [(n, k, m) for m, k in enumerate(ks)]
                    pt_last = last
                tok = mm(bo, po[0:r, 65 * h:65 * h + 65],
                         [(pt[n][0:ROWS[k], m, 0:r], xlx[0:ROWS[k], k, h, :]) for n, k, m in prs], pt_last)
                for n, _, _ in prs:
                    pt_used[n] = [tok]
            pb_used = [tok]
            pv = po[0:r, 0:260].rearrange("p (h c) -> p h c", h=4)
            dv(lambda e, a=a, r=r, pv=pv: e.tensor_scalar(out=rd[0:r, a, :], in0=pv[:, :, 64], scalar1=1e-16,
                                                          scalar2=None, op0=ALU.add), tok, chain=False)
            dv(lambda e, a=a, r=r: e.reciprocal(rd[0:r, a, :], rd[0:r, a, :]))
            last = dv(lambda e, a=a, r=r, pv=pv, i=i: e.tensor_tensor(
                gn[0:r, i, :].rearrange("p (h d) -> p h d", h=4), pv[:, :, 0:64],
                rd[0:r, a, :, None].broadcast_to([r, 4, 64]), ALU.mult))
            free[bo] = [last]
            b, ps = bank(6)
            for t in (*free[b], last):
                PE.wait(t)
            for k in range(2):
                f = (lambda e, k=k, ps=ps, i=i, r=r: e.transpose(
                    ps[:, 128 * k:128 * k + r], gn[0:r, i, 128 * k:128 * k + 128], ident[0:r, 0:r]))
                tok = PE.put(f, (), P if k == 1 else None, 1)
            free[b] = [ac(lambda e, ps=ps, i=i, r=r: e.activation(
                gT[:, :, 128 * i:128 * i + r], ps[:, 0:256].rearrange("p (k c) -> p k c", k=2)[:, :, 0:r], ACT.Copy), tok)]
        t_gT = (A, A.n)
        bar_dmas = [*s_eb, s_wd]
        barrier()

        xh = at("xh", [128, NT, D], F16, O + 40)
        xo = at("xo", [128, NT, D], F16, O + 60)
        z3 = [at(f"z3{i}", [128, D], F32, O + 80 + 4 * i) for i in range(3)]
        x2l = [at(f"x2l{i}", [128, D], F32, O + 92 + 4 * i) for i in range(3)]
        xsc = [at(f"xsc{i}", [128, D], F32, O + 104 + 4 * i) for i in range(3)]
        s_2l = [dsem(f"s_2l{i}") for i in range(3)]
        s_3o = [dsem(f"s_3o{i}") for i in range(3)]
        used = [[], [], []]
        for i in range(NT):
            r, a = ROWS[i], i % 3
            t0 = dma(SP, s_2l[a], x2l[a][0:r, :], X2[128 * i:128 * i + r, :], *used[a])
            for j in range(2):
                b, ps = bank()
                c = slice(512 * j, 512 * j + 512)
                tok = mm(b, ps[0:r, :], [(gT[:, k, 128 * i:128 * i + r], wu[:, k, c]) for k in range(2)])
                free[b] = [dv(lambda e, r=r, a=a, c=c, ps=ps: e.tensor_tensor(z3[a][0:r, c], ps[0:r, :], x2l[a][0:r, c], ALU.add),
                              tok, t0, *used[a], chain=False)]
            t_n = layer_norm(i, z3[a], z3[a], a)
            t_o = dma(AC, s_3o[a], X3[128 * i:128 * i + r, :], z3[a][0:r, :], t_n)
            t1 = ac(lambda e, r=r, a=a, i=i: e.mul(xsc[a][0:r, :], z3[a][0:r, :], XS), t_n, *used[a])
            t1 = ac(lambda e, r=r, a=a, i=i: e.activation(xh[0:r, i, :], xsc[a][0:r, :], ACT.Copy), t1)
            t2 = dv(lambda e, r=r, a=a, i=i: e.tensor_tensor(xo[0:r, i, :], xsc[a][0:r, :], xh[0:r, i, :], ALU.subtract), t1)
            used[a] = [t_n, t_o, t2]
        bar_dmas = [*s_2l, *s_3o]
        barrier()

        mt = at("mt", [128, 8, N], F32, O)
        a16 = at("a16", [128, NT, N], F16, O + 80)
        ar = [at(f"ar{i}", [128, N], F32, O + 104.5 + 5 * i) for i in range(2)]
        acc = at("acc", [128, 8, N], F32, O + 114.5)
        wq = [at(f"wq{i}", [128, 8, 256], F32, O + 154 + 8 * i) for i in range(3)]
        ib = at("ib", [128, N], F32, O + 178)
        s_ar = [dsem(f"s_ar{i}") for i in range(2)]
        s_wq = [dsem(f"s_wq{i}") for i in range(3)]
        s_br = dsem("s_br")
        dma(SP, s_br, brel[:, :], bias.rearrange("(k p) -> p k", p=128), scattered=True)
        t_br = dma(SP, s_br, bg[:, :], bgate.rearrange("(k p) -> p k", p=128), scattered=True)
        wq_used = [[], [], []]
        ar_used = [[], []]
        qturn = [0]

        def load_q(w, c):
            n = qturn[0] % 3
            qturn[0] += 1
            return n, dma(SP, s_wq[n], wq[n][:, :, :],
                          w.rearrange("(k p) n -> p k n", p=128)[:, :, 256 * c:256 * c + 256], *wq_used[n])

        a_free = []

        def load_counts(rel):
            for k in range(NT):
                a, rk = k % 2, ROWS[k]
                t0 = dma(SP, s_ar[a], ar[a][0:rk, :], TR[rel * N + 128 * k:rel * N + 128 * k + rk, :], t_tr, *ar_used[a])
                tok = ac(lambda e, k=k, rk=rk, a=a: e.activation(a16[0:rk, k, :], ar[a][0:rk, :], ACT.Copy), t0, *a_free)
                ar_used[a] = [tok]
            return tok

        def apply(w, first):
            for q in range(4):
                n, t_w = load_q(w, q)
                for o in (2 * q, 2 * q + 1):
                    for c0, cn in CH:
                        b, ps = bank()
                        oo = 128 * (o % 2)
                        tok = mm(b, ps[:, 0:cn], [(wq[n][:, k, oo:oo + 128], mt[:, k, c0:c0 + cn]) for k in range(8)],
                                 t_w, t_mt)
                        if first:
                            free[b] = [dv(lambda e, o=o, c0=c0, cn=cn, ps=ps: e.tensor_scalar(
                                out=acc[:, o, c0:c0 + cn], in0=ps[:, 0:cn], scalar1=brel[:, o:o + 1], scalar2=None,
                                op0=ALU.add), tok, t_br, chain=False)]
                        else:
                            free[b] = [dv(lambda e, o=o, c0=c0, cn=cn, ps=ps: e.tensor_tensor(
                                acc[:, o, c0:c0 + cn], ps[:, 0:cn], acc[:, o, c0:c0 + cn], ALU.add),
                                tok, t_acc, chain=False)]
                wq_used[n] = [tok]

        t_acc = (V, 0)
        for rel in range(NREL):
            t_a = load_counts(rel)
            for c0, cn in CH:
                b, ps = bank()
                tok = mm(b, ps[:, 0:cn], [(ones16[0:ROWS[k], :], a16[0:ROWS[k], k, c0:c0 + cn]) for k in range(NT)], t_a)
                dv(lambda e, c0=c0, cn=cn, ps=ps: e.tensor_scalar(
                    out=ib[:, c0:c0 + cn], in0=ps[:, 0:cn], scalar1=1.0, scalar2=XS, op0=ALU.max, op1=ALU.mult), tok)
                free[b] = [dv(lambda e, c0=c0, cn=cn: e.reciprocal(ib[:, c0:c0 + cn], ib[:, c0:c0 + cn]))]
            t_ib = free[b][0]
            for c0, cn in CH:
                for f in range(8):
                    b, ps = bank()
                    tok = mm(b, ps[:, 0:cn], [(h[0:ROWS[k], k, 128 * f:128 * f + 128], a16[0:ROWS[k], k, c0:c0 + cn])
                                              for k in range(NT) for h in (xh, xo)], t_a)
                    t_mt = dv(lambda e, f=f, c0=c0, cn=cn, ps=ps: e.tensor_tensor(
                        mt[:, f, c0:c0 + cn], ps[:, 0:cn], ib[:, c0:c0 + cn], ALU.mult), tok, t_ib, chain=False)
                    free[b] = [t_mt]
            a_free = [tok]
            apply(wrel[rel], rel == 0)
            t_acc = (V, V.n)
        bar_dmas = [*s_ar, *s_wq, s_br]
        barrier()
        x3l = [at(f"x3l{i}", [128, D], F32, O + 40 + 4 * i) for i in range(4)]
        s_3l = [dsem(f"s_3l{i}") for i in range(4)]
        used = [[], [], [], []]
        for i in range(NT):
            r, a = ROWS[i], i % 4
            t_l = dma(SP, s_3l[a], x3l[a][0:r, :], X3[128 * i:128 * i + r, :], *used[a])
            used[a] = [transpose_rows(i, x3l[a], mt, [t_l])]
        t_mt = (A, A.n)
        apply(root, False)
        t_u = (V, V.n)
        bar_dmas = [*s_3l, *s_wq]
        barrier()

        rT = at("rT", [128, 8, N], F32, O + 40)
        th = [at(f"th{i}", [128, 418], F32, O + 80 + 2 * i) for i in range(3)]
        zz = [at(f"zz{i}", [128, 418], F32, O + 86 + 2 * i) for i in range(3)]
        used = [[], [], []]
        nq = 0
        for q in range(4):
            n1, t1 = load_q(wgate[0:D, :], q)
            n2, t2 = load_q(wgate[D:2 * D, :], q)
            for o in (2 * q, 2 * q + 1):
                oo = 128 * (o % 2)
                for c0, cn in CH:
                    b, ps = bank()
                    a = nq % 3
                    nq += 1
                    tok = mm(b, ps[:, 0:cn], [(wq[n1][:, k, oo:oo + 128], acc[:, k, c0:c0 + cn]) for k in range(8)] +
                             [(wq[n2][:, k, oo:oo + 128], mt[:, k, c0:c0 + cn]) for k in range(8)], t1, t2)
                    t3 = ac(lambda e, a=a, o=o, c0=c0, cn=cn: e.activation(th[a][:, 0:cn], acc[:, o, c0:c0 + cn], ACT.Tanh),
                            *used[a])
                    dv(lambda e, a=a, o=o, cn=cn, c0=c0: e.tensor_tensor(
                        th[a][:, 0:cn], th[a][:, 0:cn], mt[:, o, c0:c0 + cn], ALU.subtract), t3, chain=False)
                    free[b] = [dv(lambda e, a=a, o=o, cn=cn, ps=ps: e.scalar_tensor_tensor(
                        out=zz[a][:, 0:cn], in0=ps[:, 0:cn], scalar=bg[:, o:o + 1], in1=th[a][:, 0:cn],
                        op0=ALU.add, op1=ALU.mult), tok)]
                    t4 = dv(lambda e, a=a, o=o, c0=c0, cn=cn: e.scalar_tensor_tensor(
                        out=rT[:, o, c0:c0 + cn], in0=mt[:, o, c0:c0 + cn], scalar=2.0, in1=zz[a][:, 0:cn],
                        op0=ALU.mult, op1=ALU.add))
                    used[a] = [t4]
            wq_used[n1] = [tok]
            wq_used[n2] = [tok]
        t_r = (V, V.n)
        on = [at(f"on{i}", [128, D], F32, O + 92 + 4 * i) for i in range(3)]
        s_out = [dsem(f"s_out{i}") for i in range(3)]
        used = [[], [], []]
        for i in range(NT):
            r, a = ROWS[i], i % 3
            for h in range(2):
                b, ps = bank()
                for t in (*free[b], t_r):
                    PE.wait(t)
                for m in range(4):
                    f = (lambda e, m=m, h=h, ps=ps, i=i, r=r: e.transpose(
                        ps[0:r, 128 * m:128 * m + 128], rT[:, 4 * h + m, 128 * i:128 * i + r], ident[:, :]))
                    tok = PE.put(f, (), P if m == 3 else None, 1)
                free[b] = [ac(lambda e, h=h, ps=ps, r=r, a=a: e.activation(
                    on[a][0:r, 512 * h:512 * h + 512], ps[0:r, :], ACT.Copy), tok, *used[a])]
            t_n = layer_norm(i, on[a], on[a], a, deps=[(A, A.n)])
            used[a] = [dma(SP, s_out[a], out[128 * i:128 * i + r, :], on[a][0:r, :], t_n)]
        for s in dmas:
            SP.wait((s, s.n))

        block = ctx.enter_context(nc.Block())

        @block.sync
        def _(e):
            SP.run(e)

        @block.tensor
        def _(e):
            PE.run(e)

        @block.vector
        def _(e):
            DV.run(e)

        @block.scalar
        def _(e):
            AC.run(e)

        @block.gpsimd
        def _(e):
            PL.run(e)


def diag_logits(dv, zg, zh, ed, atb, xlx, xrn, i0, i1, r, dep):
    for i in range(i0, i1):
        dv(lambda e, i=i: e.tensor_tensor(zg[0:r, i, :].rearrange("p (h d) -> p h d", h=4), xlx[0:r, i, :, 0:64],
                                          xrn[0:r, i, :].rearrange("p (h d) -> p h d", h=4), ALU.add), dep)
        dv(lambda e, i=i: e.scalar_tensor_tensor(out=zh[0:r, i, :], in0=zg[0:r, i, :], scalar=0.2, in1=zg[0:r, i, :],
                                                 op0=ALU.mult, op1=ALU.max))
        dv(lambda e, i=i: e.tensor_tensor(zg[0:r, i, :], zh[0:r, i, :], atb[0:r, :], ALU.mult))
        t = dv(lambda e, i=i: e.tensor_reduce(out=ed[0:r, i, :], in_=zg[0:r, i, :].rearrange("p (h d) -> p h d", h=4),
                                              axis=AX.X, op=ALU.add))
    return t


_INS = ["x", "src", "dst", "edge_type_8", "L0_gnn_W", "L0_gnn_b", "L1_gnn_W_self0", "L1_gnn_W_neigh0", "L1_gnn_b0",
        "L1_gnn_W_self1", "L1_gnn_W_neigh1", "L1_gnn_b1", "L2_gnn_rms_w", "L2_gnn_W_down", "L2_gnn_Wl", "L2_gnn_Wr",
        "L2_gnn_att", "L2_gnn_W_up", "L3_gnn_weight", "L3_gnn_root", "L3_gnn_bias", "L3_gnn_w_gate", "L3_gnn_b_gate"]


def kernel(**inputs):
    import numpy as np
    import concourse.bacc as bacc
    from concourse.bass_utils import run_bass_kernel_spmd

    nc = bacc.Bacc("TRN2", target_bir_lowering=False, num_devices=1)
    arrays, args = {}, []
    for name in _INS:
        a = np.ascontiguousarray(inputs[name])
        arrays[f"in_{name}"] = a
        args.append(nc.dram_tensor(f"in_{name}", a.shape, mybir.dt.from_np(a.dtype), kind="ExternalInput").ap())
    args.append(nc.dram_tensor("out_0", (N, D), F32, kind="ExternalOutput").ap())
    program(nc, *args)
    r = run_bass_kernel_spmd(nc, [arrays], core_ids=[0])
    return r.results[0]["out_0"]
```

```python
from contextlib import ExitStack

import concourse.bass as bass
from concourse import mybir

F32 = mybir.dt.float32
F32R = mybir.dt.float32r
F16 = mybir.dt.float16
I32 = mybir.dt.int32
ALU = mybir.AluOpType
ACT = mybir.ActivationFunctionType
AX = mybir.AxisListType

N = 1250
D = 1024
NT = 10
EP = 125
ET = 170
NREL = 8
ROWS = [128] * 9 + [98]
HW = [640, 610]
HC = [[(0, 384), (384, 256)], [(0, 384), (384, 226)]]
CH = [(0, 418), (418, 416), (834, 416)]
TPAD = 1280
RPAD = 10240
LN_EPS = 1e-5
RMS_EPS = 1e-6
NEG = -3.0e38
XS = 1024.0
KB = 1024
BASE = 16512


class Sem:

    def __init__(self, h):
        self.h = h
        self.n = 0


class Queue:

    def __init__(self):
        self.items = []
        self.seen = {}

    def wait(self, tok):
        sem, v = tok
        if v > self.seen.get(sem, 0):
            self.seen[sem] = v
            self.items.append(lambda e: e.wait_ge(sem.h, v))

    def put(self, fn, deps, sem, k):
        last = {}
        for s, v in deps:
            last[s] = max(v, last.get(s, 0))
        for t in last.items():
            self.wait(t)
        if sem is None:
            self.items.append(fn)
            return None
        sem.n += k
        self.items.append(lambda e: fn(e).then_inc(sem.h, k))
        return (sem, sem.n)

    def run(self, e):
        for f in self.items:
            f(e)


def program(nc, x, src, dst, ety, w0, b0, ws0, wn0, bb0, ws1, wn1, bb1, rmsw, wdown, wl, wr, att, wup,
            wrel, root, bias, wgate, bgate, out):
    ctx = ExitStack()
    with ctx:
        def sem(name):
            return Sem(ctx.enter_context(nc.semaphore(name)))

        def at(name, shape, dt, kb):
            return nc.alloc_sbuf_tensor_at(name, shape, dt, offset=BASE + int(kb * KB))

        def dram(name, shape):
            return nc.dram_tensor(name, shape, F32, kind="Internal").ap()

        T0 = [dram(f"T0_{i}", (TPAD, N)) for i in range(3)]
        TR = dram("TR", (RPAD, N))
        EM = dram("EM", (TPAD, N * 4))
        X1 = dram("X1", (N, D))
        X2 = dram("X2", (N, D))
        HD = dram("HD", (N, D))
        ZD = dram("ZD", (N, D))
        XL = dram("XL", (N, 256))
        XR = dram("XR", (N, 256))

        PE, DV, AC, PL, SP = Queue(), Queue(), Queue(), Queue(), Queue()
        P, V, A, G = sem("P"), sem("V"), sem("A"), sem("G")
        dmas = []

        def dsem(name):
            s = sem(name)
            dmas.append(s)
            return s

        def pe(fn, *deps):
            return PE.put(fn, deps, P, 1)

        def dv(fn, *deps, chain=True):
            if chain:
                DV.wait((V, V.n))
            return DV.put(fn, deps, V, 1)

        def ac(fn, *deps):
            return AC.put(fn, deps, A, 1)

        def pl(fn, *deps):
            return PL.put(fn, deps, G, 1)

        def dma(q, s, o, i, *deps, scattered=False):
            return q.put(lambda e: e.dma_start(o, i, allow_slow_non_contiguous=scattered), deps, s, 16)

        def barrier(also=()):
            for q in (PE, DV, AC, SP):
                for s in (P, V, A, *bar_dmas, *also):
                    q.wait((s, s.n))

        banks = [ctx.enter_context(nc.psum_tensor(f"ps{i}", [128, 512], F32)) for i in range(8)]
        free = [[] for _ in range(8)]
        turn = [0]

        def bank(n=8):
            b = turn[0] % n
            turn[0] += 1
            return b, banks[b]

        def mm(b, ap, pairs, *deps):
            for t in (*free[b], *deps):
                PE.wait(t)
            n = len(pairs)
            for q, (l, r) in enumerate(pairs):
                f = (lambda e, l=l, r=r, q=q: e.matmul(ap, l, r, start=(q == 0), stop=(q == n - 1)))
                tok = PE.put(f, (), P if q == n - 1 else None, 1)
            return tok

        ident = at("ident", [128, 128], F32, 0)
        lmask = at("lmask", [128, 128], F32, 0.5)
        zero = at("zero", [128, 625], F32, 1)
        neg = at("neg", [128, 625], F32, 3.5)
        bc = at("bc", [128, D], F32, 6)
        ei = at("ei", [EP, 3, ET], I32, 10)
        ef = at("ef", [EP, 3, ET], F32, 12)
        key = at("key", [EP, 2, ET], F32, 14)
        cnt = at("cnt", [EP, 2, ET], F32, 15.375)
        dup = at("dup", [EP, 2, ET], F32, 16.75)
        adr = at("adr", [EP, 2, ET], I32, 18.125)
        eqj = at("eqj", [EP, 2, 125], F32, 19.5)
        trash_i = at("trash_i", [128, 2], I32, 20.5)
        trash = at("trash", [128, 2], F32, 20.53125)
        onesr = at("onesr", [128, 2], F32R, 20.5625)
        deg = at("deg", [128, 10], F32, 20.625)
        dis = at("dis", [128, 10], F32, 20.6875)
        t10 = at("t10", [128, 2, 10], F32, 20.75)
        dinv = at("dinv", [128, 10], F32, 20.875)
        st = at("st", [128, 3, 2, 6], F32, 20.9375)
        mv = at("mv", [128, 3, 12], F32, 21.125)
        rw = at("rw", [128, 8], F32, 21.3125)
        brel = at("brel", [128, 8], F32, 21.34375)
        bg = at("bg", [128, 8], F32, 21.375)
        ident16 = at("ident16", [128, 128], F16, 21.4375)
        onesf = at("onesf", [128, 2], F32, 21.6875)
        stb = at("stb", [128, NT, 2, 6], F32, 21.75)
        mvb = at("mvb", [128, NT, 2], F32, 22.25)
        rsd = at("rsd", [128, NT], F32, 22.34375)
        vpe = at("vpe", [128, NT], F32, 22.40625)
        nmr = at("nmr", [128, NT], F32, 22.46875)
        O = 22.53125

        g_zero = pl(lambda e: e.memset(zero[:, :], 0.0))
        g_neg = pl(lambda e: e.memset(neg[:, :], NEG))
        g0 = pl(lambda e: e.memset(ident[:, :], 0.0))
        g1 = pl(lambda e: e.memset(lmask[:, :], 1.0))
        pl(lambda e: e.affine_select(out=ident[:, :], in_=ident[:, :], compare_op=ALU.not_equal, fill=1.0, base=0,
                                     pattern=[[-1, 128]], channel_multiplier=1), g0)
        pl(lambda e: e.affine_select(out=lmask[:, :], in_=lmask[:, :], compare_op=ALU.is_gt, fill=0.0, base=0,
                                     pattern=[[-1, 128]], channel_multiplier=1), g1)
        pl(lambda e: e.iota(trash_i[:, 0:1], pattern=[[0, 1]], base=N * N, channel_multiplier=1))
        pl(lambda e: e.iota(trash_i[:, 1:2], pattern=[[0, 1]], base=NREL * N * N, channel_multiplier=1))
        g_const = pl(lambda e: e.memset(onesf[:, :], 1.0))

        s_e = dsem("s_e")
        for n, a in enumerate((src, dst, ety)):
            t_e = dma(SP, s_e, ei[:, n, :], a.rearrange("(p t) -> p t", t=ET))
        s_z0 = dsem("s_z0")
        for t in T0:
            t_z0 = dma(SP, s_z0, t.rearrange("(p a) (b f) -> p (a b) f", p=128, f=625),
                       zero[:, None, :].broadcast_to([128, 20, 625]), g_zero)
        s_w0 = dsem("s_w0")
        wnat = at("wnat", [128, 8, D], F32, O + 120)
        t_w0 = dma(SP, s_w0, wnat[:, :, :], w0.rearrange("(k p) n -> p k n", p=128))
        s_bc = dsem("s_bc")
        t_b = dma(SP, s_bc, bc[:, :], b0.rearrange("(a n) -> a n", a=1).broadcast_to([128, D]))

        t_ef = dv(lambda e: e.tensor_copy(ef[:, :, :], ei[:, :, :]), t_e)
        dv(lambda e: e.tensor_copy(trash[:, :], trash_i[:, :]), g_const, chain=False)
        dv(lambda e: e.tensor_copy(ident16[:, :], ident[:, :]), chain=False)
        dv(lambda e: e.tensor_copy(onesr[:, :], onesf[:, :]), chain=False)
        dv(lambda e: e.scalar_tensor_tensor(out=key[:, 0, :], in0=ef[:, 1, :], scalar=float(N), in1=ef[:, 0, :],
                                            op0=ALU.mult, op1=ALU.add))
        dv(lambda e: e.scalar_tensor_tensor(out=key[:, 1, :], in0=ef[:, 2, :], scalar=float(N), in1=ef[:, 0, :],
                                            op0=ALU.mult, op1=ALU.add))
        t_key = dv(lambda e: e.scalar_tensor_tensor(out=key[:, 1, :], in0=key[:, 1, :], scalar=float(N),
                                                    in1=ef[:, 1, :], op0=ALU.mult, op1=ALU.add))
        t_adr = {}

        def dedupe(w, t0, n):
            for g in range(t0, t0 + n, 4):
                ts = list(range(g, min(g + 4, t0 + n)))
                b, ps = bank()
                for t in free[b]:
                    PE.wait(t)
                for m, t in enumerate(ts):
                    tok = mm(b, ps[0:EP, 125 * m:125 * m + 125],
                             [(key[:, w, t:t + 1].broadcast_to([EP, EP]), ident[0:EP, 0:EP])], t_key, g_const)
                for m, t in enumerate(ts):
                    pv = ps[0:EP, 125 * m:125 * m + 125]
                    dv(lambda e, pv=pv, t=t: e.tensor_scalar(
                        out=eqj[:, 0, :], in0=pv, scalar1=key[:, w, t:t + 1], scalar2=0.0, op0=ALU.is_equal,
                        op1=ALU.add, accum_out=cnt[:, w, t:t + 1]), tok)
                    last = dv(lambda e, pv=pv, t=t: e.scalar_tensor_tensor(
                        out=eqj[:, 1, :], in0=pv, scalar=key[:, w, t:t + 1], in1=lmask[0:EP, 0:125],
                        op0=ALU.is_equal, op1=ALU.mult, accum_out=dup[:, w, t:t + 1]))
                free[b] = [last]
            s = slice(t0, t0 + n)
            dv(lambda e: e.tensor_scalar(out=dup[:, w, s], in0=dup[:, w, s], scalar1=1.0, scalar2=None, op0=ALU.min))
            dv(lambda e: e.tensor_scalar(out=ef[:, w, s], in0=key[:, w, s], scalar1=trash[0:EP, w:w + 1],
                                         scalar2=-1.0, op0=ALU.subtract, op1=ALU.mult))
            dv(lambda e: e.tensor_tensor(ef[:, w, s], ef[:, w, s], dup[:, w, s], ALU.mult))
            tok = dv(lambda e: e.tensor_tensor(adr[:, w, s], ef[:, w, s], key[:, w, s], ALU.add))
            for t in range(t0, t0 + n):
                t_adr[w, t] = tok

        for q in range(5):
            dedupe(0, 34 * q, 34)

        def scatter(s, table, w, t, bound, *deps):
            flat = table.rearrange("a b -> (a b)").rearrange("(c d) -> c d", d=1)
            return PL.put(lambda e: e.indirect_dma_start(
                out=flat, out_offset=bass.IndirectOffsetOnAxis(ap=adr[:, w, t:t + 1], axis=0),
                in_=cnt[:, w, t:t + 1], in_offset=None, bounds_check=bound, oob_is_err=True, compute_op=ALU.add),
                deps, s, 16)

        s_t0 = [dsem(f"s_t0{i}") for i in range(3)]
        for t in range(ET):
            s = s_t0[t % 3]
            scatter(s, T0[t % 3], 0, t, TPAD * N - 1, t_z0, (s, s.n), t_adr[0, t])
        t_t0 = [(s, s.n) for s in s_t0]

        wt = at("wt", [128, 8, D], F32, O + 80)
        xT = at("xT", [128, 8, N], F32, O)
        yraw = at("yraw", [128, NT, D], F32, O + 40)
        xin = [at(f"xin{i}", [128, D], F32, O + 152 + 4 * i) for i in range(3)]
        s_xin = [dsem(f"s_xin{i}") for i in range(3)]
        s_xin_use = [[], [], []]
        bar_dmas = []

        def transpose_rows(i, tile, dst_t, deps, scale=None, use=None):
            r = ROWS[i]
            for h in range(2):
                b, ps = bank()
                for t in (*free[b], *deps):
                    PE.wait(t)
                for m in range(4):
                    k = 4 * h + m
                    f = (lambda e, k=k, m=m, ps=ps: e.transpose(
                        ps[:, 128 * m:128 * m + r], tile[0:r, 128 * k:128 * k + 128], ident[0:r, 0:r]))
                    tok = PE.put(f, (), P if m == 3 else None, 1)
                pv = ps[:, :].rearrange("p (m c) -> p m c", m=4)[:, :, 0:r]
                if scale is None:
                    free[b] = [ac(lambda e, pv=pv, h=h: e.activation(
                        dst_t[:, 4 * h:4 * h + 4, 128 * i:128 * i + r], pv, ACT.Copy), tok)]
                else:
                    for m in range(4):
                        k = 4 * h + m
                        free[b] = [ac(lambda e, pv=pv, k=k, m=m: e.mul(
                            dst_t[:, k, 128 * i:128 * i + r], pv[:, m, :], scale[:, k:k + 1]), tok)]
            return tok

        PE.wait(g_const)
        for i in range(NT):
            r = ROWS[i]
            t_x = dma(SP, s_xin[i % 3], xin[i % 3][0:r, :], x[128 * i:128 * i + r, :], *s_xin_use[i % 3])
            s_xin_use[i % 3] = [transpose_rows(i, xin[i % 3], xT, [t_x])]
        for k in range(8):
            for h in range(2):
                b, ps = bank()
                for t in (*free[b], t_w0):
                    PE.wait(t)
                for m in range(4):
                    o = 4 * h + m
                    f = (lambda e, k=k, m=m, o=o, ps=ps: e.transpose(
                        ps[:, 128 * m:128 * m + 128], wnat[:, o, 128 * k:128 * k + 128], ident[:, :]))
                    tok = PE.put(f, (), P if m == 3 else None, 1)
                free[b] = [ac(lambda e, k=k, h=h, ps=ps: e.activation(
                    wt[:, k, 512 * h:512 * h + 512], ps[:, :], ACT.Copy), tok)]
        t_wt = (A, A.n)
        for i in range(NT):
            r = ROWS[i]
            for j in range(2):
                b, ps = bank()
                tok = mm(b, ps[0:r, :], [(xT[:, k, 128 * i:128 * i + r], wt[:, k, 512 * j:512 * j + 512])
                                         for k in range(8)], t_wt)
                free[b] = [dv(lambda e, i=i, j=j, r=r, ps=ps: e.tensor_tensor(
                    yraw[0:r, i, 512 * j:512 * j + 512], ps[0:r, :], bc[0:r, 512 * j:512 * j + 512], ALU.add),
                    tok, t_b, chain=False)]
        for q in range(5):
            dedupe(1, 34 * q, 34)

        s_z1 = dsem("s_z1")
        for c in range(4):
            t_z1 = dma(SP, s_z1, TR[2560 * c:2560 * c + 2560, :].rearrange("(p a) (b f) -> p (a b) f", p=128, f=625),
                       zero[:, None, :].broadcast_to([128, 40, 625]))
        s_tr = dsem("s_tr")
        for t in range(ET):
            scatter(s_tr, TR, 1, t, RPAD * N - 1, t_z1, (s_tr, s_tr.n), t_adr[1, t])
        t_tr = (s_tr, s_tr.n)
        s_em = dsem("s_em")
        for c in range(2):
            t_em = dma(SP, s_em, EM[640 * c:640 * c + 640, :].rearrange("(p a) (b f) -> p (a b) f", p=128, f=625),
                       neg[:, None, :].broadcast_to([128, 40, 625]), g_neg)

        bar_dmas = [s_w0, s_bc, *s_xin]
        barrier()
        bp = at("bp", [128, NT, N], F32R, O + 120)
        slab = [[at(f"slab{a}{i}", [128, N], F32, O + 5 * (3 * a + i)) for i in range(3)] for a in range(2)]
        s_sl = [[dsem(f"s_sl{a}{i}") for i in range(3)] for a in range(2)]
        used = [[], []]
        for i in range(NT):
            r, a = ROWS[i], i % 2
            toks = [dma(SP, s_sl[a][n], slab[a][n][0:r, :], T0[n][128 * i:128 * i + r, :], t_t0[n], *used[a])
                    for n in range(3)]
            dv(lambda e, a=a, r=r: e.tensor_tensor(slab[a][0][0:r, :], slab[a][0][0:r, :], slab[a][1][0:r, :], ALU.add),
               *toks)
            dv(lambda e, a=a, r=r: e.tensor_tensor(slab[a][0][0:r, :], slab[a][0][0:r, :], slab[a][2][0:r, :], ALU.add))
            dv(lambda e, a=a, r=r, i=i: e.tensor_tensor(
                slab[a][0][0:r, 128 * i:128 * i + r], slab[a][0][0:r, 128 * i:128 * i + r], ident[0:r, 0:r], ALU.add))
            used[a] = [dv(lambda e, a=a, r=r, i=i: e.tensor_copy(bp[0:r, i, :], slab[a][0][0:r, :]))]
        t_bp = used[1][0]

        def degrees(mat, dst, *deps):
            b, ps = bank()
            t0 = dv(lambda e: e.memset(dst[:, :], 1.0))
            for i in range(NT):
                tok = mm(b, ps[0:ROWS[i], 2 * i:2 * i + 2],
                         [(mat[0:ROWS[k], k, 128 * i:128 * i + ROWS[i]], onesr[0:ROWS[k], :]) for k in range(NT)], *deps)
            pv = ps[:, 0:20].rearrange("p (i c) -> p i c", c=2)
            dv(lambda e: e.tensor_copy(dst[:, 0:9], pv[:, 0:9, 0]), tok)
            free[b] = [dv(lambda e: e.tensor_copy(dst[0:98, 9:10], pv[0:98, 9:10, 0]), tok)]

        def rsqrt(y, v, t, deps=()):
            s = ac(lambda e: e.activation(y, v, ACT.Sqrt), (V, V.n), *deps)
            dv(lambda e: e.reciprocal(y, y), s)
            dv(lambda e: e.tensor_tensor(t, v, y, ALU.mult))
            dv(lambda e: e.tensor_tensor(t, t, y, ALU.mult))
            dv(lambda e: e.tensor_scalar(out=t, in0=t, scalar1=-0.5, scalar2=1.5, op0=ALU.mult, op1=ALU.add))
            return dv(lambda e: e.tensor_tensor(y, y, t, ALU.mult))

        def stats(i, j, v, deps):
            return dv(lambda e: e.bn_stats(stb[0:ROWS[i], i, j, :], v), *deps, chain=False)

        def aggregate(i):
            r = ROWS[i]
            return dv(lambda e: e.bn_aggr(mvb[0:r, i, :], stb[0:r, i, :, :].rearrange("p a b -> p (a b)")))

        def rstd(i0, i1):
            dv(lambda e: e.tensor_scalar(out=vpe[:, i0:i1], in0=mvb[:, i0:i1, 1], scalar1=LN_EPS, scalar2=None, op0=ALU.add))
            rsqrt(rsd[:, i0:i1], vpe[:, i0:i1], nmr[:, i0:i1])
            return dv(lambda e: e.scalar_tensor_tensor(out=nmr[:, i0:i1], in0=mvb[:, i0:i1, 0], scalar=-1.0,
                                                       in1=rsd[:, i0:i1], op0=ALU.mult, op1=ALU.mult))

        degrees(bp, deg, t_bp)
        rsqrt(dis[:, :], deg[:, :], t10[:, 0, :])

        yhi = at("yhi", [128, NT, D], F32R, O + 40)
        ylo = at("ylo", [128, NT, D], F32R, O + 80)
        yt = [at(f"yt{i}", [128, D], F32, O + 30 + 4 * i) for i in range(2)]
        for i in range(NT):
            r, a = ROWS[i], i % 2
            t0 = dv(lambda e, i=i, r=r, a=a: e.tensor_scalar(
                out=yt[a][0:r, :], in0=yraw[0:r, i, :], scalar1=dis[0:r, i:i + 1], scalar2=None, op0=ALU.mult))
            t1 = ac(lambda e, i=i, r=r, a=a: e.activation(yhi[0:r, i, :], yt[a][0:r, :], ACT.Copy), t0)
            t_y = dv(lambda e, i=i, r=r, a=a: e.tensor_tensor(
                ylo[0:r, i, :], yt[a][0:r, :], yhi[0:r, i, :].bitcast(F32), ALU.subtract), t1)
        barrier()

        zt = [at(f"zt{i}", [128, D], F32, O + 169 + 4 * i) for i in range(2)]
        xres = [at(f"xres{i}", [128, D], F32, O + 177 + 4 * i) for i in range(2)]
        s_xr = [dsem(f"s_xr{i}") for i in range(2)]
        s_xo = [dsem(f"s_xo{i}") for i in range(2)]

        def layer_norm(i, z, o, m, deps=()):
            r = ROWS[i]
            for h in range(2):
                dv(lambda e, h=h: e.bn_stats(st[0:r, m, h, :], z[0:r, 512 * h:512 * h + 512]), *deps, chain=(h == 0))
            dv(lambda e: e.bn_aggr(mv[0:r, m, 0:2], st[0:r, m, :, :].rearrange("p a b -> p (a b)")))
            dv(lambda e: e.tensor_scalar(out=mv[0:r, m, 2:3], in0=mv[0:r, m, 1:2], scalar1=LN_EPS, scalar2=None,
                                         op0=ALU.add))
            rsqrt(mv[0:r, m, 3:4], mv[0:r, m, 2:3], mv[0:r, m, 4:5])
            return dv(lambda e: e.tensor_scalar(out=o[0:r, :], in0=z[0:r, :], scalar1=mv[0:r, m, 0:1],
                                                scalar2=mv[0:r, m, 3:4], op0=ALU.subtract, op1=ALU.mult))

        used = [[], []]
        for i in range(NT):
            r, a = ROWS[i], i % 2
            t_x = dma(SP, s_xr[a], xres[a][0:r, :], x[128 * i:128 * i + r, :], *used[a])
            for j in range(2):
                b, ps = bank()
                c = slice(512 * j, 512 * j + 512)
                tok = mm(b, ps[0:r, :], [(bp[0:ROWS[k], k, 128 * i:128 * i + r], y[0:ROWS[k], k, c])
                                         for k in range(NT) for y in (yhi, ylo)])
                free[b] = [dv(lambda e, i=i, r=r, a=a, c=c, ps=ps: e.scalar_tensor_tensor(
                    out=zt[a][0:r, c], in0=ps[0:r, :], scalar=dis[0:r, i:i + 1], in1=xres[a][0:r, c],
                    op0=ALU.mult, op1=ALU.add), tok, t_x, *used[a], chain=False)]
            t_n = layer_norm(i, zt[a], zt[a], a)
            t_o = dma(AC, s_xo[a], X1[128 * i:128 * i + r, :], zt[a][0:r, :], t_n)
            t_p = transpose_rows(i, zt[a], xT, [t_n])
            used[a] = [t_n, t_o, t_p]
        bar_dmas = [*s_xr, *s_xo]
        barrier()

        am = at("am", [128, NT, N], F32R, O + 40)
        for k in range(NT):
            rk = ROWS[k]
            for g in range(3):
                b, ps = bank()
                ds = list(range(4 * g, min(4 * g + 4, NT)))
                for t in free[b]:
                    PE.wait(t)
                for m, d in enumerate(ds):
                    f = (lambda e, m=m, d=d, ps=ps, k=k, rk=rk: e.transpose(
                        ps[0:rk, 128 * m:128 * m + ROWS[d]],
                        bp[0:ROWS[d], d, 128 * k:128 * k + rk].bitcast(F32), ident[0:ROWS[d], 0:ROWS[d]]))
                    tok = PE.put(f, (), P if d == ds[-1] else None, 1)
                w = sum(ROWS[d] for d in ds)
                free[b] = [ac(lambda e, ps=ps, k=k, g=g, rk=rk, w=w: e.activation(
                    am[0:rk, k, 512 * g:512 * g + w], ps[0:rk, 0:w], ACT.Copy), tok)]
        for k in range(NT):
            rk = ROWS[k]
            blk = (lambda k=k, rk=rk: am[0:rk, k, 128 * k:128 * k + rk])
            t_am = dv(lambda e, blk=blk, rk=rk: e.tensor_tensor(blk(), blk().bitcast(F32), ident[0:rk, 0:rk],
                                                                ALU.subtract), (A, A.n), chain=False)
        degrees(am, deg, t_am)
        dv(lambda e: e.tensor_scalar(out=deg[:, :], in0=deg[:, :], scalar1=1.0, scalar2=None, op0=ALU.max))
        dv(lambda e: e.reciprocal(dinv[:, :], deg[:, :]))
        barrier()

        wb = [at(f"wb{i}", [128, 8, 512], F32, O + 129 + 16 * i) for i in range(3)]
        hhi = at("hhi", [128, NT, 512], F32R, O + 89)
        hlo = at("hlo", [128, NT, 512], F32R, O + 109)
        tt = [at(f"tt{i}", [128, 512], F32, O + 177 + 2 * i) for i in range(4)]
        s_wb = [dsem(f"s_wb{i}") for i in range(3)]
        s_ho = [dsem(f"s_ho{i}") for i in range(4)]
        wb_used = [[], [], []]
        tt_used = [[], [], [], []]
        wturn = [0]

        def load_w(w, j):
            n = wturn[0] % 3
            wturn[0] += 1
            return n, dma(SP, s_wb[n], wb[n][:, :, :],
                          w.rearrange("(k p) n -> p k n", p=128)[:, :, 512 * j:512 * j + 512], *wb_used[n])

        def sage(ws, wn, bias_v, dest, relu):
            t_b = dma(SP, s_bc, bc[:, :], bias_v.rearrange("(a n) -> a n", a=1).broadcast_to([128, D]))
            for j in range(2):
                n1, t_n = load_w(wn, j)
                n2, t_s = load_w(ws, j)
                for i in range(NT):
                    r = ROWS[i]
                    b, ps = bank()
                    tok = mm(b, ps[0:r, :], [(xT[:, k, 128 * i:128 * i + r], wb[n1][:, k, :]) for k in range(8)], t_n)
                    wb_used[n1] = [tok]
                    t1 = ac(lambda e, i=i, r=r, ps=ps: e.activation(hhi[0:r, i, :], ps[0:r, :], ACT.Copy), tok)
                    t_h = dv(lambda e, i=i, r=r, ps=ps: e.tensor_tensor(
                        hlo[0:r, i, :], ps[0:r, :], hhi[0:r, i, :].bitcast(F32), ALU.subtract), t1, chain=False)
                    free[b] = [t_h]
                for i in range(NT):
                    r = ROWS[i]
                    a = (NT * j + i) % 4
                    b, ps = bank()
                    tok = mm(b, ps[0:r, :], [(xT[:, k, 128 * i:128 * i + r], wb[n2][:, k, :]) for k in range(8)], t_s)
                    wb_used[n2] = [tok]
                    free[b] = [dv(lambda e, r=r, a=a, j=j, ps=ps: e.tensor_tensor(
                        tt[a][0:r, :], ps[0:r, :], bc[0:r, 512 * j:512 * j + 512], ALU.add),
                        tok, t_b, *tt_used[a], chain=False)]
                    b, ps = bank()
                    tok = mm(b, ps[0:r, :], [(am[0:ROWS[k], k, 128 * i:128 * i + r], h[0:ROWS[k], k, :])
                                             for k in range(NT) for h in (hhi, hlo)], t_h)
                    last = dv(lambda e, i=i, r=r, a=a, ps=ps: e.scalar_tensor_tensor(
                        out=tt[a][0:r, :], in0=ps[0:r, :], scalar=dinv[0:r, i:i + 1], in1=tt[a][0:r, :],
                        op0=ALU.mult, op1=ALU.add), tok)
                    free[b] = [last]
                    if relu:
                        last = dv(lambda e, r=r, a=a: e.tensor_scalar(
                            out=tt[a][0:r, :], in0=tt[a][0:r, :], scalar1=0.0, scalar2=None, op0=ALU.max))
                    tt_used[a] = [dma(AC, s_ho[a], dest[128 * i:128 * i + r, 512 * j:512 * j + 512],
                                      tt[a][0:r, :], last)]

        bar_dmas = [*s_wb, *s_ho, s_bc]
        sage(ws0, wn0, bb0, HD, True)
        barrier()
        lt = [at(f"lt{i}", [128, D], F32, O + 89 + 4 * i) for i in range(4)]
        s_lt = [dsem(f"s_lt{i}") for i in range(4)]
        used = [[], [], [], []]
        for i in range(NT):
            r, a = ROWS[i], i % 4
            t_l = dma(SP, s_lt[a], lt[a][0:r, :], HD[128 * i:128 * i + r, :], *used[a])
            used[a] = [transpose_rows(i, lt[a], xT, [t_l])]
        bar_dmas = [*s_lt]
        barrier()
        bar_dmas = [*s_wb, *s_ho, s_bc]
        sage(ws1, wn1, bb1, ZD, False)
        barrier()

        t_rw = dma(SP, s_bc, rw[:, :], rmsw.rearrange("(k p) -> p k", p=128), scattered=True)
        zl = [at(f"zl{i}", [128, D], F32, O + 89 + 4 * i) for i in range(3)]
        xl2 = [at(f"xl2{i}", [128, D], F32, O + 101 + 4 * i) for i in range(3)]
        xn = [at(f"xn{i}", [128, D], F32, O + 113 + 4 * i) for i in range(3)]
        s_zl = [dsem(f"s_zl{i}") for i in range(3)]
        s_x2 = [dsem(f"s_x2{i}") for i in range(3)]
        used = [[], [], []]
        for i in range(NT):
            r, a = ROWS[i], i % 3
            t0 = dma(SP, s_zl[a], zl[a][0:r, :], ZD[128 * i:128 * i + r, :], *used[a])
            t1 = dma(SP, s_zl[a], xl2[a][0:r, :], X1[128 * i:128 * i + r, :], *used[a])
            dv(lambda e, a=a, r=r: e.tensor_tensor(zl[a][0:r, :], zl[a][0:r, :], xl2[a][0:r, :], ALU.add), t0, t1)
            t_n = layer_norm(i, zl[a], zl[a], a)
            t_o = dma(AC, s_x2[a], X2[128 * i:128 * i + r, :], zl[a][0:r, :], t_n)
            t_q = ac(lambda e, a=a, r=r: e.activation(xn[a][0:r, :], zl[a][0:r, :], ACT.Square,
                                                      accum_out=mv[0:r, a, 5:6]), t_n, *used[a])
            dv(lambda e, a=a, r=r: e.tensor_scalar(out=mv[0:r, a, 6:7], in0=mv[0:r, a, 5:6], scalar1=1.0 / D,
                                                   scalar2=RMS_EPS, op0=ALU.mult, op1=ALU.add), t_q)
            rsqrt(mv[0:r, a, 7:8], mv[0:r, a, 6:7], mv[0:r, a, 8:9])
            t_s = dv(lambda e, a=a, r=r: e.tensor_scalar(out=xn[a][0:r, :], in0=zl[a][0:r, :],
                                                         scalar1=mv[0:r, a, 7:8], scalar2=None, op0=ALU.mult))
            AC.wait(t_rw)
            t_p = transpose_rows(i, xn[a], xT, [t_s], scale=rw)
            used[a] = [t_n, t_s, t_o, t_p]
        bar_dmas = [*s_zl, *s_x2, s_bc]
        barrier()

        wd = at("wd", [128, 8, 256], F32, O + 89)
        wlr = at("wlr", [128, 2, 2, 256], F32, O + 97)
        xd = at("xd", [128, 2, N], F32, O + 101)
        xlx = at("xlx", [128, NT, 4, 65], F32, O + 111)
        xrn = at("xrn", [128, NT, 256], F32, O + 121.5)
        atb = at("atb", [128, 256], F32, O + 131.5)
        zg = at("zg", [128, NT, 256], F32, O + 132.5)
        zh = at("zh", [128, NT, 256], F32, O + 142.5)
        ed = at("ed", [128, NT, 4], F32, O + 152.5)
        s_wd = dsem("s_wd")
        dma(SP, s_wd, wd[:, :, :], wdown.rearrange("(k p) n -> p k n", p=128))
        dma(SP, s_wd, wlr[:, 0, :, :], wl.rearrange("(k p) n -> p k n", p=128))
        dma(SP, s_wd, wlr[:, 1, :, :], wr.rearrange("(k p) n -> p k n", p=128))
        t_wd = dma(SP, s_wd, atb[:, :],
                   att.rearrange("h d -> (h d)").rearrange("(a n) -> a n", a=1).broadcast_to([128, 256]))
        for o in range(2):
            for c0, cn in CH:
                b, ps = bank()
                tok = mm(b, ps[:, 0:cn], [(wd[:, k, 128 * o:128 * o + 128], xT[:, k, c0:c0 + cn]) for k in range(8)], t_wd)
                free[b] = [ac(lambda e, o=o, c0=c0, cn=cn, ps=ps: e.activation(
                    xd[:, o, c0:c0 + cn], ps[:, 0:cn], ACT.Copy), tok)]
        t_xd = (A, A.n)
        t_on = dv(lambda e: e.memset(xlx[:, :, :, 64:65], 1.0))
        s_xl = dsem("s_xl")
        for i in range(NT):
            r = ROWS[i]
            b, ps = bank()
            for w in range(2):
                tok = mm(b, ps[0:r, 256 * w:256 * w + 256],
                         [(xd[:, k, 128 * i:128 * i + r], wlr[:, w, k, :]) for k in range(2)], t_xd, t_wd)
            dv(lambda e, i=i, r=r, ps=ps: e.tensor_copy(
                xlx[0:r, i, :, 0:64], ps[0:r, 0:256].rearrange("p (h d) -> p h d", h=4)), tok, chain=False)
            t0 = dv(lambda e, i=i, r=r, ps=ps: e.tensor_copy(xrn[0:r, i, :], ps[0:r, 256:512]), chain=False)
            free[b] = [t0]
            dma(AC, s_xl, XL[128 * i:128 * i + r, :].rearrange("p (h d) -> p h d", h=4), xlx[0:r, i, :, 0:64], t0)
            t_xl = dma(AC, s_xl, XR[128 * i:128 * i + r, :], xrn[0:r, i, :], t0)

        def logits(z, tmp, tgt, m, xa, xb, *deps):
            pr = z.shape[0]
            dv(lambda e: e.tensor_tensor(z, xa, xb, ALU.add), *deps, chain=False)
            dv(lambda e: e.scalar_tensor_tensor(out=tmp.rearrange("p m f -> p (m f)"), in0=z.rearrange("p m f -> p (m f)"),
                                                scalar=0.2, in1=z.rearrange("p m f -> p (m f)"), op0=ALU.mult,
                                                op1=ALU.max))
            dv(lambda e: e.tensor_tensor(z, tmp, atb[0:pr, None, :].broadcast_to([pr, m, 256]), ALU.mult))
            return dv(lambda e: e.tensor_reduce(out=tgt, in_=z.rearrange("p m (h d) -> p (m h) d", h=4), axis=AX.X,
                                                op=ALU.add))

        for i0, i1, r in ((0, 9, 128), (9, 10, 98)):
            t_ed = diag_logits(dv, zg, zh, ed, atb, xlx, xrn, i0, i1, r, t_wd)
        s_ed = dsem("s_ed")
        diag = EM.rearrange("a (b h) -> (a b) h", h=4)
        for i in range(NT):
            r = ROWS[i]
            a0 = 128 * i * (N + 1)
            t_dg = dma(AC, s_ed, diag[a0:a0 + (r - 1) * (N + 1) + 1:N + 1, :], ed[0:r, i, :], t_ed, t_em)

        NB = 5
        gl = [at(f"gl{i}", [EP, NB, 256], F32, O + 153 + 5 * i) for i in range(2)]
        gr = [at(f"gr{i}", [EP, NB, 256], F32, O + 163 + 5 * i) for i in range(2)]
        ee = at("ee", [EP, ET, 4], F32, O + 173)
        s_g = [dsem(f"s_g{i}") for i in range(2)]
        s_sc = dsem("s_sc")
        t_ee = {}
        used = [[], []]
        LAG = 8

        def put_logits(t):
            PL.put(lambda e: e.indirect_dma_start(
                out=diag, out_offset=bass.IndirectOffsetOnAxis(ap=adr[:, 0, t:t + 1], axis=0),
                in_=ee[:, t, :], in_offset=None, bounds_check=TPAD * N - 1, oob_is_err=True),
                (t_ee[t], t_dg, (s_sc, s_sc.n)), s_sc, 16)

        for t in range(ET):
            a, m = (t // NB) % 2, t % NB
            for buf, tab, row in ((gl, XL, 0), (gr, XR, 1)):
                tok = PL.put(lambda e, buf=buf, tab=tab, row=row, a=a, m=m, t=t: e.indirect_dma_start(
                    out=buf[a][:, m, :], out_offset=None, in_=tab,
                    in_offset=bass.IndirectOffsetOnAxis(ap=ei[:, row, t:t + 1], axis=0)),
                    (t_xl, *used[a]), s_g[a], 16)
            if m == NB - 1:
                last = logits(gl[a][:, :, :], gr[a][:, :, :],
                              ee[:, t - NB + 1:t + 1, :].rearrange("p m h -> p (m h)"), NB,
                              gl[a][:, :, :], gr[a][:, :, :], tok)
                used[a] = [last]
                for q in range(t - NB + 1, t + 1):
                    t_ee[q] = last
            if t >= LAG:
                put_logits(t - LAG)
        for t in range(ET - LAG, ET):
            put_logits(t)
        t_sc = (s_sc, s_sc.n)
        for k in range(NT):
            rk = ROWS[k]
            blk = (lambda k=k, rk=rk: am[0:rk, k, 128 * k:128 * k + rk])
            t_am = dv(lambda e, blk=blk, rk=rk: e.tensor_tensor(blk(), blk().bitcast(F32), ident[0:rk, 0:rk],
                                                                ALU.add), chain=False)
        bar_dmas = [s_wd, s_xl, s_ed, *s_g]
        barrier()

        eb = [at(f"eb{i}", [128, N, 4], F32, O + 123 + 19.75 * i) for i in range(2)]
        pb = [at(f"pb{i}", [128, N], F32, O + 30 + 4.90625 * i) for i in range(2)]
        pb += [at(f"pb{i + 2}", [128, N], F32, O + 163 + 4.90625 * i) for i in range(4)]
        NPT = 11
        pt = [at(f"pt{i}", [128, 4, 128], F32, O + 89 + 2 * i) for i in range(NPT)]
        gn = at("gn", [128, NT, 256], F32, O)
        gT = at("gT", [128, 2, N], F32, O + 10)
        wu = at("wu", [128, 2, D], F32, O + 20)
        mx = at("mx", [128, 2, 4], F32, O + 28)
        rd = at("rd", [128, 2, 4], F32, O + 28.0625)
        s_eb = [dsem(f"s_eb{i}") for i in range(2)]
        t_wu = dma(SP, s_wd, wu[:, :, :], wup.rearrange("(k p) n -> p k n", p=128))
        t_exp, t_eb, eb_used, t_max = {}, {}, [[], []], {}
        pt_used = [[] for _ in range(NPT)]
        pb_used = [[] for _ in range(6)]
        pturn = [0]
        parts_of, t_sum, t_gn = {}, {}, {}

        def load_logits(i):
            r, a = ROWS[i], i % 2
            t_eb[i] = dma(SP, s_eb[a], eb[a][0:r, :, :], EM[128 * i:128 * i + r, :].rearrange("p (s h) -> p s h", h=4),
                          t_sc, *eb_used[a])

        def maxima(i):
            r, a = ROWS[i], i % 2
            t_max[i] = dv(lambda e: e.tensor_reduce(
                out=mx[0:r, a, :], in_=eb[a][0:r, :, :].rearrange("p s h -> p h s"), axis=AX.X, op=ALU.max, negate=True),
                t_eb[i], *eb_used[a], chain=False)

        def exponentials(i, h):
            r, a, n = ROWS[i], i % 2, (4 * i + h) % 6
            t_exp[i, h] = ac(lambda e: e.activation(pb[n][0:r, :], eb[a][0:r, :, h], ACT.Exp, bias=mx[0:r, a, h:h + 1]),
                             t_max[i], *pb_used[n])
            if h == 3:
                eb_used[a] = [t_exp[i, h]]

        def turn_over(i, h):
            r, s = ROWS[i], (4 * i + h) % 6
            parts_of[i, h] = []
            for g in range(3):
                ks = list(range(4 * g, min(4 * g + 4, NT)))
                b, ps = bank(6)
                for t in (*free[b], t_exp[i, h]):
                    PE.wait(t)
                for m, k in enumerate(ks):
                    f = (lambda e, m=m, k=k, ps=ps: e.transpose(
                        ps[0:ROWS[k], 128 * m:128 * m + r], pb[s][0:r, 128 * k:128 * k + ROWS[k]], ident[0:r, 0:r]))
                    tok = PE.put(f, (), P if k == ks[-1] else None, 1)
                n = pturn[0] % NPT
                pturn[0] += 1
                for kk, rk in ([(ks, 128)] if g < 2 else [(ks[0:1], 128), (ks[1:2], 98)]):
                    m0 = kk[0] - ks[0]
                    pv = ps[0:rk, :].rearrange("p (m c) -> p m c", m=4)[:, m0:m0 + len(kk), 0:r]
                    last = dv(lambda e, n=n, kk=kk, rk=rk, m0=m0, pv=pv: e.tensor_tensor(
                        pt[n][0:rk, m0:m0 + len(kk), 0:r], pv,
                        am[0:rk, kk[0]:kk[0] + len(kk), 128 * i:128 * i + r].bitcast(F32), ALU.mult),
                        tok, t_am, *pt_used[n], chain=False)
                free[b] = [last]
                parts_of[i, h] += [(n, k, m, last) for m, k in enumerate(ks)]
            pb_used[s] = [tok]

        def weighted_sum(i, h):
            r, b = ROWS[i], 6 + i % 2
            prs = parts_of[i, h]
            tok = mm(b, banks[b][0:r, 65 * h:65 * h + 65],
                     [(pt[n][0:ROWS[k], m, 0:r], xlx[0:ROWS[k], k, h, :]) for n, k, m, _ in prs], prs[-1][3])
            for n, _, _, _ in prs:
                pt_used[n] = [tok]
            t_sum[i] = tok

        def normalise(i):
            r, a, b = ROWS[i], i % 2, 6 + i % 2
            pv = banks[b][0:r, 0:260].rearrange("p (h c) -> p h c", h=4)
            dv(lambda e: e.tensor_scalar(out=rd[0:r, a, :], in0=pv[:, :, 64], scalar1=1e-16, scalar2=None, op0=ALU.add),
               t_sum[i], chain=False)
            dv(lambda e: e.reciprocal(rd[0:r, a, :], rd[0:r, a, :]))
            t_gn[i] = dv(lambda e: e.tensor_tensor(
                gn[0:r, i, :].rearrange("p (h d) -> p h d", h=4), pv[:, :, 0:64],
                rd[0:r, a, :, None].broadcast_to([r, 4, 64]), ALU.mult))
            free[b] = [t_gn[i]]

        def turn_back(i):
            r = ROWS[i]
            b, ps = bank(6)
            for t in (*free[b], t_gn[i]):
                PE.wait(t)
            for k in range(2):
                f = (lambda e, k=k: e.transpose(
                    ps[:, 128 * k:128 * k + r], gn[0:r, i, 128 * k:128 * k + 128], ident[0:r, 0:r]))
                tok = PE.put(f, (), P if k == 1 else None, 1)
            free[b] = [ac(lambda e: e.activation(
                gT[:, :, 128 * i:128 * i + r], ps[:, 0:256].rearrange("p (k c) -> p k c", k=2)[:, :, 0:r], ACT.Copy), tok)]

        load_logits(0)
        load_logits(1)
        maxima(0)
        exponentials(0, 0)
        exponentials(0, 1)
        heads = [(i, h) for i in range(NT) for h in range(4)]
        for g, (i, h) in enumerate(heads):
            turn_over(i, h)
            if g + 2 < len(heads):
                i2, h2 = heads[g + 2]
                exponentials(i2, h2)
                if h2 == 3 and i2 + 2 < NT:
                    load_logits(i2 + 2)
            if h == 0 and i + 1 < NT:
                maxima(i + 1)
            if g > 0:
                weighted_sum(*heads[g - 1])
            if h == 1 and i > 0:
                normalise(i - 1)
            if h == 3 and i > 0:
                turn_back(i - 1)
        weighted_sum(NT - 1, 3)
        normalise(NT - 1)
        turn_back(NT - 1)
        t_gT = (A, A.n)

        z3 = [at(f"z3{i}", [128, D], F32, O + 123 + 4 * i) for i in range(NT)]
        s_2l = dsem("s_2l")
        t_2l = [dma(SP, s_2l, z3[i][0:ROWS[i], :], X2[128 * i:128 * i + ROWS[i], :], *eb_used[0],
                    *(eb_used[1] if i > 3 else ())) for i in range(NT)][-1]
        bar_dmas = [*s_eb, s_wd]
        barrier()
        mh = at("mh", [128, 8, 640], F32R, O)
        ml = at("ml", [128, 8, 640], F32R, O + 20)
        xh = at("xh", [128, NT, D], F16, O + 40)
        xo = at("xo", [128, NT, D], F16, O + 60)
        a16 = [at(f"a16{i}", [128, NT, 640], F16, O + 80 + 12.5 * i) for i in range(2)]
        acc = at("acc", [128, 8, N], F32, O + 123)
        wraw = [at(f"wraw{i}", [128, 8, 128], F32, O + 163 + 4 * i) for i in range(3)]
        whl = [at(f"whl{i}", [128, 2, 8, 128], F32R, O + (105, 113, 175)[i]) for i in range(3)]
        ar = [at(f"ar{i}", [128, 640], F32, 1 + 2.5 * i) for i in range(4)]
        asum = at("asum", [128, 640], F32, 11)
        ib = at("ib", [128, 640], F32, 13.5)
        tmp = [at(f"tmp{i}", [128, 384], F32, 16 + 1.5 * i) for i in range(3)]
        s_ar = [dsem(f"s_ar{i}") for i in range(4)]
        s_wq = [dsem(f"s_wq{i}") for i in range(3)]
        s_br = dsem("s_br")
        dma(SP, s_br, brel[:, :], bias.rearrange("(k p) -> p k", p=128), scattered=True)
        t_br = dma(SP, s_br, bg[:, :], bgate.rearrange("(k p) -> p k", p=128), scattered=True)
        ar_used = [[] for _ in range(4)]
        a_free = [[], []]
        t_pad = [dv(lambda e, a=a: e.memset(a16[a][:, 9, :], 0.0), chain=False) for a in range(2)][-1]
        halves = [(h, rel) for rel in range(NREL) for h in range(2)]

        def load_counts(n, k):
            (h, rel), q, rk = halves[n], (NT * n + k) % 4, ROWS[k]
            w = HW[h]
            t0 = dma(SP, s_ar[q], ar[q][0:rk, 0:w], TR[rel * N + 128 * k:rel * N + 128 * k + rk, 640 * h:640 * h + w],
                     t_tr, *ar_used[q])
            t = ac(lambda e: e.activation(a16[n % 2][0:rk, k, 0:w], ar[q][0:rk, 0:w], ACT.Copy), t0, t_pad, *a_free[n % 2])
            ar_used[q] = [t]
            return t

        wlist = [wrel[rel, o] for h, rel in halves for o in range(8)]
        wlist += [w[o] for _ in range(2) for w in (root, wgate[1], wgate[0]) for o in range(8)]
        t_raw, t_hi, t_w = {}, {}, {}
        raw_used = [[], [], []]
        whl_used = [[], [], []]

        def w_load(n):
            if n < len(wlist):
                t_raw[n] = dma(SP, s_wq[n % 3], wraw[n % 3][:, :, :], wlist[n], *raw_used[n % 3])

        def w_hi(n):
            if n < len(wlist):
                t_hi[n] = ac(lambda e: e.activation(whl[n % 3][:, 0, :, :], wraw[n % 3][:, :, :], ACT.Copy),
                             t_raw[n], *whl_used[n % 3])

        def w_lo(n):
            if n < len(wlist):
                t_w[n] = dv(lambda e: e.tensor_tensor(whl[n % 3][:, 1, :, :], wraw[n % 3][:, :, :],
                                                      whl[n % 3][:, 0, :, :].bitcast(F32), ALU.subtract),
                            t_hi[n], chain=False)
                raw_used[n % 3] = [t_w[n]]

        for n in range(3):
            w_load(n)

        ones = at("ones", [128, 128], F32, 0.5)
        dv(lambda e: e.memset(ones[:, :], 1.0))
        dv(lambda e: e.memset(mvb[:, :, :], 1.0))
        for i in range(NT):
            r = ROWS[i]
            for j in range(2):
                b, ps = bank()
                c = slice(512 * j, 512 * j + 512)
                tok = mm(b, ps[0:r, :], [(gT[:, k, 128 * i:128 * i + r], wu[:, k, c]) for k in range(2)], t_gT, t_wu)
                free[b] = [dv(lambda e, r=r, i=i, c=c, ps=ps: e.tensor_tensor(z3[i][0:r, c], ps[0:r, :], z3[i][0:r, c], ALU.add),
                              tok, t_2l, chain=False)]
                stats(i, j, z3[i][0:r, c], free[b])
            aggregate(i)
            t_cnt = load_counts(0, i)
            if i in (4, 9):
                t_rs = rstd(i - 4, i + 1)
                for q in range(i - 4, i + 1):
                    r = ROWS[q]
                    t1 = ac(lambda e, r=r, q=q: e.activation(z3[q][0:r, :], z3[q][0:r, :], ACT.Identity,
                                                             scale=rsd[0:r, q:q + 1], bias=nmr[0:r, q:q + 1]), t_rs)
                    t1 = ac(lambda e, r=r, q=q: e.mul(xh[0:r, q, :], z3[q][0:r, :], XS), t1)
                    t_x3 = dv(lambda e, r=r, q=q: e.scalar_tensor_tensor(
                        out=xo[0:r, q, :], in0=z3[q][0:r, :], scalar=XS, in1=xh[0:r, q, :], op0=ALU.mult,
                        op1=ALU.subtract), t1, chain=False)

        t_m = [[], []]

        def split_m(f, c, o0, cn, src_ap, *deps):
            t = ac(lambda e: e.activation(mh[:, f, o0:o0 + cn], src_ap, ACT.Copy), *deps)
            t = dv(lambda e: e.tensor_tensor(ml[:, f, o0:o0 + cn], src_ap, mh[:, f, o0:o0 + cn].bitcast(F32),
                                             ALU.subtract), t, chain=False)
            t_m[c] = [t]
            return t

        step = [0]

        def weigh(h, evac, *deps):
            for o in range(8):
                n = step[0]
                step[0] += 1
                w_hi(n + 2)
                w_load(n + 3) if n + 3 not in t_raw else None
                hi, lo = whl[n % 3][:, 0], whl[n % 3][:, 1]
                for c, (o0, cn) in enumerate(HC[h]):
                    b, ps = bank()
                    tok = mm(b, ps[:, 0:cn], [p for k in range(8) for p in (
                        (hi[:, k, :], mh[:, k, o0:o0 + cn]), (hi[:, k, :], ml[:, k, o0:o0 + cn]),
                        (lo[:, k, :], mh[:, k, o0:o0 + cn]))], t_w[n], *t_m[c])
                    evac(o, c, 640 * h + o0, o0, cn, b, ps, tok)
                whl_used[n % 3] = [tok]
                w_lo(n + 2)
                yield o

        tmp_n = [0]
        t_acc = {}
        for n in range(2):
            w_hi(n)
            w_lo(n)

        def add_scaled(rel):
            def evac(o, c, c0, o0, cn, b, ps, tok):
                q = tmp_n[0] % 3
                tmp_n[0] += 1
                t = dv(lambda e: e.tensor_tensor(tmp[q][:, 0:cn], ps[:, 0:cn], ib[:, o0:o0 + cn], ALU.mult), tok, chain=False)
                free[b] = [t]
                if rel == 0:
                    dv(lambda e: e.tensor_scalar(out=acc[:, o, c0:c0 + cn], in0=tmp[q][:, 0:cn], scalar1=brel[:, o:o + 1],
                                                 scalar2=None, op0=ALU.add), t, t_br, t_x3)
                else:
                    dv(lambda e: e.tensor_tensor(acc[:, o, c0:c0 + cn], tmp[q][:, 0:cn], acc[:, o, c0:c0 + cn], ALU.add), t)
            return evac

        def total_counts(n, t):
            return dv(lambda e: e.tensor_reduce(out=asum[:, 0:HW[halves[n][0]]],
                                                in_=a16[n % 2][:, :, 0:HW[halves[n][0]]].rearrange("p k d -> p d k"),
                                                axis=AX.X, op=ALU.add), t)

        t_as = total_counts(0, t_cnt)
        for n, (h, rel) in enumerate(halves):
            av = a16[n % 2]
            for f in range(8):
                for c, (o0, cn) in enumerate(HC[h]):
                    b, ps = bank()
                    tok = mm(b, ps[:, 0:cn], [(x[0:ROWS[k], k, 128 * f:128 * f + 128], av[0:ROWS[k], k, o0:o0 + cn])
                                              for k in range(NT) for x in (xh, xo)], t_cnt, t_x3)
                    free[b] = [split_m(f, c, o0, cn, ps[:, 0:cn], tok)]
                if f == 0:
                    for o0, cn in HC[h]:
                        b, ps = bank()
                        tok = mm(b, ps[:, 0:cn], [(ones[:, :], asum[:, o0:o0 + cn])], t_as)
                        dv(lambda e, o0=o0, cn=cn, ps=ps: e.tensor_scalar(
                            out=ib[:, o0:o0 + cn], in0=ps[:, 0:cn], scalar1=1.0, scalar2=XS, op0=ALU.max, op1=ALU.mult), tok)
                        free[b] = [dv(lambda e, o0=o0, cn=cn: e.reciprocal(ib[:, o0:o0 + cn], ib[:, o0:o0 + cn]))]
            a_free[n % 2] = [(P, P.n)]
            for o in weigh(h, add_scaled(rel)):
                if n + 1 < len(halves):
                    if o < 5:
                        load_counts(n + 1, 2 * o)
                        t_cnt = load_counts(n + 1, 2 * o + 1)
                    if o == 6:
                        t_as = total_counts(n + 1, t_cnt)

        zx = at("zx", [128, 8, 640], F32, O + 80)
        zz = [at(f"zz{i}", [128, 384], F32, 1 + 1.5 * i) for i in range(3)]
        on = [at(f"on{i}", [128, D], F32, O + 80 + 4 * i) for i in range(5)]
        s_out = dsem("s_out")
        t_out = ()

        def x_turned(o, tiles, ps):
            for m, i in enumerate(tiles):
                r = ROWS[i]
                for q, x in enumerate((xh, xo)):
                    PE.items.append(lambda e, m=m, i=i, r=r, q=q, x=x: e.matmul(
                        ps[:, 128 * m:128 * m + r], x[0:r, i, 128 * o:128 * o + 128], ident16[0:r, 0:r],
                        start=(q == 0), stop=(q == 1))) if (m, q) != (len(tiles) - 1, 1) else None
            return PE.put(lambda e: e.matmul(ps[:, 128 * m:128 * m + r], x[0:r, i, 128 * o:128 * o + 128],
                                             ident16[0:r, 0:r], start=False, stop=True), (), P, 1)

        for h in range(2):
            tiles = [[5 * h, 5 * h + 1, 5 * h + 2], [5 * h + 3, 5 * h + 4]]
            for f in range(8):
                for c, (o0, cn) in enumerate(HC[h]):
                    b, ps = bank()
                    for t in free[b]:
                        PE.wait(t)
                    tok = x_turned(f, tiles[c], ps)
                    free[b] = [split_m(f, c, o0, cn, ps[:, 0:cn], tok)]

            def add_root(o, c, c0, o0, cn, b, ps, tok):
                free[b] = [dv(lambda e: e.scalar_tensor_tensor(
                    out=acc[:, o, c0:c0 + cn], in0=ps[:, 0:cn], scalar=1.0 / XS, in1=acc[:, o, c0:c0 + cn],
                    op0=ALU.mult, op1=ALU.add), tok)]
                t_acc[o, c] = free[b][0]

            def keep_zx(o, c, c0, o0, cn, b, ps, tok):
                free[b] = [dv(lambda e: e.tensor_scalar(
                    out=zx[:, o, o0:o0 + cn], in0=ps[:, 0:cn], scalar1=1.0 / XS, scalar2=bg[:, o:o + 1],
                    op0=ALU.mult, op1=ALU.add), tok, *t_out, t_br, chain=False)]

            def gate(o, c, c0, o0, cn, b, ps, tok):
                q = tmp_n[0] % 3
                tmp_n[0] += 1
                bx, px = bank()
                for t in free[bx]:
                    PE.wait(t)
                tx = x_turned(o, tiles[c], px)
                t = ac(lambda e: e.activation(tmp[q][:, 0:cn], acc[:, o, c0:c0 + cn], ACT.Tanh), (V, V.n))
                t1 = dv(lambda e: e.tensor_tensor(zz[q][:, 0:cn], ps[:, 0:cn], zx[:, o, o0:o0 + cn], ALU.add), tok, chain=False)
                free[b] = [t1]
                t2 = dv(lambda e: e.scalar_tensor_tensor(
                    out=tmp[q][:, 0:cn], in0=px[:, 0:cn], scalar=-1.0 / XS, in1=tmp[q][:, 0:cn], op0=ALU.mult,
                    op1=ALU.add), t, tx, chain=False)
                t3 = dv(lambda e: e.tensor_tensor(zz[q][:, 0:cn], zz[q][:, 0:cn], tmp[q][:, 0:cn], ALU.mult), t1, t2)
                free[bx] = [dv(lambda e: e.scalar_tensor_tensor(
                    out=acc[:, o, c0:c0 + cn], in0=px[:, 0:cn], scalar=2.0 / XS, in1=zz[q][:, 0:cn], op0=ALU.mult,
                    op1=ALU.add), t3)]

            for o in weigh(h, add_root):
                pass
            for o in weigh(h, keep_zx):
                pass
            for f in range(8):
                for c, (o0, cn) in enumerate(HC[h]):
                    split_m(f, c, o0, cn, acc[:, f, 640 * h + o0:640 * h + o0 + cn], t_acc[f, c], (P, P.n))
            for o in weigh(h, gate):
                pass
            t_r = (V, V.n)
            for m, i in enumerate(range(5 * h, 5 * h + 5)):
                r = ROWS[i]
                for j in range(2):
                    b, ps = bank()
                    for t in (*free[b], t_r):
                        PE.wait(t)
                    for q in range(4):
                        f = (lambda e, q=q, j=j, ps=ps, i=i, r=r: e.transpose(
                            ps[0:r, 128 * q:128 * q + 128], acc[:, 4 * j + q, 128 * i:128 * i + r], ident[:, :]))
                        tok = PE.put(f, (), P if q == 3 else None, 1)
                    t = ac(lambda e, j=j, ps=ps, r=r, m=m: e.activation(
                        on[m][0:r, 512 * j:512 * j + 512], ps[0:r, :], ACT.Copy), tok, t_r)
                    free[b] = [t]
                    stats(i, j, on[m][0:r, 512 * j:512 * j + 512], (t,))
                aggregate(i)
            t_rs = rstd(5 * h, 5 * h + 5)
            for m, i in enumerate(range(5 * h, 5 * h + 5)):
                r = ROWS[i]
                if m % 2:
                    t = ac(lambda e, r=r, i=i, m=m: e.activation(
                        on[m][0:r, :], on[m][0:r, :], ACT.Identity, scale=rsd[0:r, i:i + 1], bias=nmr[0:r, i:i + 1]),
                        t_rs, (A, A.n))
                else:
                    t = dv(lambda e, r=r, i=i, m=m: e.tensor_scalar(
                        out=on[m][0:r, :], in0=on[m][0:r, :], scalar1=mvb[0:r, i, 0:1], scalar2=rsd[0:r, i:i + 1],
                        op0=ALU.subtract, op1=ALU.mult), (A, A.n), chain=False)
                t_out = (dma(SP, s_out, out[128 * i:128 * i + r, :], on[m][0:r, :], t),)
        for s in dmas:
            SP.wait((s, s.n))

        block = ctx.enter_context(nc.Block())

        @block.sync
        def _(e):
            SP.run(e)

        @block.tensor
        def _(e):
            PE.run(e)

        @block.vector
        def _(e):
            DV.run(e)

        @block.scalar
        def _(e):
            AC.run(e)

        @block.gpsimd
        def _(e):
            PL.run(e)


def diag_logits(dv, zg, zh, ed, atb, xlx, xrn, i0, i1, r, dep):
    for i in range(i0, i1):
        dv(lambda e, i=i: e.tensor_tensor(zg[0:r, i, :].rearrange("p (h d) -> p h d", h=4), xlx[0:r, i, :, 0:64],
                                          xrn[0:r, i, :].rearrange("p (h d) -> p h d", h=4), ALU.add), dep)
        dv(lambda e, i=i: e.scalar_tensor_tensor(out=zh[0:r, i, :], in0=zg[0:r, i, :], scalar=0.2, in1=zg[0:r, i, :],
                                                 op0=ALU.mult, op1=ALU.max))
        dv(lambda e, i=i: e.tensor_tensor(zg[0:r, i, :], zh[0:r, i, :], atb[0:r, :], ALU.mult))
        t = dv(lambda e, i=i: e.tensor_reduce(out=ed[0:r, i, :], in_=zg[0:r, i, :].rearrange("p (h d) -> p h d", h=4),
                                              axis=AX.X, op=ALU.add))
    return t


_INS = ["x", "src", "dst", "edge_type_8", "L0_gnn_W", "L0_gnn_b", "L1_gnn_W_self0", "L1_gnn_W_neigh0", "L1_gnn_b0",
        "L1_gnn_W_self1", "L1_gnn_W_neigh1", "L1_gnn_b1", "L2_gnn_rms_w", "L2_gnn_W_down", "L2_gnn_Wl", "L2_gnn_Wr",
        "L2_gnn_att", "L2_gnn_W_up", "L3_gnn_weight", "L3_gnn_root", "L3_gnn_bias", "L3_gnn_w_gate", "L3_gnn_b_gate"]


_TILED = ("L3_gnn_weight", "L3_gnn_root", "L3_gnn_w_gate")


def kernel(**inputs):
    import numpy as np
    import concourse.bacc as bacc
    from concourse.bass_utils import run_bass_kernel_spmd

    nc = bacc.Bacc("TRN2", target_bir_lowering=False, num_devices=1)
    arrays, args = {}, []
    for name in _INS:
        a = np.asarray(inputs[name])
        if name in _TILED:
            a = a.reshape(-1, 8, 128, 8, 128).transpose(0, 3, 2, 1, 4)
            a = a[0] if len(a) == 1 else a
        a = np.ascontiguousarray(a)
        arrays[f"in_{name}"] = a
        args.append(nc.dram_tensor(f"in_{name}", a.shape, mybir.dt.from_np(a.dtype), kind="ExternalInput").ap())
    args.append(nc.dram_tensor("out_0", (N, D), F32, kind="ExternalOutput").ap())
    program(nc, *args)
    r = run_bass_kernel_spmd(nc, [arrays], core_ids=[0])
    return r.results[0]["out_0"]
```

```python
from contextlib import ExitStack

import concourse.bass as bass
from concourse import mybir

F32 = mybir.dt.float32
F32R = mybir.dt.float32r
F16 = mybir.dt.float16
I32 = mybir.dt.int32
ALU = mybir.AluOpType
ACT = mybir.ActivationFunctionType
AX = mybir.AxisListType

N = 1250
D = 1024
NT = 10
EP = 125
ET = 170
NREL = 8
ROWS = [128] * 9 + [98]
HW = [640, 610]
HC = [[(0, 384), (384, 256)], [(0, 384), (384, 226)]]
CH = [(0, 418), (418, 416), (834, 416)]
TPAD = 1280
RPAD = 10240
LN_EPS = 1e-5
RMS_EPS = 1e-6
NEG = -3.0e38
XS = 1024.0
KB = 1024
BASE = 16512


class Sem:

    def __init__(self, h):
        self.h = h
        self.n = 0


class Queue:

    def __init__(self):
        self.items = []
        self.seen = {}

    def wait(self, tok):
        sem, v = tok
        if v > self.seen.get(sem, 0):
            self.seen[sem] = v
            self.items.append(lambda e: e.wait_ge(sem.h, v))

    def put(self, fn, deps, sem, k):
        last = {}
        for s, v in deps:
            last[s] = max(v, last.get(s, 0))
        for t in last.items():
            self.wait(t)
        if sem is None:
            self.items.append(fn)
            return None
        sem.n += k
        self.items.append(lambda e: fn(e).then_inc(sem.h, k))
        return (sem, sem.n)

    def run(self, e):
        for f in self.items:
            f(e)


def program(nc, x, xt, src, dst, ety, w0, b0, ws0, wn0, bb0, ws1, wn1, bb1, rmsw, wdown, wl, wr, att, wup, wupt,
            wrel, root, bias, wgate, bgate, out):
    ctx = ExitStack()
    with ctx:
        def sem(name):
            return Sem(ctx.enter_context(nc.semaphore(name)))

        def at(name, shape, dt, kb):
            return nc.alloc_sbuf_tensor_at(name, shape, dt, offset=BASE + int(kb * KB))

        def dram(name, shape, dt=F32):
            return nc.dram_tensor(name, shape, dt, kind="Internal").ap()

        T0 = [dram(f"T0_{i}", (TPAD, N)) for i in range(3)]
        TR = dram("TR", (RPAD, N))
        EM = dram("EM", (TPAD, N * 4))
        X1 = dram("X1", (N, D))
        X2 = dram("X2", (N, D))
        HD = dram("HD", (N, D))
        ZD = dram("ZD", (N, D))
        BD = dram("BD", (N, N))
        XW = dram("XW", (2, 8, 128, N))
        WW = dram("WW", (2, 8, 128, 2, 2, 128))
        GD = dram("GD", (128, 2, N))
        XL = dram("XL", (N, 256))
        XR = dram("XR", (N, 256))

        PE, DV, AC, PL, SP = Queue(), Queue(), Queue(), Queue(), Queue()
        P, V, A, G = sem("P"), sem("V"), sem("A"), sem("G")
        dmas = []

        def dsem(name):
            s = sem(name)
            dmas.append(s)
            return s

        def pe(fn, *deps):
            return PE.put(fn, deps, P, 1)

        def dv(fn, *deps, chain=True):
            if chain:
                DV.wait((V, V.n))
            return DV.put(fn, deps, V, 1)

        def ac(fn, *deps):
            return AC.put(fn, deps, A, 1)

        def pl(fn, *deps):
            return PL.put(fn, deps, G, 1)

        def dma(q, s, o, i, *deps, scattered=False):
            return q.put(lambda e: e.dma_start(o, i, allow_slow_non_contiguous=scattered), deps, s, 16)

        def barrier(also=()):
            for q in (PE, DV, AC, SP):
                for s in (P, V, A, *bar_dmas, *also):
                    q.wait((s, s.n))

        banks = [ctx.enter_context(nc.psum_tensor(f"ps{i}", [128, 512], F32)) for i in range(8)]
        free = [[] for _ in range(8)]
        turn = [0]

        def bank(n=8):
            b = turn[0] % n
            turn[0] += 1
            return b, banks[b]

        def mm(b, ap, pairs, *deps):
            for t in (*free[b], *deps):
                PE.wait(t)
            n = len(pairs)
            for q, (l, r, *t) in enumerate(pairs):
                for tok in t:
                    PE.wait(tok)
                f = (lambda e, l=l, r=r, q=q: e.matmul(ap, l, r, start=(q == 0), stop=(q == n - 1)))
                tok = PE.put(f, (), P if q == n - 1 else None, 1)
            return tok

        ident = at("ident", [128, 128], F32, 0)
        lmask = at("lmask", [128, 128], F32, 0.5)
        zero = at("zero", [128, 250], F32, 1)
        neg = at("neg", [128, 250], F32, 2)
        bc = at("bc", [128, D], F32, 3)
        ei = at("ei", [EP, 3, ET], I32, 7)
        cnt = at("cnt", [EP, 2, ET], F32, 9)
        adr = at("adr", [EP, 2, ET], I32, 10.375)
        ef = at("ef", [EP, 3, ET], F32, 11.75)
        key = at("key", [EP, 2, ET], F32, 13.75)
        dup = at("dup", [EP, 2, ET], F32, 15.125)
        tt = [at(f"tt{i}", [128, 256], F32, 11.75 + i) for i in range(5)]
        trash_i = at("trash_i", [128, 2], I32, 17.5)
        trash = at("trash", [128, 2], F32, 17.53125)
        onesr = at("onesr", [128, 2], F32R, 17.5625)
        onesf = at("onesf", [128, 2], F32, 17.59375)
        rw = at("rw", [128, 8], F32, 17.625)
        brel = at("brel", [128, 8], F32, 17.65625)
        bg = at("bg", [128, 8], F32, 17.6875)
        ident16 = at("ident16", [128, 128], F16, 17.71875)
        deg = at("deg", [128, 10], F32, 17.96875)
        dis = at("dis", [128, 10], F32, 18.03125)
        dinv = at("dinv", [128, 10], F32, 18.09375)
        rms = at("rms", [128, 10], F32, 18.15625)
        t10 = at("t10", [128, 10], F32, 18.21875)
        mvb = at("mvb", [128, NT, 2], F32, 18.28125)
        rsd = at("rsd", [128, NT], F32, 18.375)
        vpe = at("vpe", [128, NT], F32, 18.4375)
        nmr = at("nmr", [128, NT], F32, 18.5)
        stb = at("stb", [128, NT, 4, 6], F32, 18.5625)
        O = 19.5
        eqj = at("eqj", [EP, 8, 125], F16, O + 186.25)
        g_zero = pl(lambda e: e.memset(zero[:, :], 0.0))
        g_neg = pl(lambda e: e.memset(neg[:, :], NEG))
        g0 = pl(lambda e: e.memset(ident[:, :], 0.0))
        g1 = pl(lambda e: e.memset(lmask[:, :], 1.0))
        pl(lambda e: e.affine_select(out=ident[:, :], in_=ident[:, :], compare_op=ALU.not_equal, fill=1.0, base=0,
                                     pattern=[[-1, 128]], channel_multiplier=1), g0)
        pl(lambda e: e.affine_select(out=lmask[:, :], in_=lmask[:, :], compare_op=ALU.is_gt, fill=0.0, base=0,
                                     pattern=[[-1, 128]], channel_multiplier=1), g1)
        pl(lambda e: e.iota(trash_i[:, 0:1], pattern=[[0, 1]], base=N * N, channel_multiplier=1))
        pl(lambda e: e.iota(trash_i[:, 1:2], pattern=[[0, 1]], base=NREL * N * N, channel_multiplier=1))
        g_const = pl(lambda e: e.memset(onesf[:, :], 1.0))

        def fill(s, table, value, r0, r1, *deps):
            n = (r1 - r0) // 128 * (table.shape[1] // 250)
            return dma(SP, s, table[r0:r1, :].rearrange("(p a) (b f) -> p (a b) f", p=128, f=250),
                       value[:, None, :].broadcast_to([128, n, 250]), *deps)

        s_e = dsem("s_e")
        for n, a in enumerate((src, dst, ety)):
            t_e = dma(SP, s_e, ei[:, n, :], a.rearrange("(p t) -> p t", t=ET))
        s_z0 = [dsem(f"s_z0{i}") for i in range(3)]
        s_z2 = [dsem(f"s_z2{i}") for i in range(2)]
        s_w0 = [dsem(f"s_w0{i}") for i in range(2)]
        paced = []

        def pace():
            return paced[-2:-1] or [g_zero]

        wt = at("wt", [128, 8, D], F32, O + 40)
        xin = at("xin", [128, 8, N], F32, O + 72)
        t_z0 = [[fill(s_z0[0], T0[0], zero, 0, TPAD, g_zero)]]
        for i in (1, 2):
            for c in range(10):
                paced.append(fill((s_z0[i], s_z2[i - 1])[c % 2], T0[i], zero, 128 * c, 128 * c + 128, *pace()))
            t_z0.append(paced[-2:])
        for k in range(8):
            paced.append(dma(SP, s_w0[0], xin[:, k, :], xt[:, k, :], *pace()))
            paced.append(dma(SP, s_w0[1], wt[:, k, :], w0[:, k, :], *pace()))
        t_w0 = paced[-2:]
        s_bc = dsem("s_bc")
        t_b = dma(SP, s_bc, bc[:, :], b0.rearrange("(a n) -> a n", a=1).broadcast_to([128, D]))
        s_z1 = dsem("s_z1")

        t_ef = dv(lambda e: e.tensor_copy(ef[:, :, :], ei[:, :, :]), t_e)
        dv(lambda e: e.tensor_copy(trash[:, :], trash_i[:, :]), g_const, chain=False)
        dv(lambda e: e.tensor_copy(ident16[:, :], ident[:, :]), chain=False)
        dv(lambda e: e.tensor_copy(onesr[:, :], onesf[:, :]), chain=False)
        dv(lambda e: e.scalar_tensor_tensor(out=key[:, 0, :], in0=ef[:, 1, :], scalar=float(N), in1=ef[:, 0, :],
                                            op0=ALU.mult, op1=ALU.add))
        dv(lambda e: e.scalar_tensor_tensor(out=key[:, 1, :], in0=ef[:, 2, :], scalar=float(N), in1=ef[:, 0, :],
                                            op0=ALU.mult, op1=ALU.add))
        t_key = dv(lambda e: e.scalar_tensor_tensor(out=key[:, 1, :], in0=key[:, 1, :], scalar=float(N),
                                                    in1=ef[:, 1, :], op0=ALU.mult, op1=ALU.add))
        t_adr = {}
        eq_used = [() for _ in range(8)]
        eq_turn = [0]

        def dedupe(w, t0, n):
            for g in range(t0, t0 + n, 4):
                ts = list(range(g, min(g + 4, t0 + n)))
                b, ps = bank(5)
                for t in free[b]:
                    PE.wait(t)
                for m, t in enumerate(ts):
                    tok = mm(b, ps[0:EP, 125 * m:125 * m + 125],
                             [(key[:, w, t:t + 1].broadcast_to([EP, EP]), ident[0:EP, 0:EP])], t_key, g_const)
                for m, t in enumerate(ts):
                    pv = ps[0:EP, 125 * m:125 * m + 125]
                    j = eq_turn[0] % 8
                    eq_turn[0] += 2
                    eq_used[j] = (dv(lambda e, pv=pv, t=t, j=j: e.tensor_scalar(
                        out=eqj[:, j, :], in0=pv, scalar1=key[:, w, t:t + 1], scalar2=0.0, op0=ALU.is_equal,
                        op1=ALU.add, accum_out=cnt[:, w, t:t + 1]), tok, *eq_used[j], chain=False),)
                    last = dv(lambda e, pv=pv, t=t, j=j: e.scalar_tensor_tensor(
                        out=eqj[:, j + 1, :], in0=pv, scalar=key[:, w, t:t + 1], in1=lmask[0:EP, 0:125],
                        op0=ALU.is_equal, op1=ALU.mult, accum_out=dup[:, w, t:t + 1]), *eq_used[j + 1], chain=False)
                    eq_used[j + 1] = (last,)
                free[b] = [last]
                yield
            s = slice(t0, t0 + n)
            dv(lambda e: e.tensor_scalar(out=dup[:, w, s], in0=dup[:, w, s], scalar1=1.0, scalar2=None, op0=ALU.min))
            dv(lambda e: e.tensor_scalar(out=ef[:, w, s], in0=key[:, w, s], scalar1=trash[0:EP, w:w + 1],
                                         scalar2=-1.0, op0=ALU.subtract, op1=ALU.mult))
            dv(lambda e: e.tensor_tensor(ef[:, w, s], ef[:, w, s], dup[:, w, s], ALU.mult))
            tok = dv(lambda e: e.tensor_tensor(adr[:, w, s], ef[:, w, s], key[:, w, s], ALU.add))
            for t in range(t0, t0 + n):
                t_adr[w, t] = tok

        for q in range(10):
            for _ in dedupe(0, 17 * q, 17):
                pass

        def scatter(s, table, w, t, bound, *deps):
            flat = table.rearrange("a b -> (a b)").rearrange("(c d) -> c d", d=1)
            return PL.put(lambda e: e.indirect_dma_start(
                out=flat, out_offset=bass.IndirectOffsetOnAxis(ap=adr[:, w, t:t + 1], axis=0),
                in_=cnt[:, w, t:t + 1], in_offset=None, bounds_check=bound, oob_is_err=True, compute_op=ALU.add),
                deps, s, 16)

        s_t0 = [dsem(f"s_t0{i}") for i in range(3)]
        order = ([0] * 9 + [0, 1] * 9 + [1, 2, 0] * ET)[:ET]
        for t, n in enumerate(order):
            s = s_t0[n]
            scatter(s, T0[n], 0, t, TPAD * N - 1, *t_z0[n], (s, s.n), t_adr[0, t])
        t_t0 = [(s, s.n) for s in s_t0]

        bar_dmas = []
        yraw = at("yraw", [128, NT, D], F32, O)
        t_ones = dv(lambda e: e.memset(mvb[:, :, :], 1.0), chain=False)
        more = (None for q in range(5) for _ in dedupe(1, 34 * q, 34))
        def project(n):
            i, j = n // 2, n % 2
            r, c = ROWS[i], slice(512 * j, 512 * j + 512)
            b, ps = bank(5)
            tok = mm(b, ps[0:r, :], [(xin[:, k, 128 * i:128 * i + r], wt[:, k, c]) for k in range(8)], *t_w0)
            free[b] = [dv(lambda e: e.tensor_tensor(yraw[0:r, i, c], ps[0:r, :], bc[0:r, c], ALU.add), tok, t_b, chain=False)]

        for n in range(16):
            project(n)
            for _ in range(3):
                next(more, None)
        for _ in more:
            pass

        bp = at("bp", [128, NT, N], F32R, O + 137)
        slab = [at(f"slab{i}", [128, N], F32, O + 111.5 + 5 * i) for i in range(5)]
        s_sl = [dsem(f"s_sl{i}") for i in range(5)]
        used = [[] for _ in range(5)]
        onesb = at("onesb", [128, 128], F32R, 18.5625)
        t_onesb = dv(lambda e: e.tensor_copy(onesb[:, :], onesf[:, 0:1].broadcast_to([128, 128])), chain=False)
        t_ones = dv(lambda e: e.memset(deg[:, :], 1.0))
        for k in range(NT):
            r = ROWS[k]
            sl = [(3 * k + n) % 5 for n in range(3)]
            toks = [dma(SP, s_sl[a], slab[a][0:r, :], T0[n][128 * k:128 * k + r, :], t_t0[n], *used[a])
                    for n, a in enumerate(sl)]
            t0 = dv(lambda e, sl=sl, r=r: e.tensor_tensor(slab[sl[0]][0:r, :], slab[sl[0]][0:r, :], slab[sl[1]][0:r, :],
                                                          ALU.add), *toks[0:2], chain=False)
            t1 = dv(lambda e, sl=sl, r=r, k=k: e.scalar_tensor_tensor(
                out=bp[0:r, k, :], in0=slab[sl[0]][0:r, :], scalar=1.0, in1=slab[sl[2]][0:r, :], op0=ALU.mult,
                op1=ALU.add, accum_out=dinv[0:r, k:k + 1]), t0, toks[2], t_ones, chain=False)
            used[sl[1]] = [t0]
            used[sl[0]] = used[sl[2]] = [t1]
            t_bp = dv(lambda e, r=r, k=k: e.tensor_tensor(
                bp[0:r, k, 128 * k:128 * k + r], bp[0:r, k, 128 * k:128 * k + r].bitcast(F32), ident[0:r, 0:r], ALU.add))
            if k == 0:
                for n in range(16, 20):
                    project(n)
            for t in (t_bp, t_onesb, *(free[5] + free[6] + free[7])):
                PE.wait(t)
            for c, (c0, cn) in enumerate(CH):
                f = (lambda e, k=k, r=r, c=c, c0=c0, cn=cn: e.matmul(
                    banks[5 + c][:, 0:cn], onesb[0:r, :], bp[0:r, k, c0:c0 + cn], start=(k == 0), stop=(k == NT - 1)))
                t_d = PE.put(f, (), P if c == 2 else None, 1)
        s_bd = dsem("s_bd")
        for k in range(NT):
            t_bd = dma(SP, s_bd, BD[128 * k:128 * k + ROWS[k], :], bp[0:ROWS[k], k, :].bitcast(F32), t_bp)
        dgj = at("dgj", [128, 2, 128], F32, O + 120)
        dgp = at("dgp", [128, 2, NT], F32, O + 121)
        dv(lambda e: e.memset(dgp[:, :, :], 0.0), t_bp)
        for i in range(NT):
            m = 0
            for c, (c0, cn) in enumerate(CH):
                lo, hi = max(128 * i, c0), min(128 * i + ROWS[i], c0 + cn)
                if lo < hi:
                    t = dv(lambda e, i=i, m=m, c=c, lo=lo, hi=hi, c0=c0: e.scalar_tensor_tensor(
                        out=dgj[:, m, 0:hi - lo], in0=banks[5 + c][:, lo - c0:hi - c0], scalar=1.0,
                        in1=ident[:, lo - 128 * i:hi - 128 * i], op0=ALU.mult, op1=ALU.mult, accum_out=dgp[:, m, i:i + 1]), t_d)
                    m += 1
        free[5] = free[6] = free[7] = [t]
        dv(lambda e: e.tensor_tensor(dgp[:, 0, :], dgp[:, 0, :], dgp[:, 1, :], ALU.add))
        dv(lambda e: e.tensor_copy(deg[:, 0:9], dgp[:, 0, 0:9]))
        dv(lambda e: e.tensor_copy(deg[0:98, 9:10], dgp[0:98, 0, 9:10]))

        def rsqrt(y, v, t, deps=()):
            s = ac(lambda e: e.activation(y, v, ACT.Sqrt), (V, V.n), *deps)
            dv(lambda e: e.reciprocal(y, y), s)
            dv(lambda e: e.tensor_tensor(t, v, y, ALU.mult))
            dv(lambda e: e.tensor_tensor(t, t, y, ALU.mult))
            dv(lambda e: e.tensor_scalar(out=t, in0=t, scalar1=-0.5, scalar2=1.5, op0=ALU.mult, op1=ALU.add))
            return dv(lambda e: e.tensor_tensor(y, y, t, ALU.mult))

        def stats(i, j, v, deps):
            return dv(lambda e: e.bn_stats(stb[0:ROWS[i], i, j, :], v), *deps, chain=False)

        def aggregate(i, n):
            r = ROWS[i]
            return dv(lambda e: e.bn_aggr(mvb[0:r, i, :], stb[0:r, i, 0:n, :].rearrange("p a b -> p (a b)")))

        def rstd(i0, i1):
            dv(lambda e: e.tensor_scalar(out=vpe[:, i0:i1], in0=mvb[:, i0:i1, 1], scalar1=LN_EPS, scalar2=None, op0=ALU.add))
            rsqrt(rsd[:, i0:i1], vpe[:, i0:i1], nmr[:, i0:i1])
            return dv(lambda e: e.scalar_tensor_tensor(out=nmr[:, i0:i1], in0=mvb[:, i0:i1, 0], scalar=-1.0,
                                                       in1=rsd[:, i0:i1], op0=ALU.mult, op1=ALU.mult))

        t_dis = rsqrt(dis[:, :], deg[:, :], t10[:, :])

        yhi = at("yhi", [128, NT, D], F32R, O + 40)
        ylo = at("ylo", [128, NT, D], F32R, O + 80)
        t_y = {}
        for j in range(2):
            c = slice(512 * j, 512 * j + 512)
            for i in range(NT):
                r = ROWS[i]
                t1 = ac(lambda e, i=i, r=r, c=c: e.mul(yhi[0:r, i, c], yraw[0:r, i, c], dis[0:r, i:i + 1]), t_dis)
                t_y[i, j] = dv(lambda e, i=i, r=r, c=c: e.scalar_tensor_tensor(
                    out=ylo[0:r, i, c], in0=yraw[0:r, i, c], scalar=dis[0:r, i:i + 1], in1=yhi[0:r, i, c].bitcast(F32),
                    op0=ALU.mult, op1=ALU.subtract), t1, chain=False)
        dv(lambda e: e.tensor_scalar(out=dinv[:, 0:9], in0=dinv[:, 0:9], scalar1=1.0, scalar2=None, op0=ALU.max))
        dv(lambda e: e.tensor_scalar(out=dinv[0:98, 9:10], in0=dinv[0:98, 9:10], scalar1=1.0, scalar2=None, op0=ALU.max))
        dv(lambda e: e.reciprocal(dinv[:, 0:9], dinv[:, 0:9]))
        dv(lambda e: e.reciprocal(dinv[0:98, 9:10], dinv[0:98, 9:10]))

        xT = at("xT", [128, 8, N], F32, O)
        xtl = at("xtl", [128, 8, N], F32R, O)
        xth = at("xth", [128, 8, N], F32R, O + 39.25)
        am = at("am", [128, NT, N], F32R, O + 78.5)
        zt = [at(f"zt{i}", [128, D], F32, kb) for i, kb in enumerate((3, 11.75, O + 128, O + 132))]
        NX = 4
        s_xr = [dsem(f"s_xr{i}") for i in range(NX)]
        s_xo = [dsem(f"s_xo{i}") for i in range(NX)]

        def transpose_rows(i, tile, deps, split):
            r = ROWS[i]
            for h in range(2):
                b, ps = bank()
                for t in (*free[b], *deps):
                    PE.wait(t)
                for m in range(4):
                    k = 4 * h + m
                    f = (lambda e, k=k, m=m, ps=ps: e.transpose(
                        ps[:, 128 * m:128 * m + r], tile[0:r, 128 * k:128 * k + 128], ident[0:r, 0:r]))
                    tok = PE.put(f, (), P if m == 3 else None, 1)
                pv = ps[:, :].rearrange("p (m c) -> p m c", m=4)[:, :, 0:r]
                s = (slice(None), slice(4 * h, 4 * h + 4), slice(128 * i, 128 * i + r))
                if split:
                    t = ac(lambda e, pv=pv, s=s: e.activation(xth[s], pv, ACT.Copy), tok)
                    free[b] = [dv(lambda e, pv=pv, s=s: e.tensor_tensor(xtl[s], pv, xth[s].bitcast(F32), ALU.subtract),
                                  t, chain=False)]
                else:
                    free[b] = [ac(lambda e, pv=pv, s=s: e.activation(xT[s], pv, ACT.Copy), tok)]
            return tok

        def turn_counts(d):
            r = ROWS[d]
            for g in range(3):
                b, ps = bank()
                ks = list(range(4 * g, min(4 * g + 4, NT)))
                for t in free[b]:
                    PE.wait(t)
                for m, k in enumerate(ks):
                    f = (lambda e, m=m, k=k, ps=ps: e.transpose(
                        ps[0:ROWS[k], 128 * m:128 * m + r], bp[0:r, d, 128 * k:128 * k + ROWS[k]].bitcast(F32),
                        ident[0:r, 0:r]))
                    tok = PE.put(f, (), P if k == ks[-1] else None, 1)
                for k0, n, rk in ((4 * g, 4, 128),) if g < 2 else ((8, 1, 128), (9, 1, 98)):
                    pv = ps[0:rk, :].rearrange("p (m c) -> p m c", m=4)[:, k0 - 4 * g:k0 - 4 * g + n, 0:r]
                    o = am[0:rk, k0:k0 + n, 128 * d:128 * d + r]
                    if g == 1:
                        t = dv(lambda e, pv=pv, o=o: e.tensor_copy(o, pv), tok, chain=False)
                    else:
                        t = ac(lambda e, pv=pv, o=o: e.activation(o, pv, ACT.Copy), tok)
                    if k0 <= d < k0 + n:
                        blk = am[0:r, d, 128 * d:128 * d + r]
                        dv(lambda e: e.tensor_tensor(blk, blk.bitcast(F32), ident[0:r, 0:r], ALU.subtract), t, chain=False)
                free[b] = [t]
            return tok

        used = [[t_bp] for _ in range(NX)]
        t_n = {}

        def fill_counts(n):
            for c in filled:
                t = fill(s_z1, TR, zero, 640 * c, 640 * c + 640)
                n -= 1
                if n == 0:
                    break
            return t

        filled = iter(range(16))

        def load_x(i):
            r, a = ROWS[i], i % NX
            t_xr[i] = dma(SP, s_xr[a], zt[a][0:r, :], x[128 * i:128 * i + r, :], *used[a])

        t_xr = {}
        for i in range(NX):
            load_x(i)

        def turn_x1(i):
            used[i % NX].append(transpose_rows(i, zt[i % NX], [t_n[i]], i >= 8))

        for i in range(NT):
            r, a = ROWS[i], i % NX
            for j in range(2):
                b, ps = bank()
                c = slice(512 * j, 512 * j + 512)
                tok = mm(b, ps[0:r, :], [(bp[0:ROWS[k], k, 128 * i:128 * i + r], y[0:ROWS[k], k, c], t_y[k, j])
                                         for k in range(NT) for y in (yhi, ylo)])
                free[b] = [dv(lambda e, i=i, r=r, a=a, c=c, ps=ps: e.scalar_tensor_tensor(
                    out=zt[a][0:r, c], in0=ps[0:r, :], scalar=dis[0:r, i:i + 1], in1=zt[a][0:r, c],
                    op0=ALU.mult, op1=ALU.add), tok, t_xr[i], chain=False)]
                stats(i, j, zt[a][0:r, c], free[b])
            aggregate(i, 2)
            t_rs = rstd(i, i + 1)
            t_n[i] = ac(lambda e, i=i, r=r, a=a: e.activation(
                zt[a][0:r, :], zt[a][0:r, :], ACT.Identity, scale=rsd[0:r, i:i + 1], bias=nmr[0:r, i:i + 1]), t_rs)
            used[a] = [dma(AC, s_xo[a], X1[128 * i:128 * i + r, :], zt[a][0:r, :], t_n[i])]
            if i > 0:
                turn_x1(i - 1)
                if i + 3 < NT:
                    load_x(i + 3)
            if i < 7:
                t_z1 = [fill_counts(1)]
        t_bp_read = {}
        turn_x1(9)
        for d in (8, 9, 2, 3, 4, 5, 6, 7, 0, 1):
            t_bp_read[d] = turn_counts(d)
        t_x1 = (P, P.n)

        hhi = at("hhi", [128, NT, 256], F32R, O + 127.5)
        hlo = at("hlo", [128, NT, 256], F32R, O + 137.5)
        wb = [at(f"wb{i}", [128, 2, 8, 256], F32R, O + 147.5 + 16 * i) for i in range(2)]
        wp = [at(f"wp{i}", [128, 8, 128], F32, O + 179.5 + 4 * i) for i in range(2)]
        s_wp = [dsem(f"s_wp{i}") for i in range(2)]
        s_ho = [dsem(f"s_ho{i}") for i in range(5)]
        s_tx = [dsem(f"s_tx{i}") for i in range(5)]
        wp_used = [[t_bp_read[9], t_bd], [t_bp_read[9], t_bd]]
        wb_used = [[t_bp_read[5], t_bd], [t_bp_read[7], t_bd]]
        tt_used = [[] for _ in range(5)]
        wturn, tturn = [0], [0]

        def load_w(w, q, n):
            for m in range(2):
                a = wturn[0] % 2
                wturn[0] += 1
                t0 = dma(SP, s_wp[a], wp[a][:, :, :], w[2 * q + m], *wp_used[a])
                c = slice(128 * m, 128 * m + 128)
                t1 = ac(lambda e, a=a, c=c: e.activation(wb[n][:, 0, :, c], wp[a][:, :, :], ACT.Copy), t0, *wb_used[n])
                t2 = dv(lambda e, a=a, c=c: e.tensor_tensor(wb[n][:, 1, :, c], wp[a][:, :, :],
                                                            wb[n][:, 0, :, c].bitcast(F32), ALU.subtract), t1, chain=False)
                wp_used[a] = [t2]
            return t2

        def three(i, n):
            s = slice(128 * i, 128 * i + ROWS[i])
            return [p for k in range(8) for p in ((xth[:, k, s], wb[n][:, 0, k, :]), (xth[:, k, s], wb[n][:, 1, k, :]),
                                                  (xtl[:, k, s], wb[n][:, 0, k, :]))]

        def sage(ws, wn, t_n, ready, finish):
            t_xi = {0: ready(0)}
            for q in range(4):
                for i in range(NT):
                    r = ROWS[i]
                    if q == 0 and i + 1 < NT:
                        t_xi[i + 1] = ready(i + 1)
                    b, ps = bank()
                    tok = mm(b, ps[0:r, 0:256], three(i, 0), *t_n, *t_xi[i])
                    t1 = ac(lambda e, i=i, r=r, ps=ps: e.activation(hhi[0:r, i, :], ps[0:r, 0:256], ACT.Copy), tok)
                    t_h = dv(lambda e, i=i, r=r, ps=ps: e.tensor_tensor(
                        hlo[0:r, i, :], ps[0:r, 0:256], hhi[0:r, i, :].bitcast(F32), ALU.subtract), t1, chain=False)
                    free[b] = [t_h]
                    if q == 0 and i == 8:
                        t_s = [load_w(ws, 0, 1)]
                wb_used[0] = [tok]
                for i in range(NT):
                    r = ROWS[i]
                    b, ps = bank()
                    mm(b, ps[0:r, 0:256], three(i, 1), *t_s)
                    tok = mm(b, ps[0:r, 256:512], [(am[0:ROWS[k], k, 128 * i:128 * i + r], h[0:ROWS[k], k, :])
                                                   for k in range(NT) for h in (hhi, hlo)], t_h, (A, t_am_a), (V, t_am_v))
                    wb_used[1] = [tok]
                    free[b] = [finish(q, i, r, ps, tok)]
                    if i == 3 and q < 3:
                        t_n = [load_w(wn, q + 1, 0)]
                if q < 3:
                    t_s = [load_w(ws, q + 1, 1)]

        def load_bias(v, *deps):
            return dma(SP, s_bc, bc[:, :], v.rearrange("(a n) -> a n", a=1).broadcast_to([128, D]), *deps)

        t_am_a, t_am_v = A.n, V.n
        first = [load_w(wn0, 0, 0)]
        stores = [(s, s.n) for s in s_xo]
        for q in (DV, AC, SP):
            for t in (*stores, t_bd):
                q.wait(t)
        t_b = load_bias(bb0, t_x1)
        s_em = dsem("s_em")

        def split_x1(i):
            if i >= 8:
                return [(A, t_am_a), (V, t_am_v)]
            s = (slice(None), slice(None), slice(128 * i, 128 * i + 128))
            t = ac(lambda e: e.activation(xth[s], xT[s], ACT.Copy))
            return [dv(lambda e: e.tensor_tensor(xtl[s], xT[s], xth[s].bitcast(F32), ALU.subtract), t, chain=False)]

        t_hd = {}

        def finish_inner(q, i, r, ps, tok):
            a = tturn[0] % 5
            tturn[0] += 1
            cq = slice(256 * q, 256 * q + 256)
            if q == 0 and i < 9:
                t_z1.append(fill_counts(1))
            if q > 0 and i in (1, 4, 7):
                c = 3 * q - 3 + i // 3
                fill(s_em, EM, neg, 128 * c, 128 * c + 128, g_neg)
            t = dv(lambda e: e.tensor_tensor(tt[a][0:r, :], ps[0:r, 0:256], bc[0:r, cq], ALU.add),
                   tok, t_b, *tt_used[a], chain=False)
            last = dv(lambda e: e.scalar_tensor_tensor(
                out=tt[a][0:r, :], in0=ps[0:r, 256:512], scalar=dinv[0:r, i:i + 1], in1=tt[a][0:r, :],
                op0=ALU.mult, op1=ALU.add), t, chain=False)
            t = ac(lambda e: e.activation(tt[a][0:r, :], tt[a][0:r, :], ACT.Relu), last)
            t_st = dma(AC, s_ho[a], HD[128 * i:128 * i + r, cq], tt[a][0:r, :], t)
            t_hd.setdefault(i, []).append(t_st)
            tt_used[a] = [t_st]
            return last

        sage(ws0, wn0, first, split_x1, finish_inner)
        s_tr = dsem("s_tr")
        for t in range(ET):
            scatter(s_tr, TR, 1, t, RPAD * N - 1, t_z1[-1], (s_tr, s_tr.n), t_adr[1, t])
        t_tr = (s_tr, s_tr.n)
        t_em = fill(s_em, EM, neg, 1152, 1280)

        NL = 4
        lt = [at(f"lt{i}", [128, D], F32, O + 163.5 + 4 * i) for i in range(NL)]
        s_lt = [dsem(f"s_lt{i}") for i in range(NL)]
        lt_used = [[(P, P.n)] for _ in range(NL)]
        t_lt = {}

        def load_h(i):
            r, a = ROWS[i], i % NL
            t_lt[i] = dma(SP, s_lt[a], lt[a][0:r, :], HD[128 * i:128 * i + r, :], *lt_used[a], *t_hd[i])

        first = [load_w(wn1, 0, 0)]
        t_b = load_bias(bb1, (V, V.n))
        for i in range(NL):
            load_h(i)

        def turn_h(i):
            lt_used[i % NL] = wb_used[1] = [transpose_rows(i, lt[i % NL], [t_lt[i]], True)]
            if i + NL < NT:
                load_h(i + NL)
            return [(A, A.n), (V, V.n)]

        zl = [at(f"zl{i}", [128, D], F32, kb) for i, kb in enumerate(
            (11.75, O + 147.5, O + 151.5, O + 155.5, O + 159.5, O + 179.5, O + 183.5))]
        NZ = len(zl)
        s_zl = [dsem(f"s_zl{i}") for i in range(NZ)]
        s_x2 = [dsem(f"s_x2{i}") for i in range(NZ)]
        t_zl, t_x2, z_rows = {}, {}, {}
        t3 = [at("t31", [128, 256], F32, 1), at("t32", [128, 256], F32, 2), tt[4]]

        def finish_outer(q, i, r, ps, tok):
            cq = slice(256 * q, 256 * q + 256)
            if q == 3 and i == 0:
                slots = [*tt_used[0], *tt_used[1], *tt_used[2], *tt_used[3]], *[wb_used[0]] * 4, *[wp_used[0] + wp_used[1]] * 2
                for m in range(NZ):
                    rm = ROWS[m]
                    dma(SP, s_zl[m], zl[m][0:rm, 0:768], ZD[128 * m:128 * m + rm, 0:768], *slots[m], *z_rows[m])
                    t_zl[m] = dma(SP, s_zl[m], zl[m][0:rm, 768:1024], X1[128 * m:128 * m + rm, 768:1024])
            kept = q == 3 and i < NZ
            if kept:
                o, t_x = zl[i][0:r, 768:1024], t_zl[i]
            else:
                a = tturn[0] % 5 if q < 3 else i - NZ + 2
                tturn[0] += 1
                o = (tt[a] if q < 3 else t3[i - NZ])[0:r, :]
                t_x = dma(SP, s_tx[a], o, X1[128 * i:128 * i + r, cq], *tt_used[a], *((t_em,) if q == 3 else ()))
            t = dv(lambda e: e.tensor_tensor(o, o, bc[0:r, cq], ALU.add), t_x, t_b, chain=False)
            t = dv(lambda e: e.tensor_tensor(o, o, ps[0:r, 0:256], ALU.add), tok, t, chain=False)
            last = dv(lambda e: e.scalar_tensor_tensor(out=o, in0=ps[0:r, 256:512], scalar=dinv[0:r, i:i + 1], in1=o,
                                                       op0=ALU.mult, op1=ALU.add), t, chain=False)
            t = stats(i, q, o, (last,))
            if not kept:
                z_rows.setdefault(i, []).append(dma(AC, s_ho[a], ZD[128 * i:128 * i + r, cq], o, last))
                tt_used[a] = [z_rows[i][-1], t]
            if q == 3:
                aggregate(i, 4)
                for i0, i1 in ((0, 5), (5, NZ), (NZ, NT)):
                    if i == i1 - 1:
                        t = rstd(i0, i1)
                        for m in range(i0, i1):
                            t_rs[m] = t
                            if kept:
                                norm_x2(m, ())
            return last

        def norm_x2(i, t):
            r, a = ROWS[i], i % NZ
            t_x2[i] = ac(lambda e: e.activation(zl[a][0:r, :], zl[a][0:r, :], ACT.Identity, scale=rsd[0:r, i:i + 1],
                                                bias=nmr[0:r, i:i + 1]), t_rs[i], *t)
            t_st[i] = dma(AC, s_x2[a], X2[128 * i:128 * i + r, :], zl[a][0:r, :], t_x2[i])

        t_rs, t_st = {}, {}
        wd = at("wd", [128, 8, 256], F32, O + 127.5)
        wlr = at("wlr", [128, 2, 2, 256], F32, O + 135.5)
        xd = at("xd", [128, 2, N], F32, O + 94.5)
        wds = at("wds", [128, 2, 8, 256], F32R, O + 78.5)
        xlx = at("xlx", [128, NT, 4, 65], F32, O + 150)
        xrn = at("xrn", [128, NT, 256], F32, O + 160.25)
        atb = at("atb", [128, 256], F32, O + 171)
        zg = at("zg", [128, NT, 256], F32, O + 104.5)
        zh = at("zh", [128, NT, 256], F32, O + 114.5)
        ed = at("ed", [128, NT, 4], F32, O + 187.5)
        s_wd = dsem("s_wd")
        sage(ws1, wn1, first, turn_h, finish_outer)

        t_l1 = (P, P.n)
        dma(SP, s_wd, rw[:, :], rmsw.rearrange("(k p) -> p k", p=128), scattered=True)
        dma(SP, s_wd, wd[:, :, :], wdown.rearrange("(k p) n -> p k n", p=128), t_l1)
        dma(SP, s_wd, wlr[:, 0, :, :], wl.rearrange("(k p) n -> p k n", p=128))
        dma(SP, s_wd, wlr[:, 1, :, :], wr.rearrange("(k p) n -> p k n", p=128))
        t_wd = dma(SP, s_wd, atb[:, :],
                   att.rearrange("h d -> (h d)").rearrange("(a n) -> a n", a=1).broadcast_to([128, 256]), t_l1)
        t_xt = {}
        for i in range(NT):
            t_p = transpose_rows(i, zl[i % NZ], [t_x2[i]], True)
            n = i + NZ
            if n < NT:
                r, a = ROWS[n], n % NZ
                t = dma(SP, s_zl[a], zl[a][0:r, :], ZD[128 * n:128 * n + r, :], t_p, t_st[i], *z_rows[n])
                norm_x2(n, (t,))
            if i == 3:
                t = dv(lambda e: e.tensor_tensor(wd[:, :, :], wd[:, :, :], rw[:, :, None].broadcast_to([128, 8, 256]), ALU.mult), t_wd)
                t = ac(lambda e: e.activation(wds[:, 0, :, :], wd[:, :, :], ACT.Copy), t)
                t_wd2 = dv(lambda e: e.tensor_tensor(wds[:, 1, :, :], wd[:, :, :], wds[:, 0, :, :].bitcast(F32), ALU.subtract), t)
            t_xt[i] = (V, V.n)
            for c, o in {6: ((0, 0), (0, 1), (1, 0), (1, 1)), 9: ((2, 0), (2, 1))}.get(i, ()):
                c0, cn = CH[c]
                b, ps = bank()
                oo = slice(128 * o, 128 * o + 128)
                tok = mm(b, ps[:, 0:cn], [p for k in range(8) for p in (
                    (wds[:, 0, k, oo], xth[:, k, c0:c0 + cn]), (wds[:, 0, k, oo], xtl[:, k, c0:c0 + cn]),
                    (wds[:, 1, k, oo], xth[:, k, c0:c0 + cn]))], t_wd2, t_xt[3 * c + 3])
                free[b] = [ac(lambda e, o=o, c0=c0, cn=cn, ps=ps: e.activation(
                    xd[:, o, c0:c0 + cn], ps[:, 0:cn], ACT.Copy), tok)]
        t_xd = (A, A.n)
        dv(lambda e: e.tensor_tensor(t10[:, :], rsd[:, :], rsd[:, :], ALU.mult))
        dv(lambda e: e.tensor_tensor(t10[:, :], t10[:, :], mvb[:, :, 1], ALU.mult))
        dv(lambda e: e.tensor_scalar(out=vpe[:, :], in0=t10[:, :], scalar1=RMS_EPS, scalar2=None, op0=ALU.add))
        t_rms = rsqrt(rms[:, :], vpe[:, :], t10[:, :])
        t_kept = [t_st[i] for i in range(NT)]
        t_on = dv(lambda e: e.memset(xlx[:, :, :, 64:65], 1.0), t_p, *t_kept)
        s_xl = dsem("s_xl")
        for i in range(NT):
            r = ROWS[i]
            b, ps = bank()
            for w in range(2):
                tok = mm(b, ps[0:r, 256 * w:256 * w + 256],
                         [(xd[:, k, 128 * i:128 * i + r], wlr[:, w, k, :]) for k in range(2)], t_xd, t_wd)
            dv(lambda e, i=i, r=r, ps=ps: e.tensor_scalar(
                out=xlx[0:r, i, :, 0:64], in0=ps[0:r, 0:256].rearrange("p (h d) -> p h d", h=4), scalar1=rms[0:r, i:i + 1],
                scalar2=None, op0=ALU.mult), tok, chain=False)
            t0 = dv(lambda e, i=i, r=r, ps=ps: e.tensor_scalar(
                out=xrn[0:r, i, :], in0=ps[0:r, 256:512], scalar1=rms[0:r, i:i + 1], scalar2=None, op0=ALU.mult),
                chain=False)
            free[b] = [t0]
            dma(AC, s_xl, XL[128 * i:128 * i + r, :].rearrange("p (h d) -> p h d", h=4), xlx[0:r, i, :, 0:64], t0)
            t_xl = dma(AC, s_xl, XR[128 * i:128 * i + r, :], xrn[0:r, i, :], t0)

        def logits(z, tmp, tgt, m, xa, xb, *deps):
            pr = z.shape[0]
            dv(lambda e: e.tensor_tensor(z, xa, xb, ALU.add), *deps, chain=False)
            dv(lambda e: e.scalar_tensor_tensor(out=tmp.rearrange("p m f -> p (m f)"), in0=z.rearrange("p m f -> p (m f)"),
                                                scalar=0.2, in1=z.rearrange("p m f -> p (m f)"), op0=ALU.mult,
                                                op1=ALU.max))
            dv(lambda e: e.tensor_tensor(z, tmp, atb[0:pr, None, :].broadcast_to([pr, m, 256]), ALU.mult))
            return dv(lambda e: e.tensor_reduce(out=tgt, in_=z.rearrange("p m (h d) -> p (m h) d", h=4), axis=AX.X,
                                                op=ALU.add))

        for i0, i1, r in ((0, 9, 128), (9, 10, 98)):
            t_ed = diag_logits(dv, zg, zh, ed, atb, xlx, xrn, i0, i1, r, t_wd)
        s_ed = dsem("s_ed")
        diag = EM.rearrange("a (b h) -> (a b) h", h=4)
        for i in range(NT):
            r = ROWS[i]
            a0 = 128 * i * (N + 1)
            t_dg = dma(AC, s_ed, diag[a0:a0 + (r - 1) * (N + 1) + 1:N + 1, :], ed[0:r, i, :], t_ed, t_em)

        def weights(tiles, raw, parts, sems, raw_used, parts_used):
            t_raw, t_hi, t_w = {}, {}, {}

            def load(n):
                if n < len(tiles):
                    t_raw[n] = dma(SP, sems[n % 3], raw[n % 3][:, :, :], tiles[n], *raw_used[n % 3])

            def hi(n):
                if n < len(tiles):
                    t_hi[n] = ac(lambda e: e.activation(parts[n % 3][:, 0, :, :], raw[n % 3][:, :, :], ACT.Copy),
                                 t_raw[n], *parts_used[n % 3])

            def lo(n):
                if n < len(tiles):
                    t_w[n] = dv(lambda e: e.tensor_tensor(parts[n % 3][:, 1, :, :], raw[n % 3][:, :, :],
                                                          parts[n % 3][:, 0, :, :].bitcast(F32), ALU.subtract),
                                t_hi[n], chain=False)
                    raw_used[n % 3] = [t_w[n]]

            return load, hi, lo, t_w

        wraw2 = [at(f"wraw2{i}", [128, 8, 128], F32, O + 172.25 + 4 * i) for i in range(3)]
        whl2 = [at(f"whl2{i}", [128, 2, 8, 128], F32R, O + 78.5 + 8 * i) for i in range(3)]
        wut = at("wut", [128, 8, 256], F32, O + 104.5)
        wus = at("wus", [128, 2, 8, 256], F32R, O + 112.5)
        ones = at("ones", [128, 128], F32, 0.5)
        wmean = at("wmean", [128, 256], F32, 15.75)
        xw_t = [at(f"xw_t{i}", [128, 418], F32, 1 + 1.65625 * i) for i in range(3)]
        wa_t = at("wa_t", [128, 256], F32, 6)
        wb_t = [at(f"wb_t{i}", [128, 2, 2, 128], F32R, 11.75 + 2 * i) for i in range(2)]
        s_xw = [dsem(f"s_xw{i}") for i in range(3)]
        s_ww = [dsem(f"s_ww{i}") for i in range(2)]
        s_w2 = [dsem(f"s_w2{i}") for i in range(3)]
        s_wut = dsem("s_wut")
        dv(lambda e: e.memset(ones[:, :], 1.0))
        t_early = [t_ed, (P, P.n), *t_kept]
        tiles2 = [w[o] for w in (root, wgate[1]) for o in range(8)]
        whl_used2 = [list(t_early) for _ in range(3)]
        load2, hi2, lo2, t_w2 = weights(tiles2, wraw2, whl2, s_w2, [t_early] * 3, whl_used2)
        tt_done = [(s, s.n) for s in (*s_ho, *s_tx)] + t_kept
        t_wut = dma(SP, s_wut, wut[:, :, :], wupt, *t_early)

        def meanwhile():
            b, ps = bank()
            tok = mm(b, ps[:, 0:256], [(ones[:, :], wut[:, k, :]) for k in range(8)], t_wut, (V, V.n))
            free[b] = [dv(lambda e, ps=ps: e.tensor_scalar(out=wmean[:, :], in0=ps[:, 0:256], scalar1=1.0 / D, scalar2=None,
                                                           op0=ALU.mult), tok, *tt_done, chain=False)]
            t = dv(lambda e: e.tensor_tensor(wut[:, :, :], wut[:, :, :], wmean[:, None, :].broadcast_to([128, 8, 256]),
                                             ALU.subtract))
            t = ac(lambda e: e.activation(wus[:, 0, :, :], wut[:, :, :], ACT.Copy), t)
            t_wus = dv(lambda e: e.tensor_tensor(wus[:, 1, :, :], wut[:, :, :], wus[:, 0, :, :].bitcast(F32), ALU.subtract), t)
            for n in range(3):
                load2(n)
            for n in range(2):
                hi2(n)
                lo2(n)
            xw_used = [tt_done] * 3
            wa_used = list(tt_done)
            wb_used = [tt_done] * 2
            m = 0
            yield
            for n in range(16):
                hi2(n + 2)
                load2(n + 3)
                w = whl2[n % 3]
                b, ps = bank()
                tok = mm(b, ps[:, 0:256], [p for k in range(8) for p in (
                    (w[:, 0, k, :], wus[:, 0, k, :]), (w[:, 0, k, :], wus[:, 1, k, :]), (w[:, 1, k, :], wus[:, 0, k, :]))],
                    t_w2[n], t_wus)
                free[b] = [ac(lambda e, ps=ps: e.activation(wa_t[:, :], ps[:, 0:256], ACT.Copy), tok, *wa_used)]
                t_wa = free[b][0]
                for c0, cn in CH:
                    a = m % 3
                    m += 1
                    b, ps = bank()
                    tok = mm(b, ps[:, 0:cn], [p for k in range(8) for p in (
                        (w[:, 0, k, :], xth[:, k, c0:c0 + cn]), (w[:, 0, k, :], xtl[:, k, c0:c0 + cn]),
                        (w[:, 1, k, :], xth[:, k, c0:c0 + cn]))])
                    free[b] = [ac(lambda e, ps=ps, a=a, cn=cn: e.activation(xw_t[a][:, 0:cn], ps[:, 0:cn], ACT.Copy),
                                  tok, *xw_used[a])]
                    xw_used[a] = [dma(AC, s_xw[a], XW[n // 8, n % 8, :, c0:c0 + cn], xw_t[a][:, 0:cn], free[b][0])]
                b, ps = bank()
                for t in (*free[b], t_wa):
                    PE.wait(t)
                for g in range(2):
                    f = (lambda e, g=g, ps=ps: e.transpose(
                        ps[:, 128 * g:128 * g + 128], wa_t[:, 128 * g:128 * g + 128], ident[:, :]))
                    tok = PE.put(f, (), P if g else None, 1)
                wa_used = [tok]
                whl_used2[n % 3][:] = [tok]
                a = n % 2
                pv = ps[:, 0:256].rearrange("p (g c) -> p g c", g=2)
                t = ac(lambda e, pv=pv, a=a: e.activation(wb_t[a][:, 0, :, :], pv, ACT.Copy), tok, *wb_used[a])
                t = dv(lambda e, pv=pv, a=a: e.tensor_tensor(wb_t[a][:, 1, :, :], pv, wb_t[a][:, 0, :, :].bitcast(F32),
                                                             ALU.subtract), t, *wb_used[a], chain=False)
                free[b] = [t]
                wb_used[a] = [dma(AC, s_ww[a], WW[n // 8, n % 8], wb_t[a][:, :, :, :].bitcast(F32), t)]
                lo2(n + 2)
                yield

        NB = 5
        gl = [at(f"gl{i}", [EP, NB, 256], F32, O + 129 + 5 * i) for i in range(2)]
        gr = [at(f"gr{i}", [EP, NB, 256], F32, O + 139 + 5 * i) for i in range(2)]
        ee = at("ee", [EP, ET, 4], F32, O + 184.5)
        s_g = [dsem(f"s_g{i}") for i in range(2)]
        s_sc = dsem("s_sc")
        t_ee = {}
        used = [[], []]
        LAG = 8

        def put_logits(t):
            PL.put(lambda e: e.indirect_dma_start(
                out=diag, out_offset=bass.IndirectOffsetOnAxis(ap=adr[:, 0, t:t + 1], axis=0),
                in_=ee[:, t, :], in_offset=None, bounds_check=TPAD * N - 1, oob_is_err=True),
                (t_ee[t], t_dg, (s_sc, s_sc.n)), s_sc, 16)

        other = meanwhile()
        next(other)
        for t in range(ET):
            a, m = (t // NB) % 2, t % NB
            for buf, tab, row in ((gl, XL, 0), (gr, XR, 1)):
                tok = PL.put(lambda e, buf=buf, tab=tab, row=row, a=a, m=m, t=t: e.indirect_dma_start(
                    out=buf[a][:, m, :], out_offset=None, in_=tab,
                    in_offset=bass.IndirectOffsetOnAxis(ap=ei[:, row, t:t + 1], axis=0)),
                    (t_xl, *used[a]), s_g[a], 16)
            if m == NB - 1:
                last = logits(gl[a][:, :, :], gr[a][:, :, :],
                              ee[:, t - NB + 1:t + 1, :].rearrange("p m h -> p (m h)"), NB,
                              gl[a][:, :, :], gr[a][:, :, :], tok)
                used[a] = [last]
                for q in range(t - NB + 1, t + 1):
                    t_ee[q] = last
                next(other, None)
            if t >= LAG:
                put_logits(t - LAG)
        for t in range(ET - LAG, ET):
            put_logits(t)
        t_sc = (s_sc, s_sc.n)
        bar_dmas = [s_wd, s_xl, s_ed, *s_g, *s_xw, *s_ww]
        barrier()

        eb = [at(f"eb{i}", [128, N, 4], F32, O + 19.75 * i) for i in range(2)]
        pb = [at(f"pb{i}", [128, N], F32, O + 40 + 4.90625 * i) for i in range(6)]
        NPT = 11
        pt = [at(f"pt{i}", [128, 4, 128], F32, O + 128 + 2 * i) for i in range(NPT)]
        gn = at("gn", [128, NT, 256], F32, O + 160.25)
        gT = at("gT", [128, 2, N], F32, O + 170.25)
        wu = at("wu", [128, 2, D], F32, O + 180.25)
        mx = at("mx", [128, 2, 4], F32, O + 69.5)
        rd = at("rd", [128, 2, 4], F32, O + 69.5625)
        s_eb = [dsem(f"s_eb{i}") for i in range(2)]
        t_exp, t_eb, eb_used, t_max = {}, {}, [[], []], {}
        pt_used = [[] for _ in range(NPT)]
        pb_used = [[] for _ in range(6)]
        pturn = [0]
        parts_of, t_sum, t_gn = {}, {}, {}

        def load_logits(i):
            r, a = ROWS[i], i % 2
            t_eb[i] = dma(SP, s_eb[a], eb[a][0:r, :, :], EM[128 * i:128 * i + r, :].rearrange("p (s h) -> p s h", h=4),
                          t_sc, *eb_used[a])

        def load_bp(i):
            r, a = ROWS[i], i % 2
            t_nb[i] = dma(SP, s_nb[a], nb[a][0:r, :], BD[128 * i:128 * i + r, :], *nb_used[a])

        nb = [at(f"nb{i}", [128, N], F32, 1 + 5 * i) for i in range(2)]
        s_nb = [dsem(f"s_nb{i}") for i in range(2)]
        t_nb, nb_used = {}, [[], []]

        def maxima(i, h):
            r, a = ROWS[i], i % 2
            t_max[i, h] = dv(lambda e: e.tensor_reduce(
                out=mx[0:r, a, h:h + 1], in_=eb[a][0:r, :, h], axis=AX.X, op=ALU.max, negate=True),
                t_eb[i], *eb_used[a], chain=False)

        def exponentials(i, h):
            r, a, n = ROWS[i], i % 2, (4 * i + h) % 6
            t = ac(lambda e: e.activation(pb[n][0:r, :], eb[a][0:r, :, h], ACT.Exp, bias=mx[0:r, a, h:h + 1]),
                   t_max[i, h], *pb_used[n])
            if h == 3:
                eb_used[a] = [t]
            weigh_by = (lambda e: e.tensor_tensor(pb[n][0:r, :], pb[n][0:r, :], nb[a][0:r, :], ALU.mult))
            if h < 3:
                t_exp[i, h] = pl(weigh_by, t, t_nb[i])
            else:
                late.append((i, a, weigh_by, t))

        late = []

        def weigh_late():
            while late:
                i, a, f, t = late.pop()
                t_exp[i, 3] = dv(f, t, t_nb[i], chain=False)
                nb_used[a] = [t_exp[i, 2], t_exp[i, 3]]
                if i + 2 < NT:
                    load_bp(i + 2)

        def turn_over(i, h):
            r, s = ROWS[i], (4 * i + h) % 6
            parts_of[i, h] = []
            for g in range(3):
                ks = list(range(4 * g, min(4 * g + 4, NT)))
                b, ps = bank(6)
                for t in (*free[b], t_exp[i, h]):
                    PE.wait(t)
                for m, k in enumerate(ks):
                    f = (lambda e, m=m, k=k, ps=ps: e.transpose(
                        ps[0:ROWS[k], 128 * m:128 * m + r], pb[s][0:r, 128 * k:128 * k + ROWS[k]], ident[0:r, 0:r]))
                    tok = PE.put(f, (), P if k == ks[-1] else None, 1)
                n = pturn[0] % NPT
                pturn[0] += 1
                for kk, rk in ([(ks, 128)] if g < 2 else [(ks[0:1], 128), (ks[1:2], 98)]):
                    m0 = kk[0] - ks[0]
                    pv = ps[0:rk, :].rearrange("p (m c) -> p m c", m=4)[:, m0:m0 + len(kk), 0:r]
                    o = pt[n][0:rk, m0:m0 + len(kk), 0:r]
                    if g < 2:
                        last = ac(lambda e, o=o, pv=pv: e.activation(o, pv, ACT.Copy), tok, *pt_used[n])
                    else:
                        last = dv(lambda e, o=o, pv=pv: e.tensor_copy(o, pv), tok, *pt_used[n], chain=False)
                free[b] = [last]
                parts_of[i, h] += [(n, k, m, last) for m, k in enumerate(ks)]
            pb_used[s] = [tok]

        def weighted_sum(i, h):
            r, b = ROWS[i], 6 + i % 2
            prs = parts_of[i, h]
            tok = mm(b, banks[b][0:r, 65 * h:65 * h + 65],
                     [(pt[n][0:ROWS[k], m, 0:r], xlx[0:ROWS[k], k, h, :]) for n, k, m, _ in prs], *[p[3] for p in prs])
            for n, _, _, _ in prs:
                pt_used[n] = [tok]
            t_sum[i] = tok

        def normalise(i):
            r, a, b = ROWS[i], i % 2, 6 + i % 2
            pv = banks[b][0:r, 0:260].rearrange("p (h c) -> p h c", h=4)
            dv(lambda e: e.tensor_scalar(out=rd[0:r, a, :], in0=pv[:, :, 64], scalar1=1e-16, scalar2=None, op0=ALU.add),
               t_sum[i], chain=False)
            dv(lambda e: e.reciprocal(rd[0:r, a, :], rd[0:r, a, :]))
            t_gn[i] = dv(lambda e: e.tensor_tensor(
                gn[0:r, i, :].rearrange("p (h d) -> p h d", h=4), pv[:, :, 0:64],
                rd[0:r, a, :, None].broadcast_to([r, 4, 64]), ALU.mult))
            free[b] = [t_gn[i]]

        def turn_back(i):
            r = ROWS[i]
            b, ps = bank(6)
            for t in (*free[b], t_gn[i]):
                PE.wait(t)
            for k in range(2):
                f = (lambda e, k=k: e.transpose(
                    ps[:, 128 * k:128 * k + r], gn[0:r, i, 128 * k:128 * k + 128], ident[0:r, 0:r]))
                tok = PE.put(f, (), P if k == 1 else None, 1)
            free[b] = [ac(lambda e: e.activation(
                gT[:, :, 128 * i:128 * i + r], ps[:, 0:256].rearrange("p (k c) -> p k c", k=2)[:, :, 0:r], ACT.Copy), tok)]

        load_logits(0)
        load_logits(1)
        load_bp(0)
        load_bp(1)
        t_wu = dma(SP, s_wd, wu[:, :, :], wup.rearrange("(k p) n -> p k n", p=128), t_sc)
        for h in range(4):
            maxima(0, h)
        for h in range(3):
            exponentials(0, h)
        heads = [(i, h) for i in range(NT) for h in range(4)]
        for g, (i, h) in enumerate(heads):
            turn_over(i, h)
            weigh_late()
            if g + 3 < len(heads):
                i2, h2 = heads[g + 3]
                exponentials(i2, h2)
                if h2 == 3 and i2 + 2 < NT:
                    load_logits(i2 + 2)
            if i + 1 < NT:
                maxima(i + 1, h)
            if g > 1:
                weighted_sum(*heads[g - 2])
            if h == 2 and i > 0:
                normalise(i - 1)
            if h == 3 and i > 0:
                turn_back(i - 1)
        weighted_sum(NT - 1, 2)
        weighted_sum(NT - 1, 3)
        normalise(NT - 1)
        turn_back(NT - 1)
        t_gT = (A, A.n)

        z3 = [at(f"z3{i}", [128, D], F32, O + 4 * i) for i in range(NT)]
        s_2l = dsem("s_2l")
        t_2l = [dma(SP, s_2l, z3[i][0:ROWS[i], :], X2[128 * i:128 * i + ROWS[i], :], *eb_used[0],
                    *(eb_used[1] if i > 3 else ())) for i in range(NT)][-1]
        bar_dmas = [*s_eb, s_wd]
        barrier()
        mh = at("mh", [128, 8, 640], F32R, O)
        ml = at("ml", [128, 8, 640], F32R, O + 20)
        xh = at("xh", [128, NT, D], F16, O + 40)
        xo = at("xo", [128, NT, D], F16, O + 60)
        a16 = [at(f"a16{i}", [128, NT, 640], F16, O + 80 + 12.5 * i) for i in range(2)]
        acc = at("acc", [128, 8, N], F32, O + 121)
        wraw = [at(f"wraw{i}", [128, 8, 128], F32, O + 160.25 + 4 * i) for i in range(3)]
        whl = [at(f"whl{i}", [128, 2, 8, 128], F32R, O + (105, 113, 172.25)[i]) for i in range(3)]
        NA = 3
        ar = [at(f"ar{i}", [128, 640], F32, 1 + 2.5 * i) for i in range(NA)]
        tmp = [at(f"tmp{i}", [128, 384], F32, 8.5 + 1.5 * i) for i in range(3)]
        asum = at("asum", [128, 640], F32, 13)
        ib = at("ib", [128, 640], F32, O + 180.25)
        rsb = at("rsb", [128, N], F32, O + 182.75)
        gs = at("gs", [128, 2, 2, 640], F32R, O + 93)
        ws = [at(f"ws{i}", [128, 2, 2, 128], F32R, kb) for i, kb in enumerate((O + 103, 15.5, O + 168.25, 8.5, 10.5, 13))]
        s_ws = [dsem(f"s_ws{i}") for i in range(6)]
        s_gd = dsem("s_gd")
        s_g2 = dsem("s_g2")
        s_acc = dsem("s_acc")
        s_ar = [dsem(f"s_ar{i}") for i in range(NA)]
        s_wq = [dsem(f"s_wq{i}") for i in range(3)]
        s_br = dsem("s_br")
        dma(SP, s_br, brel[:, :], bias.rearrange("(k p) -> p k", p=128), scattered=True)
        t_br = dma(SP, s_br, bg[:, :], bgate.rearrange("(k p) -> p k", p=128), scattered=True)
        ar_used = [[] for _ in range(NA)]
        a_free = [[], []]
        t_pad = [dv(lambda e: e.memset(a16[0][:, 9, :], 0.0), chain=False)]
        halves = [(h, rel) for rel in range(NREL) for h in range(2)]

        def load_counts(n, k):
            (h, rel), q, rk = halves[n], (NT * n + k) % NA, ROWS[k]
            w = HW[h]
            t0 = dma(SP, s_ar[q], ar[q][0:rk, 0:w], TR[rel * N + 128 * k:rel * N + 128 * k + rk, 640 * h:640 * h + w],
                     t_tr, *ar_used[q])
            t = ac(lambda e: e.activation(a16[n % 2][0:rk, k, 0:w], ar[q][0:rk, 0:w], ACT.Copy), t0, t_pad[n % 2],
                   *a_free[n % 2])
            ar_used[q] = [t]
            return t

        wlist = [wrel[rel, o] for h, rel in halves for o in range(8)] + [wgate[0][o] for _ in range(2) for o in range(8)]
        raw_used = [[], [], []]
        whl_used = [[], [], []]
        w_load, w_hi, w_lo, t_w = weights(wlist, wraw, whl, s_wq, raw_used, whl_used)
        t_acc0 = dma(SP, s_acc, acc[:, :, :], XW[0].rearrange("o p n -> p o n"))
        for n in range(2):
            w_load(n)

        def split_g(h, *deps):
            hs = slice(640 * h, 640 * h + HW[h])
            t = ac(lambda e: e.activation(gs[:, 0, :, 0:HW[h]], gT[:, :, hs], ACT.Copy), t_gT, *deps)
            return (dv(lambda e: e.tensor_tensor(gs[:, 1, :, 0:HW[h]], gT[:, :, hs], gs[:, 0, :, 0:HW[h]].bitcast(F32),
                                                 ALU.subtract), t, *deps, chain=False),)

        t_h = split_g(0)

        t_xh = {}

        def norm_x3(tiles):
            for q in tiles:
                r = ROWS[q]
                t = ac(lambda e, r=r, q=q: e.activation(z3[q][0:r, :], z3[q][0:r, :], ACT.Identity,
                                                        scale=rsd[0:r, q:q + 1], bias=nmr[0:r, q:q + 1]), t_rs)
                t_xh[q] = ac(lambda e, r=r, q=q: e.mul(xh[0:r, q, :], z3[q][0:r, :], XS), t)

        def rest_x3(tiles):
            for q in tiles:
                r = ROWS[q]
                t = dv(lambda e, r=r, q=q: e.scalar_tensor_tensor(
                    out=xo[0:r, q, :], in0=z3[q][0:r, :], scalar=XS, in1=xh[0:r, q, :], op0=ALU.mult,
                    op1=ALU.subtract), t_xh[q], chain=False)
            return t

        for i in range(NT):
            r = ROWS[i]
            for j in range(2):
                b, ps = bank()
                c = slice(512 * j, 512 * j + 512)
                tok = mm(b, ps[0:r, :], [(gT[:, k, 128 * i:128 * i + r], wu[:, k, c]) for k in range(2)], t_gT, t_wu)
                free[b] = [dv(lambda e, r=r, i=i, c=c, ps=ps: e.tensor_tensor(z3[i][0:r, c], ps[0:r, :], z3[i][0:r, c], ALU.add),
                              tok, t_2l, chain=False)]
                stats(i, j, z3[i][0:r, c], free[b])
            aggregate(i, 2)
            t_cnt = load_counts(0, i)
            if i in (4, 9):
                t_rs = rstd(i - 4, i + 1)
            if i == 4:
                norm_x3(range(5))

        t_last = (P, P.n)
        ws_n = [0]
        ws_used = [[], [], [t_last], [], [], []]

        def load_ws(p, o):
            n = ws_n[0] % 6
            ws_n[0] += 1
            return n, dma(PL, s_ws[n], ws[n][:, :, :, :], WW[p, o], *ws_used[n])

        def up(n, o0, cn):
            return [p for k in range(2) for p in ((ws[n][:, 0, k, :], gs[:, 0, k, o0:o0 + cn]),
                                                  (ws[n][:, 0, k, :], gs[:, 1, k, o0:o0 + cn]),
                                                  (ws[n][:, 1, k, :], gs[:, 0, k, o0:o0 + cn]))]

        t_gd = dma(SP, s_gd, GD, gT[:, :, :], t_gT)
        wsq = [load_ws(0, o) for o in range(5)]
        t_xs = []
        for h in range(2):
            if h:
                t_h = split_g(h, (P, P.n))
            if h == 0:
                for g in range(3):
                    ks = list(range(4 * g, min(4 * g + 4, NT)))
                    b, ps = bank()
                    for m, i in enumerate(ks):
                        r = ROWS[i]
                        tok = mm(b, ps[:, 128 * m:128 * m + r],
                                 [(rsd[0:r, i:i + 1].broadcast_to([r, 128]), ident[0:r, 0:r])], t_rs)
                    w = sum(ROWS[i] for i in ks)
                    free[b] = [ac(lambda e, ps=ps, g=g, w=w: e.activation(rsb[:, 512 * g:512 * g + w], ps[:, 0:w], ACT.Copy), tok)]
                t_rsb = free[b][0]
                norm_x3(range(5, NT))
                rest_x3(range(5))
            for o in range(8):
                n, t_ws = wsq.pop(0)
                if 8 * h + o + 5 < 16:
                    wsq.append(load_ws(0, (o + 5) % 8))
                for o0, cn in HC[h]:
                    b, ps = bank()
                    tok = mm(b, ps[:, 0:cn], up(n, o0, cn), t_ws, *t_h)
                    av = acc[:, o, 640 * h + o0:640 * h + o0 + cn]
                    free[b] = [dv(lambda e, ps=ps, o=o, cn=cn, av=av: e.tensor_tensor(av, ps[:, 0:cn], av, ALU.add),
                                  tok, t_acc0, chain=False)]
                ws_used[n] = [tok]
                t_xs.append(free[b][0])
                if h == 0 and o == 3:
                    t_x3 = rest_x3(range(5, NT))
        t_sc3 = [pl(lambda e, n=n: e.tensor_tensor(
            acc[:, n % 8, 640 * (n // 8):640 * (n // 8) + HW[n // 8]], acc[:, n % 8, 640 * (n // 8):640 * (n // 8) + HW[n // 8]],
            rsb[:, 640 * (n // 8):640 * (n // 8) + HW[n // 8]], ALU.mult), t_xs[n], t_rsb) for n in range(16)]
        t_init = (P, P.n)
        a_free[1] = [t_init, t_gd]
        t_pad.append(dv(lambda e: e.memset(a16[1][:, 9, :], 0.0), *a_free[1], chain=False))

        t_m = {}

        def split_m(f, c, o0, cn, src_ap, *deps):
            t = ac(lambda e: e.activation(mh[:, f, o0:o0 + cn], src_ap, ACT.Copy), *deps)
            t = dv(lambda e: e.tensor_tensor(ml[:, f, o0:o0 + cn], src_ap, mh[:, f, o0:o0 + cn].bitcast(F32),
                                             ALU.subtract), t, chain=False)
            t_m[c, f] = t
            return t

        step = [0]

        def weigh(h, evac, more=None):
            for o in range(8):
                n = step[0]
                step[0] += 1
                w_hi(n + 2)
                w_load(n + 3)
                hi, lo = whl[n % 3][:, 0], whl[n % 3][:, 1]
                for c, (o0, cn) in enumerate(HC[h]):
                    b, ps = bank()
                    tok = mm(b, ps[:, 0:cn], [p for k in range(8) for p in (
                        (hi[:, k, :], mh[:, k, o0:o0 + cn], t_m[c, k]), (hi[:, k, :], ml[:, k, o0:o0 + cn]),
                        (lo[:, k, :], mh[:, k, o0:o0 + cn]))] + (more(o, o0, cn) if more else []), t_w[n])
                    evac(o, c, 640 * h + o0, o0, cn, b, ps, tok)
                whl_used[n % 3] = [tok]
                w_lo(n + 2)
                yield o

        tmp_n = [0]
        t_acc = {}
        raw_used[2] = [*t_h, t_init]
        whl_used[2] = [*t_h, t_gd]
        w_load(2)
        for n in range(2):
            w_hi(n)
            w_lo(n)

        def add_scaled(rel):
            def evac(o, c, c0, o0, cn, b, ps, tok):
                q = tmp_n[0] % 3
                tmp_n[0] += 1
                t = dv(lambda e: e.tensor_tensor(tmp[q][:, 0:cn], ps[:, 0:cn], ib[:, o0:o0 + cn], ALU.mult), tok, chain=False)
                free[b] = [t]
                av = acc[:, o, c0:c0 + cn]
                if rel == 0:
                    dv(lambda e: e.scalar_tensor_tensor(out=av, in0=tmp[q][:, 0:cn], scalar=brel[:, o:o + 1], in1=av,
                                                        op0=ALU.add, op1=ALU.add), t, t_br, t_sc3[8 * (c0 // 640) + o])
                else:
                    dv(lambda e: e.tensor_tensor(av, tmp[q][:, 0:cn], av, ALU.add), t)
            return evac

        ash = at("ash", [128, 640], F16, 15.5)
        asl = at("asl", [128, 640], F32R, 13)
        ones_h = at("ones_h", [128, 128], F16, 16.75)
        ones_l = at("ones_l", [128, 128], F32R, 17)
        dv(lambda e: e.tensor_copy(ones_h[:, :], ones[:, :]), t_init)
        dv(lambda e: e.tensor_copy(ones_l[:, :], ones[:, :]))

        def total_counts(n, t):
            w = HW[halves[n][0]]
            dv(lambda e: e.tensor_reduce(out=asum[:, 0:w], in_=a16[n % 2][:, :, 0:w].rearrange("p k d -> p d k"),
                                         axis=AX.X, op=ALU.add), t)
            dv(lambda e: e.tensor_copy(ash[:, 0:w], asum[:, 0:w]))
            return dv(lambda e: e.tensor_tensor(asl[:, 0:w], asum[:, 0:w], ash[:, 0:w], ALU.subtract))

        graw = at("graw", [128, 2, 640], F32, O + 88)

        def load_g(h):
            w, hs = HW[h], slice(640 * h, 640 * h + HW[h])
            t = dma(SP, s_g2, graw[:, :, 0:w], GD[:, :, hs], *gs_used)
            t = pl(lambda e: e.tensor_tensor(graw[:, :, 0:w], graw[:, :, 0:w], rsb[:, None, hs].broadcast_to([128, 2, w]),
                                             ALU.mult), t)
            t = ac(lambda e: e.activation(gs[:, 0, :, 0:w], graw[:, :, 0:w], ACT.Copy), t, *gs_used)
            return dv(lambda e: e.tensor_tensor(gs[:, 1, :, 0:w], graw[:, :, 0:w], gs[:, 0, :, 0:w].bitcast(F32),
                                                ALU.subtract), t, chain=False)

        t_as = total_counts(0, t_cnt)
        for n, (h, rel) in enumerate(halves):
            av = a16[n % 2]
            for f in range(8):
                for c, (o0, cn) in enumerate(HC[h]):
                    b, ps = bank()
                    tok = mm(b, ps[:, 0:cn], [(x[0:ROWS[k], k, 128 * f:128 * f + 128], av[0:ROWS[k], k, o0:o0 + cn])
                                              for k in range(NT) for x in (xh, xo)], t_cnt, t_x3)
                    free[b] = [split_m(f, c, o0, cn, ps[:, 0:cn], tok)]
                if f == 0:
                    for o0, cn in HC[h]:
                        b, ps = bank()
                        tok = mm(b, ps[:, 0:cn], [(ones_h[:, :], ash[:, o0:o0 + cn]),
                                                       (ones_l[:, :], asl[:, o0:o0 + cn])], t_as)
                        dv(lambda e, o0=o0, cn=cn, ps=ps: e.tensor_scalar(
                            out=ib[:, o0:o0 + cn], in0=ps[:, 0:cn], scalar1=1.0, scalar2=XS, op0=ALU.max, op1=ALU.mult), tok)
                        free[b] = [dv(lambda e, o0=o0, cn=cn: e.reciprocal(ib[:, o0:o0 + cn], ib[:, o0:o0 + cn]))]
            a_free[n % 2] = gs_used = [(P, P.n)]
            for o in weigh(h, add_scaled(rel)):
                if n + 1 == len(halves) and o == 2:
                    t_g2 = load_g(0)
                if n + 1 < len(halves):
                    if o < 5:
                        load_counts(n + 1, 2 * o)
                        t_cnt = load_counts(n + 1, 2 * o + 1)
                    if o == 6:
                        t_as = total_counts(n + 1, t_cnt)

        on = [at(f"on{i}", [128, D], F32, O + 80 + 4 * i) for i in range(2)]
        on_end = [at(f"on_end{i}", [128, D], F32, O + 4 * i) for i in range(5)]
        zz = [at(f"zz{i}", [128, 384], F32, 13 + 1.5 * i) for i in range(3)]
        xs = [at(f"xs{i}", [128, 640], F32, 1 + 2.5 * i) for i in range(3)]
        ws = [at(f"wt{i}", [128, 2, 2, 128], F32R, O + (103, 180.25)[i]) for i in range(2)]
        s_xs = [dsem(f"s_xs{i}") for i in range(3)]
        s_out = [dsem(f"s_out{i}") for i in range(8)]
        ws_used = [[(P, P.n), (V, V.n)] for _ in range(2)]
        xs_used = [[(A, A.n)] for _ in range(3)]
        gate_n = [0]
        t_xw = {}

        def gate_load(h, o):
            n = gate_n[0]
            gate_n[0] += 1
            q, a, w = n % 2, n % 3, HW[h]
            t0 = dma(PL, s_ws[q], ws[q][:, :, :, :], WW[1, o], *ws_used[q])
            t1 = dma(SP, s_xs[a], xs[a][:, 0:w], XW[1, o, :, 640 * h:640 * h + w], *xs_used[a])
            t_xw[h, o] = q, a, t0, pl(lambda e: e.tensor_tensor(xs[a][:, 0:w], xs[a][:, 0:w], rsb[:, 640 * h:640 * h + w],
                                                               ALU.mult), t1)

        def x_turned(o, tiles, ps):
            for m, i in enumerate(tiles):
                r = ROWS[i]
                for q, x in enumerate((xh, xo)):
                    PE.items.append(lambda e, m=m, i=i, r=r, q=q, x=x: e.matmul(
                        ps[:, 128 * m:128 * m + r], x[0:r, i, 128 * o:128 * o + 128], ident16[0:r, 0:r],
                        start=(q == 0), stop=(q == 1))) if (m, q) != (len(tiles) - 1, 1) else None
            return PE.put(lambda e: e.matmul(ps[:, 128 * m:128 * m + r], x[0:r, i, 128 * o:128 * o + 128],
                                             ident16[0:r, 0:r], start=False, stop=True), (), P, 1)

        t_r = {}
        for h in range(2):
            tiles = [[5 * h, 5 * h + 1, 5 * h + 2], [5 * h + 3, 5 * h + 4]]
            gate_load(h, 0)
            gate_load(h, 1)

            def more(o, o0, cn):
                (l, r), *rest = up(t_xw[h, o][0], o0, cn)
                return [(l, r, t_xw[h, o][2], t_g2), *rest]

            def gate(o, c, c0, o0, cn, b, ps, tok):
                q = tmp_n[0] % 3
                tmp_n[0] += 1
                bx, px = bank()
                for t in free[bx]:
                    PE.wait(t)
                tx = x_turned(o, tiles[c], px)
                t = ac(lambda e: e.activation(tmp[q][:, 0:cn], acc[:, o, c0:c0 + cn], ACT.Tanh), (V, V.n))
                xa = xs[t_xw[h, o][1]]
                t1 = dv(lambda e: e.scalar_tensor_tensor(
                    out=zz[q][:, 0:cn], in0=ps[:, 0:cn], scalar=bg[:, o:o + 1], in1=xa[:, o0:o0 + cn], op0=ALU.add,
                    op1=ALU.add), tok, t_xw[h, o][3], chain=False)
                xs_used[t_xw[h, o][1]] = [t1]
                ws_used[t_xw[h, o][0]] = [tok]
                free[b] = [t1]
                t2 = dv(lambda e: e.scalar_tensor_tensor(
                    out=tmp[q][:, 0:cn], in0=px[:, 0:cn], scalar=-1.0 / XS, in1=tmp[q][:, 0:cn], op0=ALU.mult,
                    op1=ALU.add), t, tx, chain=False)
                t3 = dv(lambda e: e.tensor_tensor(zz[q][:, 0:cn], zz[q][:, 0:cn], tmp[q][:, 0:cn], ALU.mult), t1, t2)
                free[bx] = [dv(lambda e: e.scalar_tensor_tensor(
                    out=acc[:, o, c0:c0 + cn], in0=px[:, 0:cn], scalar=2.0 / XS, in1=zz[q][:, 0:cn], op0=ALU.mult,
                    op1=ALU.add), t3)]
                t_r[h, c] = free[bx][0]

            t_u = (V, V.n)
            for c, (o0, cn) in enumerate(HC[h]):
                for f in range(8):
                    split_m(f, c, o0, cn, acc[:, f, 640 * h + o0:640 * h + o0 + cn], t_u, (P, P.n))
            if h:
                t_g2 = load_g(h)
            for o in weigh(h, gate, more=more):
                if o + 2 < 8:
                    gate_load(h, o + 2)
                if h == 1 and 0 < o < 6:
                    turn_out(o - 1, on[(o - 1) % 2], (o - 1) % 2)
                    put_out(o - 1, o, [(on[(o - 1) % 2], (o - 1) % 2)])
            gs_used = [(P, P.n)]
            if h == 0:
                on_used = [[] for _ in range(8)]

                def turn_out(i, to, n):
                    r, h = ROWS[i], i // 5
                    t_c = t_r[h, 0 if i % 5 < 3 else 1]
                    for j in range(2):
                        b, ps = bank()
                        for t in (*free[b], t_c):
                            PE.wait(t)
                        for q in range(4):
                            f = (lambda e, q=q, j=j, ps=ps: e.transpose(
                                ps[0:r, 128 * q:128 * q + 128], acc[:, 4 * j + q, 128 * i:128 * i + r], ident[:, :]))
                            tok = PE.put(f, (), P if q == 3 else None, 1)
                        t = ac(lambda e, j=j, ps=ps: e.activation(to[0:r, 512 * j:512 * j + 512], ps[0:r, :], ACT.Copy),
                               tok, *on_used[n], *t_free)
                        free[b] = [t]
                        stats(i, j, to[0:r, 512 * j:512 * j + 512], (t,))
                    aggregate(i, 2)

                def put_out(i0, i1, tiles):
                    t_rs = rstd(i0, i1)
                    for i, (to, n) in zip(range(i0, i1), tiles):
                        r = ROWS[i]
                        if i % 2:
                            t = ac(lambda e, r=r, i=i, to=to: e.activation(
                                to[0:r, :], to[0:r, :], ACT.Identity, scale=rsd[0:r, i:i + 1], bias=nmr[0:r, i:i + 1]),
                                t_rs, (A, A.n))
                        else:
                            t = dv(lambda e, r=r, i=i, to=to: e.tensor_scalar(
                                out=to[0:r, :], in0=to[0:r, :], scalar1=mvb[0:r, i, 0:1], scalar2=rsd[0:r, i:i + 1],
                                op0=ALU.subtract, op1=ALU.mult), (A, A.n), chain=False)
                        on_used[n] = [dma(SP, s_out[n], out[128 * i:128 * i + r, :], to[0:r, :], t)]

                t_free = ()
        t_free = (t_r[1, 0], t_r[1, 1])
        for i0, i1 in ((5, 8), (8, 10)):
            for i in range(i0, i1):
                turn_out(i, on_end[i - 5], i - 2)
            put_out(i0, i1, [(on_end[i - 5], i - 2) for i in range(i0, i1)])
        for s in dmas:
            SP.wait((s, s.n))

        block = ctx.enter_context(nc.Block())

        @block.sync
        def _(e):
            SP.run(e)

        @block.tensor
        def _(e):
            PE.run(e)

        @block.vector
        def _(e):
            DV.run(e)

        @block.scalar
        def _(e):
            AC.run(e)

        @block.gpsimd
        def _(e):
            PL.run(e)


def diag_logits(dv, zg, zh, ed, atb, xlx, xrn, i0, i1, r, dep):
    for i in range(i0, i1):
        dv(lambda e, i=i: e.tensor_tensor(zg[0:r, i, :].rearrange("p (h d) -> p h d", h=4), xlx[0:r, i, :, 0:64],
                                          xrn[0:r, i, :].rearrange("p (h d) -> p h d", h=4), ALU.add), dep)
        dv(lambda e, i=i: e.scalar_tensor_tensor(out=zh[0:r, i, :], in0=zg[0:r, i, :], scalar=0.2, in1=zg[0:r, i, :],
                                                 op0=ALU.mult, op1=ALU.max))
        dv(lambda e, i=i: e.tensor_tensor(zg[0:r, i, :], zh[0:r, i, :], atb[0:r, :], ALU.mult))
        t = dv(lambda e, i=i: e.tensor_reduce(out=ed[0:r, i, :], in_=zg[0:r, i, :].rearrange("p (h d) -> p h d", h=4),
                                              axis=AX.X, op=ALU.add))
    return t


_INS = ["x", "x_t", "src", "dst", "edge_type_8", "L0_gnn_W", "L0_gnn_b", "L1_gnn_W_self0", "L1_gnn_W_neigh0", "L1_gnn_b0",
        "L1_gnn_W_self1", "L1_gnn_W_neigh1", "L1_gnn_b1", "L2_gnn_rms_w", "L2_gnn_W_down", "L2_gnn_Wl", "L2_gnn_Wr",
        "L2_gnn_att", "L2_gnn_W_up", "W_up_t", "L3_gnn_weight", "L3_gnn_root", "L3_gnn_bias", "L3_gnn_w_gate", "L3_gnn_b_gate"]


_TILED = ("L1_gnn_W_self0", "L1_gnn_W_neigh0", "L1_gnn_W_self1", "L1_gnn_W_neigh1", "L3_gnn_weight", "L3_gnn_root", "L3_gnn_w_gate")


def kernel(**inputs):
    import numpy as np
    import concourse.bacc as bacc
    from concourse.bass_utils import run_bass_kernel_spmd

    nc = bacc.Bacc("TRN2", target_bir_lowering=False, num_devices=1)
    arrays, args = {}, []
    for name in _INS:
        a = np.asarray(inputs[{"x_t": "x", "W_up_t": "L2_gnn_W_up"}.get(name, name)])
        if name in ("x_t", "L0_gnn_W", "W_up_t"):
            a = a.T.reshape(8, 128, -1).transpose(1, 0, 2)
        if name in _TILED:
            a = a.reshape(-1, 8, 128, 8, 128).transpose(0, 3, 2, 1, 4)
            a = a[0] if len(a) == 1 else a
        a = np.ascontiguousarray(a)
        arrays[f"in_{name}"] = a
        args.append(nc.dram_tensor(f"in_{name}", a.shape, mybir.dt.from_np(a.dtype), kind="ExternalInput").ap())
    args.append(nc.dram_tensor("out_0", (N, D), F32, kind="ExternalOutput").ap())
    program(nc, *args)
    r = run_bass_kernel_spmd(nc, [arrays], core_ids=[0])
    return r.results[0]["out_0"]
```
